# Optimizing a Trainium2 kernel written in Bass

```python
import numpy as np
import jax
import jax.numpy as jnp

def _softmax(x, axis=-1):
    return jax.nn.softmax(x, axis=axis)

def _gelu(x):
    return jax.nn.gelu(x, approximate=True)

def _silu(x):
    return jax.nn.silu(x)

def _sigmoid(x):
    return jax.nn.sigmoid(x)

def _layernorm(x, axis=-1, eps=1e-05):
    m = jnp.mean(x, axis=axis, keepdims=True)
    v = jnp.var(x, axis=axis, keepdims=True)
    return (x - m) / jnp.sqrt(v + eps)

def _scatter_add(tgt, idx, src, axis=0):
    return tgt.at[idx].add(src)

def _segment_sum(src, seg, n):
    return jax.ops.segment_sum(src, seg, n)
kernel_name = 'mk_adaln_ffn_d2_seqx_r8_189ed0'

def setup_inputs(seed: int=0):
    np.random.seed(seed)
    _w = jnp.asarray

    def _rec_inputs():
        import jax
        import jax.numpy as jnp
        _rk = jax.random.key(seed)
        x = -0.0002071 + 1 * jax.random.normal(jax.random.fold_in(_rk, 1), (16, 128, 128), jnp.float32)
        _lenS = 128 - jax.random.randint(jax.random.fold_in(_rk, 7), (16,), 0, max(1, 128 // 4) + 1, jnp.int32)
        _lenS2 = 128 - jax.random.randint(jax.random.fold_in(_rk, 8), (16,), 0, max(1, 128 // 4) + 1, jnp.int32)
        cond_8 = jax.random.uniform(jax.random.fold_in(_rk, 11), (16, 8), jnp.float32, 0.0, 0.983423)
        return (x, cond_8)
    x, cond_8 = _rec_inputs()

    def _L0_cond_setup():
        import jax, jax.numpy as jnp
        import numpy as np
        R = 16
        ALPHA = 32.0
        SCALING = ALPHA / R
        key = jax.random.key(seed)
        ks = jax.random.split(key, 6)
        B, T, C, O, E = (16, 1500, 128, 128, 8)
        x = jax.random.normal(ks[0], (B, T, C), dtype=jnp.float32)
        w = jax.random.uniform(ks[1], (B, E), dtype=jnp.float32)
        W_base = jax.random.normal(ks[2], (O, C), dtype=jnp.float32) * 0.02
        b_base = jax.random.normal(ks[3], (O,), dtype=jnp.float32) * 0.02
        As = jax.random.normal(ks[4], (E, R, C), dtype=jnp.float32) * 0.02
        Bs = jax.random.normal(ks[5], (E, O, R), dtype=jnp.float32) * 0.02
        return {'x': x, 'w': w, 'W_base': W_base, 'b_base': b_base, 'As': As, 'Bs': Bs}
    _L0_cond_all = _L0_cond_setup()
    _L0_cond_in = {k: v for k, v in _L0_cond_all.items() if k in ('W_base', 'b_base', 'As', 'Bs')}
    del _L0_cond_all

    def _L0_ffn_setup():
        import math
        import jax, jax.numpy as jnp
        import numpy as np
        D_MODEL = 128
        D_FF = 512
        E = 8
        K = 2
        CF = 1.25
        CLAMP = 10000.0
        key = jax.random.key(seed)
        k0, k1, k2, k3 = jax.random.split(key, 4)
        B, S = (4, 256)
        x = jax.random.normal(k0, (B, S, D_MODEL), dtype=jnp.float32)
        ln_gamma = jnp.ones((D_MODEL,), jnp.float32)
        ln_beta = jnp.zeros((D_MODEL,), jnp.float32)
        rb = 0.02 * math.sqrt(3.0)
        Wr = jax.random.uniform(k1, (E, D_MODEL), jnp.float32, -rb, rb)
        b12 = math.sqrt(6.0 / (D_MODEL + 2 * D_FF))
        W12 = jax.random.uniform(k2, (E, 2 * D_FF, D_MODEL), jnp.float32, -b12, b12)
        b3 = math.sqrt(6.0 / (D_FF + D_MODEL))
        W3 = jax.random.uniform(k3, (E, D_MODEL, D_FF), jnp.float32, -b3, b3)
        return {'x': x, 'ln_gamma': ln_gamma, 'ln_beta': ln_beta, 'Wr': Wr, 'W12': W12, 'W3': W3}
    _L0_ffn_all = _L0_ffn_setup()
    _L0_ffn_in = {k: v for k, v in _L0_ffn_all.items() if k in ('ln_gamma', 'ln_beta', 'Wr', 'W12', 'W3')}
    del _L0_ffn_all

    def _L1_cond_setup():
        import jax, jax.numpy as jnp
        import numpy as np
        TOP_K = 2
        NUM_MOE_LAYERS = 12

        def _gemma_mlp(x, gate_w, up_w, down_w):
            g = jnp.einsum('bsh,hi->bsi', x, gate_w)
            u = jnp.einsum('bsh,hi->bsi', x, up_w)
            return jnp.einsum('bsi,ih->bsh', jax.nn.gelu(g, approximate=True) * u, down_w)
        key = jax.random.key(seed)
        ks = jax.random.split(key, 8)
        B, S, H, I, E = (32, 32, 128, 512, 8)
        std = 0.02
        return {'x': jax.random.normal(ks[0], (B, S, H), jnp.float32), 'router_logits': jax.random.normal(ks[1], (B, E), jnp.float32), 'skill_gate': jax.random.normal(ks[2], (E, H, I), jnp.float32) * std, 'skill_up': jax.random.normal(ks[3], (E, H, I), jnp.float32) * std, 'skill_down': jax.random.normal(ks[4], (E, I, H), jnp.float32) * std, 'shared_gate': jax.random.normal(ks[5], (H, I), jnp.float32) * std, 'shared_up': jax.random.normal(ks[6], (H, I), jnp.float32) * std, 'shared_down': jax.random.normal(ks[7], (I, H), jnp.float32) * std}
    _L1_cond_all = _L1_cond_setup()
    _L1_cond_in = {k: v for k, v in _L1_cond_all.items() if k in ('skill_gate', 'skill_up', 'skill_down', 'shared_gate', 'shared_up', 'shared_down')}
    del _L1_cond_all

    def _L1_ffn_setup():
        import jax, jax.numpy as jnp
        import numpy as np
        DIM = 128
        DEPTH = 2
        HEADS = 8
        DIM_HEAD = 64
        WINDOW = 64
        INNER = HEADS * DIM_HEAD
        HID = int(DIM * 4 * 2 / 3)
        B, N = (2, 1024)
        QK_SCALE = 8.0

        def shift_token(t):
            t1, t2 = jnp.split(t, 2, axis=-1)
            t2 = jnp.pad(t2, ((0, 0), (1, 0), (0, 0)))[:, :-1]
            return jnp.concatenate([t1, t2], axis=-1)

        def l2norm(t):
            return t / jnp.clip(jnp.linalg.norm(t, axis=-1, keepdims=True), 1e-12)

        def rotate_half(x):
            x1, x2 = jnp.split(x, 2, axis=-1)
            return jnp.concatenate([-x2, x1], axis=-1)

        def rotary_xpos(q, k):
            n = q.shape[-2]
            half_idx = jnp.arange(0, DIM_HEAD, 2, dtype=jnp.float32)
            inv_freq = 1.0 / 10000.0 ** (half_idx / DIM_HEAD)
            t = jnp.arange(n, dtype=jnp.float32)
            freqs = t[:, None] * inv_freq[None, :]
            freqs = jnp.concatenate([freqs, freqs], axis=-1)
            base = (half_idx + 0.4 * DIM_HEAD) / (1.4 * DIM_HEAD)
            power = (t - n // 2) / float(WINDOW // 2)
            scale = base[None, :] ** power[:, None]
            scale = jnp.concatenate([scale, scale], axis=-1)
            cos, sin = (jnp.cos(freqs), jnp.sin(freqs))
            q = q * cos * scale + rotate_half(q) * sin * scale
            k = k * cos / scale + rotate_half(k) * sin / scale
            return (q, k)

        def local_attention(q, k, v):
            b, h, n, d = q.shape
            w = n // WINDOW
            bq = q.reshape(b, h, w, WINDOW, d) * QK_SCALE
            bk = k.reshape(b, h, w, WINDOW, d)
            bv = v.reshape(b, h, w, WINDOW, d)

            def look_around(t):
                p = jnp.pad(t, ((0, 0), (0, 0), (1, 0), (0, 0), (0, 0)))
                return jnp.concatenate([p[:, :, :w], p[:, :, 1:]], axis=3)
            bk, bv = (look_around(bk), look_around(bv))
            bt = jnp.arange(n).reshape(w, WINDOW)
            btp = jnp.pad(bt, ((1, 0), (0, 0)), constant_values=-1)
            btk = jnp.concatenate([btp[:w], btp[1:]], axis=1)
            sim = jnp.einsum('bhwid,bhwjd->bhwij', bq, bk)
            i = bt[:, :, None]
            j = btk[:, None, :]
            mask = (i < j) | (i > j + WINDOW) | (j == -1)
            sim = jnp.where(mask, -jnp.finfo(sim.dtype).max, sim)
            attn = jax.nn.softmax(sim, axis=-1)
            out = jnp.einsum('bhwij,bhwjd->bhwid', attn, bv)
            return out.reshape(b, h, n, d)

        def _layer(x, wqkv, qs, ksc, wo, lg, lb, w1, b1, w2, b2):
            b, n, _ = x.shape
            h = shift_token(x)
            qkv = h @ wqkv
            q, k, v = jnp.split(qkv, 3, axis=-1)
            to_heads = lambda t: t.reshape(b, n, HEADS, DIM_HEAD).transpose(0, 2, 1, 3)
            q, k, v = (to_heads(q), to_heads(k), to_heads(v))
            q = l2norm(q) * qs
            k = l2norm(k) * ksc
            q, k = rotary_xpos(q, k)
            o = local_attention(q, k, v)
            o = o.transpose(0, 2, 1, 3).reshape(b, n, INNER)
            x = x + o @ wo
            h = shift_token(x)
            mu = h.mean(-1, keepdims=True)
            var = h.var(-1, keepdims=True)
            h = (h - mu) / jnp.sqrt(var + 1e-05) * lg + lb
            h = h @ w1 + b1
            a, g = jnp.split(h, 2, axis=-1)
            h = a * jax.nn.gelu(g, approximate=False)
            x = x + h @ w2 + b2
            return x
        key = jax.random.key(seed)
        ks = jax.random.split(key, 6)
        return {'x': jax.random.normal(ks[0], (B, N, DIM), jnp.float32), 'wqkv': jax.random.normal(ks[1], (DEPTH, DIM, 3 * INNER), jnp.float32) * 0.02, 'q_scale': jnp.ones((DEPTH, DIM_HEAD), jnp.float32), 'k_scale': jnp.ones((DEPTH, DIM_HEAD), jnp.float32), 'wo': jax.random.normal(ks[2], (DEPTH, INNER, DIM), jnp.float32) * 0.02, 'ln_g': jnp.ones((DEPTH, DIM), jnp.float32), 'ln_b': jnp.zeros((DEPTH, DIM), jnp.float32), 'w1': jax.random.normal(ks[3], (DEPTH, DIM, 2 * HID), jnp.float32) * 0.02, 'b1': jnp.zeros((DEPTH, 2 * HID), jnp.float32), 'w2': jax.random.normal(ks[4], (DEPTH, HID, DIM), jnp.float32) * 0.02, 'b2': jnp.zeros((DEPTH, DIM), jnp.float32)}
    _L1_ffn_all = _L1_ffn_setup()
    _L1_ffn_in = {k: v for k, v in _L1_ffn_all.items() if k in ('wqkv', 'q_scale', 'k_scale', 'wo', 'ln_g', 'ln_b', 'w1', 'b1', 'w2', 'b2')}
    del _L1_ffn_all
    return {'x': x, 'cond_8': cond_8, 'L0_cond_W_base': _L0_cond_in['W_base'], 'L0_cond_b_base': _L0_cond_in['b_base'], 'L0_cond_As': _L0_cond_in['As'], 'L0_cond_Bs': _L0_cond_in['Bs'], 'L0_ffn_ln_gamma': _L0_ffn_in['ln_gamma'], 'L0_ffn_ln_beta': _L0_ffn_in['ln_beta'], 'L0_ffn_Wr': _L0_ffn_in['Wr'], 'L0_ffn_W12': _L0_ffn_in['W12'], 'L0_ffn_W3': _L0_ffn_in['W3'], 'L1_cond_skill_gate': _L1_cond_in['skill_gate'], 'L1_cond_skill_up': _L1_cond_in['skill_up'], 'L1_cond_skill_down': _L1_cond_in['skill_down'], 'L1_cond_shared_gate': _L1_cond_in['shared_gate'], 'L1_cond_shared_up': _L1_cond_in['shared_up'], 'L1_cond_shared_down': _L1_cond_in['shared_down'], 'L1_ffn_wqkv': _L1_ffn_in['wqkv'], 'L1_ffn_q_scale': _L1_ffn_in['q_scale'], 'L1_ffn_k_scale': _L1_ffn_in['k_scale'], 'L1_ffn_wo': _L1_ffn_in['wo'], 'L1_ffn_ln_g': _L1_ffn_in['ln_g'], 'L1_ffn_ln_b': _L1_ffn_in['ln_b'], 'L1_ffn_w1': _L1_ffn_in['w1'], 'L1_ffn_b1': _L1_ffn_in['b1'], 'L1_ffn_w2': _L1_ffn_in['w2'], 'L1_ffn_b2': _L1_ffn_in['b2']}

def reference(x, cond_8, L0_cond_W_base, L0_cond_b_base, L0_cond_As, L0_cond_Bs, L0_ffn_ln_gamma, L0_ffn_ln_beta, L0_ffn_Wr, L0_ffn_W12, L0_ffn_W3, L1_cond_skill_gate, L1_cond_skill_up, L1_cond_skill_down, L1_cond_shared_gate, L1_cond_shared_up, L1_cond_shared_down, L1_ffn_wqkv, L1_ffn_q_scale, L1_ffn_k_scale, L1_ffn_wo, L1_ffn_ln_g, L1_ffn_ln_b, L1_ffn_w1, L1_ffn_b1, L1_ffn_w2, L1_ffn_b2):
    import jax
    import jax.numpy as jnp

    def _L0_cond_ref(x, w, W_base, b_base, As, Bs):
        import jax, jax.numpy as jnp
        import numpy as np
        R = 16
        ALPHA = 32.0
        SCALING = ALPHA / R
        out = jnp.einsum('btc,oc->bto', x, W_base) + b_base
        h = jnp.einsum('btc,erc->bter', x, As)
        lora = jnp.einsum('bter,eor,be->bto', h, Bs, w)
        return out + lora * SCALING

    def _L0_ffn_ref(x, ln_gamma, ln_beta, Wr, W12, W3):
        import math
        import jax, jax.numpy as jnp
        import numpy as np
        D_MODEL = 128
        D_FF = 512
        E = 8
        K = 2
        CF = 1.25
        CLAMP = 10000.0
        B, S, D = x.shape
        T = B * S
        xf = x.reshape(T, D)
        mu = xf.mean(-1, keepdims=True)
        var = ((xf - mu) ** 2).mean(-1, keepdims=True)
        xn = (xf - mu) / jnp.sqrt(var + 1e-05) * ln_gamma + ln_beta
        logits = jnp.clip(xn @ Wr.T, -CLAMP, CLAMP)
        m = logits.max(-1, keepdims=True)
        ex = jnp.exp(logits - m)
        probs = ex / (ex.sum(-1, keepdims=True) + 1e-12)
        top_p, top_i = jax.lax.top_k(probs, K)
        Sslots = T * K
        experts = top_i.reshape(-1)
        weights = top_p.reshape(-1)
        tokens = jnp.repeat(jnp.arange(T, dtype=jnp.int32), K)
        order = jnp.argsort(experts, stable=True)
        e_s = experts[order]
        w_s = weights[order]
        t_s = tokens[order]
        counts = jnp.bincount(e_s, length=E)
        offsets = jnp.concatenate([jnp.zeros((1,), counts.dtype), jnp.cumsum(counts)])
        rank = jnp.arange(Sslots, dtype=counts.dtype) - offsets[e_s]
        cap = max(1, math.ceil(math.ceil(T * K * CF) / E))
        kept = rank < cap
        pos = jnp.where(kept, rank, cap)
        buf = jnp.zeros((E, cap, D), x.dtype).at[e_s, pos].set(xn[t_s], mode='drop')
        gu = jnp.einsum('ecd,efd->ecf', buf, W12)
        g, u = (gu[..., :D_FF], gu[..., D_FF:])
        h = jax.nn.silu(g) * u
        y = jnp.einsum('ecf,edf->ecd', h, W3)
        y_slot = y[e_s, jnp.minimum(pos, cap - 1)] * (w_s * kept.astype(x.dtype))[:, None]
        out = jnp.zeros((T, D), x.dtype).at[t_s].add(y_slot)
        return out.reshape(B, S, D)

    def _L1_cond_ref(x, router_logits, skill_gate, skill_up, skill_down, shared_gate, shared_up, shared_down):
        import jax, jax.numpy as jnp
        import numpy as np
        TOP_K = 2
        NUM_MOE_LAYERS = 12

        def _gemma_mlp(x, gate_w, up_w, down_w):
            g = jnp.einsum('bsh,hi->bsi', x, gate_w)
            u = jnp.einsum('bsh,hi->bsi', x, up_w)
            return jnp.einsum('bsi,ih->bsh', jax.nn.gelu(g, approximate=True) * u, down_w)
        B = x.shape[0]
        E = skill_gate.shape[0]
        rw = jax.nn.softmax(router_logits.astype(jnp.float32), axis=-1)
        w, sel = jax.lax.top_k(rw, TOP_K)
        w = w / w.sum(axis=-1, keepdims=True)
        w = w.astype(x.dtype)
        scale = 1.0 / NUM_MOE_LAYERS
        w = scale * w + (1.0 - scale) * jax.lax.stop_gradient(w)
        dense_w = jnp.zeros((B, E), x.dtype).at[jnp.arange(B)[:, None], sel].add(w)

        def step(acc, params):
            g, u, d, we = params
            return (acc + we[:, None, None] * _gemma_mlp(x, g, u, d), None)
        out, _ = jax.lax.scan(step, jnp.zeros_like(x), (skill_gate, skill_up, skill_down, dense_w.T))
        out = out + _gemma_mlp(x, shared_gate, shared_up, shared_down)
        return out

    def _L1_ffn_ref(x, wqkv, q_scale, k_scale, wo, ln_g, ln_b, w1, b1, w2, b2):
        import jax, jax.numpy as jnp
        import numpy as np
        DIM = 128
        DEPTH = 2
        HEADS = 8
        DIM_HEAD = 64
        WINDOW = 64
        INNER = HEADS * DIM_HEAD
        HID = int(DIM * 4 * 2 / 3)
        B, N = (2, 1024)
        QK_SCALE = 8.0

        def shift_token(t):
            t1, t2 = jnp.split(t, 2, axis=-1)
            t2 = jnp.pad(t2, ((0, 0), (1, 0), (0, 0)))[:, :-1]
            return jnp.concatenate([t1, t2], axis=-1)

        def l2norm(t):
            return t / jnp.clip(jnp.linalg.norm(t, axis=-1, keepdims=True), 1e-12)

        def rotate_half(x):
            x1, x2 = jnp.split(x, 2, axis=-1)
            return jnp.concatenate([-x2, x1], axis=-1)

        def rotary_xpos(q, k):
            n = q.shape[-2]
            half_idx = jnp.arange(0, DIM_HEAD, 2, dtype=jnp.float32)
            inv_freq = 1.0 / 10000.0 ** (half_idx / DIM_HEAD)
            t = jnp.arange(n, dtype=jnp.float32)
            freqs = t[:, None] * inv_freq[None, :]
            freqs = jnp.concatenate([freqs, freqs], axis=-1)
            base = (half_idx + 0.4 * DIM_HEAD) / (1.4 * DIM_HEAD)
            power = (t - n // 2) / float(WINDOW // 2)
            scale = base[None, :] ** power[:, None]
            scale = jnp.concatenate([scale, scale], axis=-1)
            cos, sin = (jnp.cos(freqs), jnp.sin(freqs))
            q = q * cos * scale + rotate_half(q) * sin * scale
            k = k * cos / scale + rotate_half(k) * sin / scale
            return (q, k)

        def local_attention(q, k, v):
            b, h, n, d = q.shape
            w = n // WINDOW
            bq = q.reshape(b, h, w, WINDOW, d) * QK_SCALE
            bk = k.reshape(b, h, w, WINDOW, d)
            bv = v.reshape(b, h, w, WINDOW, d)

            def look_around(t):
                p = jnp.pad(t, ((0, 0), (0, 0), (1, 0), (0, 0), (0, 0)))
                return jnp.concatenate([p[:, :, :w], p[:, :, 1:]], axis=3)
            bk, bv = (look_around(bk), look_around(bv))
            bt = jnp.arange(n).reshape(w, WINDOW)
            btp = jnp.pad(bt, ((1, 0), (0, 0)), constant_values=-1)
            btk = jnp.concatenate([btp[:w], btp[1:]], axis=1)
            sim = jnp.einsum('bhwid,bhwjd->bhwij', bq, bk)
            i = bt[:, :, None]
            j = btk[:, None, :]
            mask = (i < j) | (i > j + WINDOW) | (j == -1)
            sim = jnp.where(mask, -jnp.finfo(sim.dtype).max, sim)
            attn = jax.nn.softmax(sim, axis=-1)
            out = jnp.einsum('bhwij,bhwjd->bhwid', attn, bv)
            return out.reshape(b, h, n, d)

        def _layer(x, wqkv, qs, ksc, wo, lg, lb, w1, b1, w2, b2):
            b, n, _ = x.shape
            h = shift_token(x)
            qkv = h @ wqkv
            q, k, v = jnp.split(qkv, 3, axis=-1)
            to_heads = lambda t: t.reshape(b, n, HEADS, DIM_HEAD).transpose(0, 2, 1, 3)
            q, k, v = (to_heads(q), to_heads(k), to_heads(v))
            q = l2norm(q) * qs
            k = l2norm(k) * ksc
            q, k = rotary_xpos(q, k)
            o = local_attention(q, k, v)
            o = o.transpose(0, 2, 1, 3).reshape(b, n, INNER)
            x = x + o @ wo
            h = shift_token(x)
            mu = h.mean(-1, keepdims=True)
            var = h.var(-1, keepdims=True)
            h = (h - mu) / jnp.sqrt(var + 1e-05) * lg + lb
            h = h @ w1 + b1
            a, g = jnp.split(h, 2, axis=-1)
            h = a * jax.nn.gelu(g, approximate=False)
            x = x + h @ w2 + b2
            return x
        for l in range(DEPTH):
            x = _layer(x, wqkv[l], q_scale[l], k_scale[l], wo[l], ln_g[l], ln_b[l], w1[l], b1[l], w2[l], b2[l])
        return x
    x = x + _L0_ffn_ref(_L0_cond_ref(x, cond_8, L0_cond_W_base, L0_cond_b_base, L0_cond_As, L0_cond_Bs), L0_ffn_ln_gamma, L0_ffn_ln_beta, L0_ffn_Wr, L0_ffn_W12, L0_ffn_W3)
    x = x + _L1_ffn_ref(_L1_cond_ref(x, cond_8, L1_cond_skill_gate, L1_cond_skill_up, L1_cond_skill_down, L1_cond_shared_gate, L1_cond_shared_up, L1_cond_shared_down), L1_ffn_wqkv, L1_ffn_q_scale, L1_ffn_k_scale, L1_ffn_wo, L1_ffn_ln_g, L1_ffn_ln_b, L1_ffn_w1, L1_ffn_b1, L1_ffn_w2, L1_ffn_b2)
    return x

_drawn_inputs = setup_inputs


def setup_inputs(seed=0):
    import zlib

    import numpy as np

    out = dict(_drawn_inputs(seed))
    spreads = {'L0_ffn_ln_gamma': (1.0, 0.6),
     'L0_ffn_ln_beta': (0.0, 0.624),
     'L1_ffn_q_scale': (1.0, 0.6),
     'L1_ffn_k_scale': (1.0, 0.6),
     'L1_ffn_ln_g': (1.0, 0.6),
     'L1_ffn_ln_b': (0.0, 0.8),
     'L1_ffn_b1': (0.0, 0.8),
     'L1_ffn_b2': (0.0, 0.1)}
    factors = {'cond_8': 3.488,
     'L0_cond_b_base': 5.854,
     'L0_cond_As': 2.991,
     'L0_cond_Bs': 2.999,
     'L1_cond_skill_gate': 4.714,
     'L1_cond_skill_up': 4.655,
     'L1_cond_skill_down': 4.65,
     'L1_cond_shared_gate': 3.49,
     'L1_cond_shared_up': 3.452,
     'L1_cond_shared_down': 3.445,
     'L1_ffn_wqkv': 5.096,
     'L1_ffn_wo': 5.647,
     'L1_ffn_w1': 3.301,
     'L1_ffn_w2': 2.958}
    for name, (base, spread) in spreads.items():
        noise = np.random.default_rng([zlib.crc32(name.encode()), seed]).standard_normal(out[name].shape)
        drawn = base * np.exp(spread * noise) if base else spread * noise
        out[name] = jnp.asarray(drawn.astype(out[name].dtype))
    for name, factor in factors.items():
        out[name] = (out[name] * factor).astype(out[name].dtype)
    return out
```

```python
import numpy as np

import concourse.bass as bass
from concourse import mybir
from concourse.alu_op_type import AluOpType as ALU

F32 = mybir.dt.float32
BF16 = mybir.dt.bfloat16
I32 = mybir.dt.int32
U32 = mybir.dt.uint32
ACT = mybir.ActivationFunctionType
X = mybir.AxisListType.X

B, S, D = 16, 128, 128
T = B * S
E = 8
RANK = 16
LORA_SCALE = 32.0 / RANK
FF = 512
NF = FF // 128
CAP = -(-(-(-T * 2 * 5 // 4)) // E)
NSLOT = E * CAP
NCH = CAP // 128
HALF = (3 * 128, 2 * 128)
HEADS, DH = 8, 64
INNER = HEADS * DH
HID = int(D * 4 * 2 / 3)
HCH = [(0, 128), (128, 128), (256, HID - 256)]
DEPTH = 2
WINDOW = 64
NV = DEPTH * B
G = 4
NG = B // G
DROP = float(1 << 20)
MASKED = -1e30


def constants():
    f = np.float32
    eye = np.eye(128, dtype=f)
    shift = np.eye(128, k=1, dtype=f)
    i, j = np.arange(128)[:, None], np.arange(128)[None, :]
    mask = np.where((i < j) | (i > j + WINDOW), MASKED, 0.0).astype(f)
    before = (i < j).astype(f)
    half = np.arange(0, DH, 2, dtype=f)
    inv = (f(1.0) / f(10000.0) ** (half / f(DH))).astype(f)
    t = np.arange(S, dtype=f)
    freqs = t[:, None] * inv[None, :]
    freqs = np.concatenate([freqs, freqs], -1).astype(f)
    base = (half + f(0.4 * DH)) / f(1.4 * DH)
    power = (t - S // 2) / f(WINDOW // 2)
    sc = (base[None, :].astype(f) ** power[:, None].astype(f)).astype(f)
    sc = np.concatenate([sc, sc], -1)
    cos, sin = np.cos(freqs).astype(f), np.sin(freqs).astype(f)
    sign = np.where(np.arange(DH) < DH // 2, -1.0, 1.0).astype(f)
    qk = np.stack([sc * f(8.0), f(1.0) / sc], 1)
    rot = np.stack([cos[:, None] * qk, (sin * sign)[:, None] * qk], 1).astype(f)
    e = np.arange(E, dtype=f)
    table = np.zeros((3, B, E), f)
    table[0] = E - e
    table[1] = e
    table[2] = e * CAP
    return {"eye": eye, "shift": shift, "masks": np.stack([mask, before], 1), "rotary": np.ascontiguousarray(rot),
            "table": table.reshape(1, -1)}


def build(nc, a, out_dram):
    from contextlib import ExitStack
    stack = ExitStack()
    with stack:
        def sb(name, shape, dt=F32, ctx=stack):
            return ctx.enter_context(nc.sbuf_tensor(name, shape, dt))

        def sem(name, ctx=stack):
            return ctx.enter_context(nc.semaphore(name))

        xbuf = nc.dram_tensor("xbuf", (NSLOT, D), F32, kind="Internal").ap()
        ybuf = nc.dram_tensor("ybuf", (NSLOT, D), F32, kind="Internal").ap()
        g = {}
        bank = stack.enter_context(nc.psum_tensor("bank", [128, 8, 512], F32))
        g["eye"] = sb("eye", [128, 128])
        g["shift"] = sb("shift", [128, 128])
        g["mask"] = sb("mask", [128, 128], BF16)
        g["eye16"] = sb("eye16", [128, 128], BF16)
        g["nhalf"] = sb("nhalf", [128, 1])
        g["wg"] = sb("wg", [128, E + 1, FF])
        g["wu"] = sb("wu", [128, E + 1, FF])
        g["wd"] = sb("wd", [128, E + 1, NF * D])
        g["wqkv"] = sb("wqkv", [128, DEPTH, 3 * INNER])
        g["wo"] = sb("wo", [128, DEPTH, NF * D])
        g["w1"] = sb("w1", [128, DEPTH, 2 * HID])
        g["b1"] = sb("b1", [128, DEPTH, 2 * HID])
        g["w2"] = sb("w2", [128, DEPTH, 3 * D])
        g["b2"] = sb("b2", [128, DEPTH, D])
        g["lngb"] = sb("lngb", [128, DEPTH, 2])
        g["rot"] = sb("rot", [128, 2, DEPTH, 2 * DH])
        g["x1"] = sb("x1_all", [128, B, D])
        g["ctok"] = sb("ctok", [128, 3 * B, D])
        g["xtok"] = g["ctok"][:, 2 * B:, :]
        g["cT"] = sb("cT", [128, 3 * B, S])
        g["sel"] = sb("sel", [128, B, 2], I32)
        g["selw"] = sb("selw", [128, B, 2])
        g["cT_ready"] = sem("cT_ready")
        g["ctok_ready"] = sem("ctok_ready")
        g["late"] = sem("late_weights")
        route(nc, a, g, bank, xbuf, stack, sb, sem)
        experts(nc, a, g, bank, xbuf, ybuf, sb, sem)
        with ExitStack() as own:
            sequence_experts(nc, g, bank, ybuf, own, sb, sem)
        with ExitStack() as own:
            transformer(nc, g, bank, out_dram, own, sb, sem)


LATE = [("wg", "wg"), ("wu", "wu"), ("wd", "wd"), ("wqkv", "wqkv"), ("wo", "wo"), ("w1", "w1"),
        ("w2", "w2"), ("lngb", "lngb"), ("shift", "shift")]
LATE_ROWS = [("b1", DEPTH * 2 * HID), ("b2", DEPTH * D)]
N_LATE = 16 * (len(LATE) + len(LATE_ROWS))


def route(nc, a, g, bank, xbuf, stack, sb, sem):
    from contextlib import ExitStack
    g["gidx"] = sb("gidx", [128, 2, B], U32)
    g["gw"] = sb("gw", [128, 2, B])
    with ExitStack() as own:
        xT = sb("xT", [128, T], ctx=own)
        AsT = sb("AsT", [128, 128], ctx=own)
        BsT = sb("BsT", [128, 128], ctx=own)
        WbT = sb("WbT", [128, 128], ctx=own)
        WrT = sb("WrT", [128, E], ctx=own)
        wcol = sb("wcol", [128, B], ctx=own)
        rows = sb("rows", [128, 3, D], ctx=own)
        cond = sb("cond", [128, B, E], ctx=own)
        table = sb("table_sb", [128, 3, B, E], ctx=own)
        qs = sb("qs", [128, DEPTH, 2 * DH], ctx=own)
        rotc = sb("rotc", [128, 2, 2 * DH], ctx=own)
        masks = sb("masks", [128, 2, 128], ctx=own)
        before = sb("before", [128, 128], BF16, ctx=own)
        ones = sb("ones", [128, 128], BF16, ctx=own)
        hs = sb("hs", [128, 2, G * S], ctx=own)
        c0 = sb("c0", [128, 2, G, D], ctx=own)
        stats = sb("stats", [128, 2, G, 6], ctx=own)
        mv = sb("mv", [128, 2, G, 2], ctx=own)
        rstd = sb("rstd", [128, 2, G], ctx=own)
        xh = sb("xh", [128, 2, G, D], ctx=own)
        xg = sb("xg", [128, G, D], ctx=own)
        xn = sb("xn", [128, B, D], ctx=own)
        xnT = sb("xnT", [128, 2, G * S], ctx=own)
        zero = sb("zero", [128, NSLOT * D // 512], ctx=own)
        lg = sb("lg", [128, B, E], ctx=own)
        ex = sb("ex", [128, B, E], ctx=own)
        pr = sb("pr", [128, B, E], ctx=own)
        pr2 = sb("pr2", [128, B, E], ctx=own)
        oh = sb("oh", [128, 2, B, E], ctx=own)
        tmp = sb("tmp", [128, B, E], ctx=own)
        tmp2 = sb("tmp2", [128, B, E], ctx=own)
        tmp3 = sb("tmp3", [128, B, E], ctx=own)
        both = sb("both", [128, B, E], BF16, ctx=own)
        col = sb("col", [128, 8, B], ctx=own)
        sidx = sb("sidx", [128, 2, B], U32, ctx=own)

        first = sem("first_loads", own)
        xin = [sem(f"x_loads{i}", own) for i in range(NG)]
        early = sem("early_loads", own)
        zeroed = sem("zero_tile", own)
        cleared = sem("xbuf_cleared", own)
        h_ps, hs_sb = sem("h_ps", own), sem("hs_sb", own)
        c0_ps, c0_sb = sem("c0_ps", own), sem("c0_sb", own)
        st_done, mv_done, rstd_done = sem("st_done", own), sem("mv_done", own), sem("rstd_done", own)
        xh_done, xg_done, xn_done = sem("xh_done", own), sem("xg_done", own), sem("xn_done", own)
        xnT_ps, xnT_sb, lg_ps = sem("xnT_ps", own), sem("xnT_sb", own), sem("lg_ps", own)
        chain = sem("router_steps", own)
        lg_ready, ex_ready = sem("lg_ready", own), sem("ex_ready", own)
        both_ready, rank_ps = sem("both_ready", own), sem("rank_ps", own)
        sidx_ready, scattered = sem("sidx_ready", own), sem("scattered", own)
        small = sem("small_constants", own)
        nh_done, rot_done = sem("nh_done", own), sem("rot_done", own)

        with nc.Block() as block:
            @block.sync
            def _(sp):
                sp.dma_start(AsT[:], a["AsT"]).then_inc(first, 16)
                sp.dma_start(xT[:, 0:G * S], a["xT"][:, 0:G * S]).then_inc(xin[0], 16)
                sp.dma_start(wcol[:], a["wcol"]).then_inc(first, 16)
                sp.dma_start(WbT[:], a["WbT"]).then_inc(first, 16)
                sp.dma_start(BsT[:], a["BsT"]).then_inc(first, 16)
                sp.dma_start(rows[:].rearrange("p a d -> p (a d)"),
                             a["rows"][0, :].partition_broadcast(128)).then_inc(first, 16)
                for i in range(1, NG):
                    sp.dma_start(xT[:, i * G * S:(i + 1) * G * S],
                                 a["xT"][:, i * G * S:(i + 1) * G * S]).then_inc(xin[i], 16)
                sp.dma_start(g["eye"][:], a["eye"]).then_inc(early, 16)
                sp.dma_start(WrT[:], a["WrT"]).then_inc(early, 16)
                sp.dma_start(cond[:].rearrange("p b e -> p (b e)"),
                             a["cond"][0, :].partition_broadcast(128)).then_inc(early, 16)
                sp.dma_start(table[:].rearrange("p k b e -> p (k b e)"),
                             a["table"][0, :].partition_broadcast(128)).then_inc(early, 16)
                sp.dma_start(masks[:], a["masks"]).then_inc(early, 16)
                sp.dma_start(qs[:].rearrange("p l d -> p (l d)"),
                             a["qs"][0, :].partition_broadcast(128)).then_inc(early, 16)
                sp.dma_start(rotc[:], a["rotary"]).then_inc(early, 16)
                sp.dma_start(g["xtok"], a["xtok"]).then_inc(early, 16)
                sp.wait_ge(zeroed, 1)
                for i in range(4):
                    sp.dma_start(xbuf.rearrange("(q p r) d -> q p (r d)", q=4, p=128)[i],
                                 zero[:]).then_inc(cleared, 16)
                for sbuf, dram in LATE:
                    sp.dma_start(g[sbuf][:], a[dram]).then_inc(g["late"], 16)
                for name, n in LATE_ROWS:
                    sp.dma_start(g[name][:].rearrange("p l d -> p (l d)"),
                                 a[name][0, :].partition_broadcast(128)).then_inc(g["late"], 16)

            @block.tensor
            def _(pe):
                pe.wait_ge(first, 80)
                for i in range(NG):
                    tok = slice(i * G * S, (i + 1) * G * S)
                    pe.wait_ge(xin[i], 16)
                    if i >= 2:
                        pe.wait_ge(hs_sb, i - 1)
                    nc.tensor.matmul(bank[:, i % 2, :], AsT[:], xT[:, tok], start=True, stop=True).then_inc(h_ps, 1)
                    pe.wait_ge(hs_sb, i + 1)
                    if i >= 2:
                        pe.wait_ge(c0_sb, i - 1)
                    for t in range(G):
                        o = bank[:, 2 + i % 2, t * D:(t + 1) * D]
                        nc.tensor.matmul(o, xT[:, i * G * S + t * S:i * G * S + (t + 1) * S], WbT[:],
                                         start=True, stop=False)
                        last = nc.tensor.matmul(o, hs[:, i % 2, t * S:(t + 1) * S], BsT[:], start=False, stop=True)
                    last.then_inc(c0_ps, 1)
                pe.wait_ge(early, 128)
                for i in range(NG):
                    pe.wait_ge(xn_done, i + 1)
                    if i >= 2:
                        pe.wait_ge(xnT_sb, i - 1)
                    for t in range(G):
                        last = nc.tensor.transpose(bank[:, 4 + i % 2, t * S:(t + 1) * S], xn[:, i * G + t, :],
                                                   g["eye"][:])
                    last.then_inc(xnT_ps, 1)
                    pe.wait_ge(xnT_sb, i + 1)
                    for t in range(G):
                        n = i * G + t
                        last = nc.tensor.matmul(bank[:, 6, n * E:(n + 1) * E], xnT[:, i % 2, t * S:(t + 1) * S],
                                                WrT[:], start=True, stop=True)
                    last.then_inc(lg_ps, 1)
                pe.wait_ge(both_ready, 1)
                pe.wait_ge(small, 2)
                nc.tensor.matmul(bank[:, 7, 0:B * E], before[:], both[:].rearrange("p b e -> p (b e)"),
                                 start=True, stop=False)
                for t in range(B - 1):
                    last = nc.tensor.matmul(bank[:, 7, (t + 1) * E:B * E], ones[:],
                                            both[:, t:t + 1, :].to_broadcast([128, B - 1 - t, E]),
                                            start=False, stop=(t == B - 2))
                last.then_inc(rank_ps, 1)

            @block.scalar
            def _(act):
                act.wait_ge(early, 128)
                nc.scalar.copy(g["eye16"][:], g["eye"][:])
                nc.scalar.copy(g["mask"][:], masks[:, 0, :])
                nc.scalar.copy(before[:], masks[:, 1, :]).then_inc(small, 1)
                for i in range(NG):
                    act.wait_ge(xnT_ps, i + 1)
                    if i >= 2:
                        act.wait_ge(lg_ps, i - 1)
                    nc.scalar.copy(xnT[:, i % 2, :], bank[:, 4 + i % 2, :]).then_inc(xnT_sb, 1)
                for i in range(2):
                    act.wait_ge(lg_ready, i + 1)
                    nc.scalar.activation(ex[:], lg[:], ACT.Exp).then_inc(ex_ready, 1)

            @block.gpsimd
            def _(pool):
                nc.gpsimd.memset(zero[:], 0.0).then_inc(zeroed, 1)
                nc.gpsimd.memset(ones[:], 1.0).then_inc(small, 1)
                nc.gpsimd.memset(g["nhalf"][:], -0.5).then_inc(nh_done, 1)
                nc.gpsimd.memset(g["cT"][:, :, 0:1], 0.0).then_inc(nh_done, 1)
                pool.wait_ge(nh_done, 2)
                pool.wait_ge(first, 80)
                for i in range(NG):
                    pool.wait_ge(mv_done, i + 1)
                    nc.gpsimd.tensor_tensor(rstd[:, i % 2, :], mv[:, i % 2, :, 1],
                                            g["nhalf"][:].to_broadcast([128, G]), ALU.pow).then_inc(rstd_done, 1)
                    pool.wait_ge(xh_done, i + 1)
                    if i >= 1:
                        pool.wait_ge(xn_done, i)
                    nc.gpsimd.tensor_tensor(xg[:], xh[:, i % 2], rows[:, 1:2, :].to_broadcast([128, G, D]),
                                            ALU.mult).then_inc(xg_done, 1)
                    pool.wait_ge(xg_done, i + 1)
                    nc.gpsimd.tensor_tensor(xn[:, i * G:(i + 1) * G, :], xg[:],
                                            rows[:, 2:3, :].to_broadcast([128, G, D]), ALU.add).then_inc(xn_done, 1)
                pool.wait_ge(early, 128)
                for l in range(DEPTH):
                    nc.gpsimd.tensor_tensor(g["rot"][:, 0, l, :], rotc[:, 0, :], qs[:, l, :], ALU.mult).then_inc(rot_done, 1)
                    for h in range(2):
                        pick = lambda t, k: t.rearrange("p (w h d) -> p w h d", w=2, h=2)[:, :, k, :]
                        nc.gpsimd.tensor_tensor(pick(g["rot"][:, 1, l, :], h), pick(rotc[:, 1, :], h),
                                                pick(qs[:, l, :], 1 - h), ALU.mult).then_inc(rot_done, 1)
                pool.wait_ge(sidx_ready, 2)
                pool.wait_ge(cleared, 64)
                for t in range(B):
                    for k in range(2):
                        nc.gpsimd.indirect_dma_start(
                            xbuf, bass.IndirectOffsetOnAxis(ap=sidx[:, k, t:t + 1], axis=0), xn[:, t, :], None,
                            bounds_check=NSLOT - 1, oob_is_err=False).then_inc(scattered, 16)
                pool.wait_ge(scattered, 2 * B * 16)

            @block.vector
            def _(dve):
                steps = [0]

                def then(ins):
                    steps[0] += 1
                    ins.then_inc(chain, 1)
                    dve.wait_ge(chain, steps[0])

                def per_tile(c):
                    return c.unsqueeze(2).to_broadcast([128, B, E])

                def softmax_top2(exps, eps, w_out):
                    then(nc.vector.reduce_sum(col[:, 1, :], exps[:], X))
                    if eps:
                        then(nc.vector.tensor_scalar_add(col[:, 1, :], col[:, 1, :], eps))
                    then(nc.vector.reciprocal(col[:, 2, :], col[:, 1, :]))
                    then(nc.vector.tensor_tensor(pr[:], exps[:], per_tile(col[:, 2, :]), ALU.mult))
                    for k, p in enumerate((pr, pr2)):
                        then(nc.vector.reduce_max(w_out[:, k, :], p[:], X))
                        then(nc.vector.tensor_tensor(tmp[:], p[:], per_tile(w_out[:, k, :]), ALU.is_equal))
                        then(nc.vector.tensor_tensor(tmp2[:], tmp[:], table[:, 0], ALU.mult))
                        then(nc.vector.reduce_max(col[:, 3, :], tmp2[:], X))
                        then(nc.vector.tensor_tensor(oh[:, k], tmp2[:], per_tile(col[:, 3, :]), ALU.is_equal))
                        if k == 0:
                            then(nc.vector.scalar_tensor_tensor(
                                out=pr2[:].rearrange("p b e -> p (b e)"), in0=oh[:, 0].rearrange("p b e -> p (b e)"),
                                scalar=-4.0, in1=pr[:].rearrange("p b e -> p (b e)"), op0=ALU.mult, op1=ALU.add))

                dve.wait_ge(first, 80)
                dve.wait_ge(early, 128)
                then(nc.vector.reduce_max(col[:, 0, :], cond[:], X))
                nc.vector.tensor_tensor(lg[:], cond[:], per_tile(col[:, 0, :]), ALU.subtract).then_inc(lg_ready, 1)
                for i in range(NG):
                    dve.wait_ge(h_ps, i + 1)
                    if i >= 2:
                        dve.wait_ge(c0_ps, i - 1)
                    nc.vector.scalar_tensor_tensor(
                        out=hs[:, i % 2, :].rearrange("p (t s) -> p t s", t=G),
                        in0=bank[:, i % 2, :].rearrange("p (t s) -> p t s", t=G), scalar=LORA_SCALE,
                        in1=wcol[:, i * G:(i + 1) * G].unsqueeze(2).to_broadcast([128, G, S]),
                        op0=ALU.mult, op1=ALU.mult).then_inc(hs_sb, 1)
                    dve.wait_ge(c0_ps, i + 1)
                    if i >= 2:
                        dve.wait_ge(xh_done, i - 1)
                    nc.vector.tensor_tensor(c0[:, i % 2], bank[:, 2 + i % 2, :].rearrange("p (t d) -> p t d", t=G),
                                            rows[:, 0:1, :].to_broadcast([128, G, D]), ALU.add).then_inc(c0_sb, 1)
                    dve.wait_ge(c0_sb, i + 1)
                    for t in range(G):
                        nc.vector.bn_stats(stats[:, i % 2, t, :], c0[:, i % 2, t, :]).then_inc(st_done, 1)
                    dve.wait_ge(st_done, (i + 1) * G)
                    if i >= 2:
                        dve.wait_ge(rstd_done, i - 1)
                    for t in range(G):
                        last = nc.vector.bn_aggr(mv[:, i % 2, t, :], stats[:, i % 2, t, :])
                    then(last)
                    nc.vector.tensor_scalar_add(mv[:, i % 2, :, 1], mv[:, i % 2, :, 1], 1e-5).then_inc(mv_done, 1)
                    dve.wait_ge(rstd_done, i + 1)
                    if i >= 2:
                        dve.wait_ge(xg_done, i - 1)
                    for t in range(G):
                        last = nc.vector.tensor_scalar(xh[:, i % 2, t, :], c0[:, i % 2, t, :], mv[:, i % 2, t, 0:1],
                                                       rstd[:, i % 2, t:t + 1], ALU.subtract, ALU.mult)
                    last.then_inc(xh_done, 1)
                dve.wait_ge(ex_ready, 1)
                softmax_top2(ex, 0.0, col[:, 4:6])
                then(nc.vector.tensor_tensor(col[:, 6, :], col[:, 4, :], col[:, 5, :], ALU.add))
                then(nc.vector.reciprocal(col[:, 7, :], col[:, 6, :]))
                for k in range(2):
                    then(nc.vector.tensor_tensor(col[:, 4 + k, :], col[:, 4 + k, :], col[:, 7, :], ALU.mult))
                    then(nc.vector.tensor_scalar_mul(col[:, 6, :], col[:, 4 + k, :], 1.0 - 1.0 / 12))
                    then(nc.vector.scalar_tensor_tensor(out=g["selw"][:, :, k], in0=col[:, 4 + k, :], scalar=1.0 / 12,
                                                        in1=col[:, 6, :], op0=ALU.mult, op1=ALU.add))
                    then(nc.vector.tensor_tensor(tmp[:], oh[:, k], table[:, 1], ALU.mult))
                    then(nc.vector.reduce_sum(col[:, 3, :], tmp[:], X))
                    then(nc.vector.tensor_copy(g["sel"][:, :, k], col[:, 3, :]))

                dve.wait_ge(lg_ps, NG)
                logits = bank[:, 6, 0:B * E].rearrange("p (b e) -> p b e", b=B)
                then(nc.vector.tensor_scalar(tmp3[:], logits, 10000.0, -10000.0, ALU.min, ALU.max))
                then(nc.vector.reduce_max(col[:, 0, :], tmp3[:], X))
                nc.vector.tensor_tensor(lg[:], tmp3[:], per_tile(col[:, 0, :]), ALU.subtract).then_inc(lg_ready, 1)
                dve.wait_ge(ex_ready, 2)
                softmax_top2(ex, 1e-12, col[:, 4:6])
                nc.vector.tensor_tensor(both[:], oh[:, 0], oh[:, 1], ALU.add).then_inc(both_ready, 1)
                dve.wait_ge(rank_ps, 1)
                rank = bank[:, 7, 0:B * E].rearrange("p (b e) -> p b e", b=B)
                then(nc.vector.tensor_scalar(tmp[:], rank, float(CAP), None, ALU.is_lt))
                then(nc.vector.tensor_tensor(tmp2[:], rank, table[:, 2], ALU.add))
                then(nc.vector.scalar_tensor_tensor(
                    out=tmp3[:].rearrange("p b e -> p (b e)"), in0=tmp[:].rearrange("p b e -> p (b e)"), scalar=-DROP,
                    in1=tmp2[:].rearrange("p b e -> p (b e)"), op0=ALU.mult, op1=ALU.add))
                for k in range(2):
                    then(nc.vector.tensor_tensor(pr[:], oh[:, k], tmp3[:], ALU.mult))
                    then(nc.vector.reduce_sum(col[:, 0, :], pr[:], X))
                    then(nc.vector.tensor_scalar_add(col[:, 0, :], col[:, 0, :], DROP))
                    nc.vector.tensor_copy(sidx[:, k, :], col[:, 0, :]).then_inc(sidx_ready, 1)
                then(nc.vector.tensor_scalar_add(pr2[:], table[:, 2], CAP - 1.0))
                then(nc.vector.tensor_tensor(tmp2[:], tmp2[:], pr2[:], ALU.min))
                for k in range(2):
                    then(nc.vector.tensor_tensor(pr[:], oh[:, k], tmp2[:], ALU.mult))
                    then(nc.vector.reduce_sum(col[:, 1, :], pr[:], X))
                    nc.vector.tensor_copy(g["gidx"][:, k, :], col[:, 1, :])
                    then(nc.vector.tensor_tensor(pr[:], oh[:, k], tmp[:], ALU.mult))
                    then(nc.vector.reduce_sum(col[:, 2, :], pr[:], X))
                    then(nc.vector.tensor_tensor(g["gw"][:, k, :], col[:, 4 + k, :], col[:, 2, :], ALU.mult))


def experts(nc, a, g, bank, xbuf, ybuf, sb, sem):
    from contextlib import ExitStack
    starts = (0, HALF[0])
    nchunk = tuple(h // 128 for h in HALF)
    with ExitStack() as own:
        w12 = sb("w12", [128, 2, 2 * FF], ctx=own)
        w3 = sb("w3", [128, 2, NF * D], ctx=own)
        xs = sb("xs", [128, 2, NCH, D], ctx=own)
        xsT = sb("xsT", [128, 2, CAP], ctx=own)
        sg = sb("sg", [128, 2, HALF[0]], ctx=own)
        h = sb("h", [128, 2, NF, CAP], ctx=own)
        ys = sb("ys", [128, 2, NCH, D], ctx=own)
        w_in = [sem(f"w_in{i}", own) for i in range(2)]
        x_in = [sem(f"x_in{i}", own) for i in range(2)]
        xsT_ps, xsT_sb = sem("xsT_ps", own), sem("xsT_sb", own)
        gu_ps, sg_sb, h_sb = sem("gu_ps", own), sem("sg_sb", own), sem("h_sb", own)
        y_ps = [sem(f"y_ps{i}", own) for i in range(2)]
        y_sb = [sem(f"y_sb{i}", own) for i in range(2)]
        y_out = [sem(f"y_out{i}", own) for i in range(2)]
        U = 2 * NF

        def turns(eng, step):
            for e in range(2):
                step(e, e)
            with eng.Fori(1, E // 2 - 1) as m:
                for p in range(2):
                    step(m * 2 + p, p)
            for e in range(E - 2, E):
                step(e, e % 2)

        first = lambda e: isinstance(e, int) and e < 1
        fresh = lambda e: isinstance(e, int) and e < 2

        with nc.Block() as block:
            @block.sync
            def _(sp):
                def load(e, p):
                    if not fresh(e):
                        sp.wait_ge(y_ps[1], e - 1)
                    at = bass.ds(e, 1) if not isinstance(e, int) else slice(e, e + 1)
                    rows = bass.ds(e * CAP, CAP) if not isinstance(e, int) else slice(e * CAP, (e + 1) * CAP)
                    sp.dma_start(xs[:, p, :, :], xbuf[rows, :].rearrange("(c p) d -> p c d", p=128)).then_inc(x_in[p], 16)
                    sp.dma_start(w12[:, p:p + 1, :], a["w12"][:, at, :]).then_inc(w_in[p], 16)
                    sp.dma_start(w3[:, p:p + 1, :], a["w3"][:, at, :]).then_inc(w_in[p], 16)
                turns(sp, load)

            @block.tensor
            def _(pe):
                def transpose_x(e, p):
                    pe.wait_ge(x_in[p], ((e - p) // 2 + 1) * 16 if isinstance(e, int) else ((e - p) >> 1) * 16 + 16)
                    if not first(e):
                        pe.wait_ge(xsT_sb, 2 * e)
                    for c in range(NCH):
                        k = 0 if c < nchunk[0] else 1
                        o = c * 128 - starts[k]
                        ins = nc.tensor.transpose(bank[:, 4 + k, o:o + 128], xs[:, p, c, :], g["eye"][:])
                        if c in (nchunk[0] - 1, NCH - 1):
                            ins.then_inc(xsT_ps, 1)

                def gate_up(e, p, k):
                    pe.wait_ge(xsT_sb, 2 * e + k + 1)
                    for f in range(NF):
                        u = k * NF + f
                        if not (first(e) and u < 2):
                            pe.wait_ge(h_sb, e * U + u - 1)
                        for j in range(2):
                            ins = nc.tensor.matmul(bank[:, 2 * (u % 2) + j, 0:HALF[k]],
                                                   w12[:, p, j * FF + f * 128:j * FF + (f + 1) * 128],
                                                   xsT[:, p, starts[k]:starts[k] + HALF[k]], start=True, stop=True)
                        ins.then_inc(gu_ps, 1)

                def down(e, p, k):
                    pe.wait_ge(h_sb, e * U + (k + 1) * NF)
                    if not first(e):
                        pe.wait_ge(y_sb[k], e)
                    for c in range(nchunk[k]):
                        at = starts[k] + c * 128
                        for f in range(NF):
                            ins = nc.tensor.matmul(bank[:, 6 + k, c * D:(c + 1) * D], h[:, p, f, at:at + 128],
                                                   w3[:, p, f * D:(f + 1) * D], start=(f == 0), stop=(f == NF - 1))
                    ins.then_inc(y_ps[k], 1)

                def step(e, p):
                    pe.wait_ge(w_in[p], ((e - p) // 2 + 1) * 32 if isinstance(e, int) else ((e - p) >> 1) * 32 + 32)
                    gate_up(e, p, 0)
                    if not first(e):
                        down(e - 1, 1 - p, 1)
                    if not (isinstance(e, int) and e == E - 1):
                        transpose_x(e + 1, 1 - p)
                    gate_up(e, p, 1)
                    down(e, p, 0)

                transpose_x(0, 0)
                turns(pe, step)
                down(E - 1, (E - 1) % 2, 1)

            @block.scalar
            def _(act):
                def step(e, p):
                    for k in range(2):
                        for f in range(NF):
                            u = k * NF + f
                            act.wait_ge(gu_ps, e * U + u + 1)
                            if not (first(e) and u < 2):
                                act.wait_ge(h_sb, e * U + u - 1)
                            nc.scalar.activation(sg[:, u % 2, 0:HALF[k]], bank[:, 2 * (u % 2), 0:HALF[k]],
                                                 ACT.Silu).then_inc(sg_sb, 1)
                            if u == 1 and not first(e):
                                store(e - 1, 1 - p, 0)
                            if u == NF and not first(e):
                                store(e - 1, 1 - p, 1)

                def store(e, p, k):
                    act.wait_ge(y_ps[k], e + 1)
                    if not fresh(e):
                        act.wait_ge(y_out[p], ((e - p) // 2) * 32 if isinstance(e, int) else ((e - p) >> 1) * 32)
                    c0 = starts[k] // 128
                    nc.scalar.copy(ys[:, p, c0:c0 + nchunk[k], :],
                                   bank[:, 6 + k, 0:nchunk[k] * D].rearrange("p (c d) -> p c d", d=D)).then_inc(y_sb[k], 1)
                    act.wait_ge(y_sb[k], e + 1)
                    rows = bass.ds(e * CAP + starts[k], HALF[k]) if not isinstance(e, int) else \
                        slice(e * CAP + starts[k], e * CAP + starts[k] + HALF[k])
                    act.dma_start(ybuf[rows, :].rearrange("(c p) d -> p c d", p=128),
                                  ys[:, p, c0:c0 + nchunk[k], :]).then_inc(y_out[p], 16)

                turns(act, step)
                for k in range(2):
                    store(E - 1, (E - 1) % 2, k)
                for p in range(2):
                    act.wait_ge(y_out[p], E // 2 * 32)

            @block.vector
            def _(dve):
                def transposed(e, p, k):
                    dve.wait_ge(xsT_ps, 2 * e + k + 1)
                    if not fresh(e):
                        dve.wait_ge(gu_ps, (e - 1) * U)
                    nc.vector.tensor_copy(xsT[:, p, starts[k]:starts[k] + HALF[k]],
                                          bank[:, 4 + k, 0:HALF[k]]).then_inc(xsT_sb, 1)

                def step(e, p):
                    for k in range(2):
                        for f in range(NF):
                            u = k * NF + f
                            dve.wait_ge(sg_sb, e * U + u + 1)
                            if not fresh(e) and f == 0:
                                dve.wait_ge(y_ps[k], e - 1)
                            nc.vector.tensor_tensor(h[:, p, f, starts[k]:starts[k] + HALF[k]],
                                                    sg[:, u % 2, 0:HALF[k]], bank[:, 2 * (u % 2) + 1, 0:HALF[k]],
                                                    ALU.mult).then_inc(h_sb, 1)
                            if u == NF and not (isinstance(e, int) and e == E - 1):
                                transposed(e + 1, 1 - p, 0)
                                transposed(e + 1, 1 - p, 1)

                transposed(0, 0, 0)
                transposed(0, 0, 1)
                turns(dve, step)


def shifted_out(g, nc, tile, ps):
    flat = lambda ap: ap.rearrange("p a s -> p (a s)")
    nc.scalar.copy(flat(g["cT"][0:64, tile, :]), ps[0:64, :])
    return nc.scalar.copy(flat(g["cT"][64:128, tile, 1:S]), ps[64:128, 0:S - 1])


def sequence_experts(nc, g, bank, ybuf, own, sb, sem):
    U = 3
    gy = sb("gy", [128, B, 2, D], ctx=own)
    xa = sb("xa", [128, 2, D], ctx=own)
    x1 = sb("x1", [128, 2, D], ctx=own)
    x1Ts = sb("x1Ts", [128, 2, S], ctx=own)
    ge = sb("ge", [128, 2, FF], ctx=own)
    h = sb("hseq", [128, 2, FF], ctx=own)
    hT = sb("hTseq", [128, 2, FF], ctx=own)
    cs = sb("cs", [128, 2, D], ctx=own)
    gsem = [sem(f"gather{i}", own) for i in range(4)]
    gathered, xa_sb, x1_sb = sem("gathered", own), sem("xa_sb", own), sem("x1_sb", own)
    x1T_ps, x1T_sb, x1_kept = sem("x1T_ps", own), sem("x1T_sb", own), sem("x1_kept", own)
    gu_ps, ge_sb, h_sb = sem("gus_ps", own), sem("ge_sb", own), sem("hs_sb2", own)
    hT_ps, hT_sb, down_done = sem("hTs_ps", own), sem("hTs_sb", own), sem("down_done", own)
    cs_sb, cT_ps = sem("cs_sb", own), sem("cTs_ps", own)
    ctok_sb, cT_sb = g["ctok_ready"], g["cT_ready"]
    LAG = 3

    def turns(eng, step):
        for n in range(6):
            step(n, n % 2)
        with eng.Fori(3, B // 2) as m:
            for p in range(2):
                step(m * 2 + p, p)
        for n in range(B, B + LAG):
            step(n, n % 2)

    def lagged(n, p, lag):
        if isinstance(n, int):
            k = n - lag
            return k, k % 2, 0 <= k < B, k >= 2
        return n - lag, (p - lag) % 2, True, True

    at = lambda k: slice(k, k + 1) if isinstance(k, int) else bass.ds(k, 1)

    with nc.Block() as block:
        @block.gpsimd
        def _(pool):
            def keep(b):
                pool.wait_ge(x1_sb, b + 1)
                nc.gpsimd.tensor_copy(g["x1"][:, b, :], x1[:, b % 2, :]).then_inc(x1_kept, 1)

            def keep_c(b):
                pool.wait_ge(cs_sb, b + 1)
                nc.gpsimd.tensor_copy(g["ctok"][:, b, :], cs[:, b % 2, :]).then_inc(ctok_sb, 1)

            for b in range(B + 5):
                if b < B:
                    for k in range(2):
                        nc.gpsimd.indirect_dma_start(
                            gy[:, b, k, :], None, ybuf,
                            bass.IndirectOffsetOnAxis(ap=g["gidx"][:, k, b:b + 1], axis=0),
                            bounds_check=NSLOT - 1, oob_is_err=False).then_inc(gsem[b % 4], 16)
                if 1 <= b <= B:
                    pool.wait_ge(gsem[(b - 1) % 4], ((b - 1) // 4 + 1) * 32)
                    pool.sem_inc(gathered, 1)
                if 2 <= b < B + 2:
                    keep(b - 2)
                if b >= 5:
                    keep_c(b - 5)

        @block.vector
        def _(dve):
            def step(n, p):
                k, q, there, later = lagged(n, p, 0)
                if there:
                    dve.wait_ge(gathered, k + 1)
                    if later:
                        dve.wait_ge(x1T_ps, k - 1)
                        dve.wait_ge(x1_kept, k - 1)
                    for j, (src, dst, done) in enumerate(((g["xtok"][:, at(k), :], xa[:, q:q + 1, :], xa_sb),
                                                          (xa[:, q:q + 1, :], x1[:, q:q + 1, :], x1_sb))):
                        if j:
                            dve.wait_ge(xa_sb, k + 1)
                        nc.vector.scalar_tensor_tensor(
                            out=dst.rearrange("p a d -> p (a d)"), in0=gy[:, at(k), j, :].rearrange("p a d -> p (a d)"),
                            scalar=g["gw"][:, j, at(k)], in1=src.rearrange("p a d -> p (a d)"),
                            op0=ALU.mult, op1=ALU.add).then_inc(done, 1)
                k, q, there, later = lagged(n, p, 1)
                if there:
                    for u in range(U):
                        r = (q * U + u) % 2
                        dve.wait_ge(ge_sb, k * U + u + 1)
                        if later or k * U + u >= 2:
                            dve.wait_ge(hT_ps, k * U + u - 1)
                        if u < 2:
                            nc.vector.scalar_tensor_tensor(
                                out=h[:, r, :], in0=ge[:, r, :],
                                scalar=g["selw"][:, at(k), u:u + 1].rearrange("p a b -> p (a b)"),
                                in1=bank[:, 2 * r + 1, :], op0=ALU.mult, op1=ALU.mult).then_inc(h_sb, 1)
                        else:
                            nc.vector.tensor_tensor(h[:, r, :], ge[:, r, :], bank[:, 2 * r + 1, :],
                                                    ALU.mult).then_inc(h_sb, 1)
                k, q, there, later = lagged(n, p, 2)
                if there:
                    dve.wait_ge(down_done, U * (k + 1))
                    if later:
                        dve.wait_ge(ctok_sb, k - 1)
                        dve.wait_ge(cT_ps, k - 1)
                    nc.vector.tensor_copy(cs[:, q, :], bank[:, 6, 0:D]).then_inc(cs_sb, 1)

            turns(dve, step)

        @block.scalar
        def _(act):
            def step(n, p):
                k, q, there, later = lagged(n, p, 0)
                if there:
                    act.wait_ge(x1T_ps, k + 1)
                    if later:
                        act.wait_ge(gu_ps, (k - 1) * U)
                    nc.scalar.copy(x1Ts[:, q, :], bank[:, 7, 0:S]).then_inc(x1T_sb, 1)
                k, q, there, later = lagged(n, p, 1)
                k2, q2, there2, later2 = lagged(n, p, 2)
                for u in range(U):
                    if there:
                        r = (q * U + u) % 2
                        act.wait_ge(gu_ps, k * U + u + 1)
                        if later or k * U + u >= 2:
                            act.wait_ge(h_sb, k * U + u - 1)
                        nc.scalar.activation(ge[:, r, :], bank[:, 2 * r, :], ACT.Gelu_apprx_tanh).then_inc(ge_sb, 1)
                    if there2:
                        r = (q2 * U + u) % 2
                        act.wait_ge(hT_ps, k2 * U + u + 1)
                        if later2 or k2 * U + u >= 2:
                            act.wait_ge(down_done, k2 * U + u - 1)
                        nc.scalar.copy(hT[:, r, :], bank[:, 4 + r, :]).then_inc(hT_sb, 1)
                k, q, there, later = lagged(n, p, 3)
                if there:
                    act.wait_ge(cT_ps, k + 1)
                    shifted_out(g, nc, at(k), bank[:, 7, S:2 * S]).then_inc(cT_sb, 1)

        
            turns(act, step)

        @block.tensor
        def _(pe):
            pe.wait_ge(g["late"], N_LATE)

            def down(k, q, u):
                r = (q * U + u) % 2
                e = E if u == 2 else chosen(k, u)
                pe.wait_ge(hT_sb, k * U + u + 1)
                for f in range(NF):
                    ins = nc.tensor.matmul(bank[:, 6, 0:D], hT[:, r, f * 128:(f + 1) * 128],
                                           g["wd"][:, at(e), f * D:(f + 1) * D],
                                           start=(u == 0 and f == 0), stop=(u == 2 and f == NF - 1))
                ins.then_inc(down_done, 1)

            def chosen(k, u):
                return pe.value_load(g["sel"][0:1, at(k), u:u + 1].rearrange("p a b -> p (a b)"), min_val=0, max_val=E - 1)

            def step(n, p):
                k, q, there, later = lagged(n, p, 0)
                k1, q1, there1, later1 = lagged(n, p, 1)
                k2, q2, there2, later2 = lagged(n, p, 2)
                k3, q3, there3, later3 = lagged(n, p, 3)
                for u in range(U):
                    if there1:
                        r = (q1 * U + u) % 2
                        if u == 0:
                            pe.wait_ge(x1T_sb, k1 + 1)
                        if later1 or k1 * U + u >= 2:
                            pe.wait_ge(h_sb, k1 * U + u - 1)
                        e = E if u == 2 else chosen(k1, u)
                        nc.tensor.matmul(bank[:, 2 * r, :], x1Ts[:, q1, :], g["wg"][:, at(e), :], start=True, stop=True)
                        nc.tensor.matmul(bank[:, 2 * r + 1, :], x1Ts[:, q1, :], g["wu"][:, at(e), :],
                                         start=True, stop=True).then_inc(gu_ps, 1)
                    if there2:
                        r = (q2 * U + u) % 2
                        pe.wait_ge(h_sb, k2 * U + u + 1)
                        if later2 or k2 * U + u >= 2:
                            pe.wait_ge(hT_sb, k2 * U + u - 1)
                        for f in range(NF):
                            ins = nc.tensor.transpose(bank[:, 4 + r, f * 128:(f + 1) * 128],
                                                      h[:, r, f * 128:(f + 1) * 128], g["eye"][:])
                        ins.then_inc(hT_ps, 1)
                        if u == 0 and (later2 or k2 >= 1):
                            pe.wait_ge(cs_sb, k2)
                        if u >= 1:
                            down(k2, q2, u - 1)
                    if u == 0 and there:
                        pe.wait_ge(x1_sb, k + 1)
                        if later or k >= 1:
                            pe.wait_ge(x1T_sb, k)
                        if not isinstance(k, int) or k >= 4:
                            pe.wait_ge(cT_sb, k - 3)
                        nc.tensor.transpose(bank[:, 7, 0:S], x1[:, q, :], g["eye"][:]).then_inc(x1T_ps, 1)
                    if u == 1 and there3:
                        pe.wait_ge(cs_sb, k3 + 1)
                        if later3 or k3 >= 1:
                            pe.wait_ge(cT_sb, k3)
                        pe.wait_ge(x1T_sb, min(k3 + 4, B) if isinstance(k3, int) else k3 + 4)
                        nc.tensor.transpose(bank[:, 7, S:2 * S], cs[:, q3, :], g["eye"][:]).then_inc(cT_ps, 1)
                if there2:
                    down(k2, q2, 2)

            turns(pe, step)


def transformer(nc, g, bank, out_dram, own, sb, sem):
    hT = sb("hT", [128, 2, S], ctx=own)
    sq = sb("sq", [128, 2 * INNER], ctx=own)
    ss = sb("ss", [128, 2, 16], ctx=own)
    rn = sb("rn", [128, 2, 16], ctx=own)
    t1 = sb("t1", [128, 2 * INNER], ctx=own)
    t2 = sb("t2", [128, 2 * INNER], ctx=own)
    kn = sb("kn", [128, INNER], ctx=own)
    qk = sb("qk", [128, 2, 2 * INNER], ctx=own)
    qkT = sb("qkT", [128, 2, 8, S], ctx=own)
    v = sb("v", [128, 2, INNER], ctx=own)
    mx = sb("mx", [128, HEADS], ctx=own)
    nb = sb("nb", [128, 2, HEADS], ctx=own)
    pa = sb("pa", [128, 2, 4, S], ctx=own)
    ls = sb("ls", [128, 2, HEADS], ctx=own)
    rl = sb("rl", [128, HEADS], ctx=own)
    pT = sb("pT", [128, 2, 4, S], ctx=own)
    on = sb("on", [128, 2, INNER], ctx=own)
    oT = sb("oT", [128, INNER], ctx=own)
    c1 = sb("c1", [128, 2, D], ctx=own)
    c1b = sb("c1b", [128, 2, D], ctx=own)
    stats = sb("stats2", [128, 6], ctx=own)
    mv = sb("mv2", [128, 2], ctx=own)
    ve = sb("ve", [128, 1], ctx=own)
    rstd = sb("rstd2", [128, 1], ctx=own)
    xh = sb("xh2", [128, D], ctx=own)
    xhT = sb("xhT", [128, S], ctx=own)
    ag = sb("ag", [128, 2, HID], ctx=own)
    gl = sb("gl", [128, HID], ctx=own)
    hh = sb("hh", [128, 2, HID], ctx=own)
    hhT = sb("hhT", [128, 3, S], ctx=own)
    c2 = sb("c2", [128, 2, D], ctx=own)
    hT_sb, qk_ps, v_ps, v_sb, sq_sb = (sem("d_" + n, own) for n in ("hT_sb", "qk_ps", "v_ps", "v_sb", "sq_sb"))
    ss0_sb, ss_sb, rn_sb = (sem("d_" + n, own) for n in ("ss0_sb", "ss_sb", "rn_sb"))
    t_sb, add_sb, kn_sb = (sem("d_" + n, own) for n in ("t_sb", "add_sb", "kn_sb"))
    qT_ps, kT_ps, qT_sb, kT_sb = (sem("d_" + n, own) for n in ("qT_ps", "kT_ps", "qT_sb", "kT_sb"))
    s_ps, mx_sb, nb_sb, p_sb = (sem("d_" + n, own) for n in ("s_ps", "mx_sb", "nb_sb", "p_sb"))
    pT_ps, pT_sb, o_ps = (sem("d_" + n, own) for n in ("pT_ps", "pT_sb", "o_ps"))
    rl_sb, on_sb, oT_ps, oT_sb = (sem("d_" + n, own) for n in ("rl_sb", "on_sb", "oT_ps", "oT_sb"))
    wo_ps, c1_sb, c1b_sb, h_ps = (sem("d_" + n, own) for n in ("wo_ps", "c1_sb", "c1b_sb", "h_ps"))
    st_sb, mv_sb, ve_sb, rstd_sb, xh_sb = (sem("d_" + n, own) for n in ("st_sb", "mv_sb", "ve_sb", "rstd_sb", "xh_sb"))
    xhT_ps, xhT_sb, w1_ps, ag_sb = (sem("d_" + n, own) for n in ("xhT_ps", "xhT_sb", "w1_ps", "ag_sb"))
    gl_sb, hh_sb, hhT_ps, hhT_sb = (sem("d_" + n, own) for n in ("gl_sb", "hh_sb", "hhT_ps", "hhT_sb"))
    w2_ps, c2_sb, cT_ps = (sem("d_" + n, own) for n in ("w2_ps", "c2_sb", "cT_ps"))
    res_sb, stored = sem("d_res_sb", own), sem("d_stored", own)
    cT_ready, ctok_ready = g["cT_ready"], g["ctok_ready"]
    LAG = 4
    FIRST = 6
    Q, K, VB, TA, TB, OB = 0, 1, 2, 5, 6, 7
    SB = (3, 4)

    def turns(eng, step):
        for n in range(FIRST):
            step(n, n % 2)
        with eng.Fori(FIRST // 2, NV // 2) as m:
            for p in range(2):
                step(m * 2 + p, p)
        for n in range(NV, NV + LAG):
            step(n, n % 2)

    def lagged(n, p, lag):
        if isinstance(n, int):
            return n - lag, (n - lag) % 2, 0 <= n - lag < NV
        return n - lag, (p - lag) % 2, True

    def wait(eng, semaphore, value, most=None):
        if isinstance(value, int):
            if most is not None:
                value = min(value, most)
            if value <= 0:
                return
        eng.wait_ge(semaphore, value)

    at = lambda k: slice(k, k + 1) if isinstance(k, int) else bass.ds(k, 1)
    layer = lambda eng, k: at(k // B) if isinstance(k, int) else \
        bass.ds(nc.s_assert_within(k >> 4, 0, DEPTH - 1, skip_runtime_bounds_check_because="k is below DEPTH * B"), 1)
    flat = lambda ap: ap.rearrange("p a d -> p (a d)")
    heads = lambda ap: ap.rearrange("p (h d) -> p h d", d=DH)

    with nc.Block() as block:
        @block.tensor
        def _(pe):
            def project(k, q):
                pe.wait_ge(hT_sb, k + 1)
                wait(pe, v_sb, k)
                wait(pe, c2_sb, k - 4)
                nc.tensor.matmul(bank[:, VB, :], hT[:, q, :], g["wqkv"][:, layer(pe, k), 2 * INNER:], start=True,
                                 stop=True).then_inc(v_ps, 1)
                wait(pe, t_sb, 3 * k)
                wait(pe, ag_sb, k - 3)
                nc.tensor.matmul(bank[:, Q, :], hT[:, q, :], g["wqkv"][:, layer(pe, k), 0:INNER], start=True, stop=True)
                nc.tensor.matmul(bank[:, K, :], hT[:, q, :], g["wqkv"][:, layer(pe, k), INNER:2 * INNER], start=True,
                                 stop=True).then_inc(qk_ps, 1)

            def scores(k, q):
                pe.wait_ge(qT_sb, k + 1)
                pe.wait_ge(kT_sb, k + 1)
                wait(pe, p_sb, 2 * k)
                for par in range(2):
                    nc.tensor.matmul(bank[:, SB[par], :], g["eye16"][:],
                                     g["mask"][:].unsqueeze(1).to_broadcast([128, 4, 128]), start=True, stop=False)
                for b in range(4):
                    for par in range(2):
                        rows = slice(64 * par, 64 * par + 64)
                        ins = nc.tensor.matmul(bank[:, SB[par], b * S:(b + 1) * S], qkT[rows, q, b, :],
                                               qkT[rows, q, 4 + b, :], start=False, stop=(b == 3))
                ins.then_inc(s_ps, 1)

            def turn(dst, src, blocks, ready):
                for b in range(blocks):
                    ins = nc.tensor.transpose(bank[:, dst, b * 128:(b + 1) * 128], src(b), g["eye"][:])
                ins.then_inc(ready, 1)

            def step(n, p):
                k, q, there = lagged(n, p, 0)
                if there:
                    project(k, q)
                k, q, there = lagged(n, p, 1)
                if there:
                    scores(k, q)
                k, q, there = lagged(n, p, 2)
                if there:
                    pe.wait_ge(on_sb, k + 1)
                    wait(pe, qT_sb, k + 2, NV)
                    turn(TA, lambda b: on[:, q, b * 128:(b + 1) * 128], 4, oT_ps)
                k, q, there = lagged(n, p, 3)
                if there:
                    pe.wait_ge(c1_sb, k + 1)
                    wait(pe, on_sb, k + 2, NV)
                    nc.tensor.matmul(bank[:, OB, 0:64], g["eye"][:], c1[:, q, 0:64], start=True, stop=True)
                    nc.tensor.matmul(bank[:, OB, 64:128], g["shift"][:], c1[:, q, 64:128], start=True,
                                     stop=True).then_inc(h_ps, 1)
                k, q, there = lagged(n, p, 4)
                if there:
                    pe.wait_ge(hh_sb, k + 1)
                    wait(pe, kT_sb, k + 4, NV)
                    for b, (c, w) in enumerate(HCH):
                        ins = nc.tensor.transpose(bank[0:w, TB, b * 128:(b + 1) * 128], hh[:, q, c:c + w], g["eye"][:])
                    ins.then_inc(hhT_ps, 1)
                k, q, there = lagged(n, p, 2)
                if there:
                    pe.wait_ge(oT_sb, k + 1)
                    for b in range(4):
                        ins = nc.tensor.matmul(bank[:, TA, 0:D], oT[:, b * 128:(b + 1) * 128],
                                               flat(g["wo"][:, layer(pe, k), b * D:(b + 1) * D]), start=(b == 0), stop=(b == 3))
                    ins.then_inc(wo_ps, 1)
                k, q, there = lagged(n, p, 4)
                if there:
                    pe.wait_ge(hhT_sb, k + 1)
                    wait(pe, v_sb, k + 5, NV)
                    wait(pe, c2_sb, k)
                    for b, (c, w) in enumerate(HCH):
                        ins = nc.tensor.matmul(bank[:, VB, 0:D], hhT[0:w, b, :],
                                               flat(g["w2"][0:w, layer(pe, k), b * D:(b + 1) * D]), start=(b == 0), stop=(b == 2))
                    ins.then_inc(w2_ps, 1)
                    pe.wait_ge(c2_sb, k + 1)
                    turn(TB, lambda b: c2[:, q, :], 1, cT_ps)
                k, q, there = lagged(n, p, 1)
                if there:
                    for par in range(2):
                        pe.wait_ge(p_sb, 2 * k + par + 1)
                        if par == 0:
                            wait(pe, c1_sb, k)
                        else:
                            wait(pe, cT_ready, B + k - 2 if not (isinstance(k, int) and k < 3) else 0)
                        turn((TA, TB)[par], lambda b: pa[:, par, b, :], 4, pT_ps)
                    wait(pe, on_sb, k)
                    wait(pe, xh_sb, k - 1)
                    for par in range(2):
                        pe.wait_ge(pT_sb, 2 * k + par + 1)
                        for b in range(4):
                            h = 2 * b + par
                            ins = nc.tensor.matmul(bank[:, OB, h * DH:(h + 1) * DH], pT[:, par, b, :],
                                                   v[:, q, h * DH:(h + 1) * DH], start=True, stop=True)
                    ins.then_inc(o_ps, 1)
                k, q, there = lagged(n, p, 3)
                if there:
                    pe.wait_ge(xh_sb, k + 1)
                    wait(pe, pT_sb, 2 * k + 5, 2 * NV)
                    turn(TA, lambda b: xh[:], 1, xhT_ps)
                    pe.wait_ge(xhT_sb, k + 1)
                    wait(pe, t_sb, 3 * k + 12, 3 * NV)
                    wait(pe, sq_sb, k + 4, NV)
                    wait(pe, ag_sb, k)
                    for j in range(2):
                        ins = nc.tensor.matmul(bank[:, (Q, K)[j], 0:HID], xhT[:],
                                               flat(g["w1"][:, layer(pe, k), j * HID:(j + 1) * HID]), start=True, stop=True)
                    ins.then_inc(w1_ps, 1)
                k, q, there = lagged(n, p, 0)
                if there:
                    pe.wait_ge(add_sb, 2 * k + 2)
                    wait(pe, xhT_sb, k - 2)
                    wait(pe, pT_sb, 2 * k - 1)
                    turn(TA, lambda b: qk[:, q, b * 128:(b + 1) * 128], 4, qT_ps)
                    pe.wait_ge(kn_sb, k + 1)
                    wait(pe, pT_sb, 2 * k)
                    turn(TB, lambda b: qk[:, q, INNER + b * 128:INNER + (b + 1) * 128], 4, kT_ps)

            turns(pe, step)

        @block.scalar
        def _(act):
            def step(n, p):
                k, q, there = lagged(n, p, 0)
                if there:
                    act.wait_ge(qk_ps, k + 1)
                    wait(act, ss0_sb, k)
                    nc.scalar.activation(sq[:], bank[:, Q:K + 1, :].rearrange("p a d -> p (a d)"),
                                         ACT.Square).then_inc(sq_sb, 1)
                    act.wait_ge(v_ps, k + 1)
                    wait(act, o_ps, k - 1)
                    nc.scalar.copy(v[:, q, :], bank[:, VB, :]).then_inc(v_sb, 1)
                k, q, there = lagged(n, p, 2)
                if there:
                    act.wait_ge(oT_ps, k + 1)
                    wait(act, wo_ps, k)
                    nc.scalar.copy(oT[:], bank[:, TA, :]).then_inc(oT_sb, 1)
                k, q, there = lagged(n, p, 4)
                if there:
                    act.wait_ge(hhT_ps, k + 1)
                    wait(act, w2_ps, k)
                    w = HCH[2][1]
                    nc.scalar.copy(hhT[:, 0:2, :], bank[:, TB, 0:2 * S].rearrange("p (a s) -> p a s", a=2))
                    nc.scalar.copy(hhT[0:w, 2, :], bank[0:w, TB, 2 * S:3 * S]).then_inc(hhT_sb, 1)
                k, q, there = lagged(n, p, 1)
                if there:
                    act.wait_ge(nb_sb, k + 1)
                    wait(act, rl_sb, k - 1)
                    for par in range(2):
                        wait(act, pT_ps, 2 * k - 1 + par)
                        for b in range(4):
                            h = 2 * b + par
                            ins = nc.scalar.activation(pa[:, par, b, :], bank[:, SB[par], b * S:(b + 1) * S], ACT.Exp,
                                                       bias=nb[:, q, h:h + 1], scale=rn[:, q, h:h + 1],
                                                       accum_out=ls[:, q, h:h + 1])
                        ins.then_inc(p_sb, 1)
                k, q, there = lagged(n, p, 4)
                if there:
                    act.wait_ge(cT_ps, k + 1)
                    shifted_out(g, nc, at(k + B), bank[:, TB, 0:S]).then_inc(cT_ready, 1)
                k, q, there = lagged(n, p, 1)
                if there:
                    for par in range(2):
                        act.wait_ge(pT_ps, 2 * k + par + 1)
                        wait(act, o_ps, k)
                        nc.scalar.copy(pT[:, par].rearrange("p a s -> p (a s)"),
                                       bank[:, (TA, TB)[par], :]).then_inc(pT_sb, 1)
                k, q, there = lagged(n, p, 3)
                if there:
                    act.wait_ge(xhT_ps, k + 1)
                    wait(act, w1_ps, k)
                    nc.scalar.activation(xhT[:], bank[:, TA, 0:S], ACT.Identity, scale=flat(g["lngb"][:, layer(act, k), 0:1]),
                                         bias=flat(g["lngb"][:, layer(act, k), 1:2])).then_inc(xhT_sb, 1)
                    act.wait_ge(ag_sb, k + 1)
                    wait(act, hh_sb, k)
                    nc.scalar.activation(gl[:], ag[:, 1, :], ACT.Gelu).then_inc(gl_sb, 1)

            turns(act, step)

        @block.vector
        def _(dve):
            def step(n, p):
                k, q, there = lagged(n, p, 0)
                if there:
                    dve.wait_ge(sq_sb, k + 1)
                    wait(dve, add_sb, 2 * k)
                    src = bank[:, Q:K + 1, :].rearrange("p w (h d) -> p w h d", d=DH)
                    both = lambda t: t[:].rearrange("p (w h d) -> p w h d", w=2, d=DH)
                    table = lambda j, lo, hi: g["rot"][:, j, layer(dve, k), :].rearrange(
                        "p a (w d) -> p (a w) d", w=2)[:, :, lo:hi].unsqueeze(2).to_broadcast([128, 2, HEADS, hi - lo])
                    nc.vector.tensor_tensor(both(t1), src, table(0, 0, DH), ALU.mult).then_inc(t_sb, 1)
                    for lo, hi, fl in ((0, 32, 32), (32, 64, 0)):
                        nc.vector.tensor_tensor(both(t2)[:, :, :, lo:hi], src[:, :, :, fl:fl + 32], table(1, lo, hi),
                                                ALU.mult).then_inc(t_sb, 1)
                    wait(dve, rn_sb, k - 1)
                    nc.vector.reduce_sum(ss[:, q, :], heads(sq[:]), X).then_inc(ss0_sb, 1)
                    dve.wait_ge(ss0_sb, k + 1)
                    nc.vector.tensor_scalar_max(ss[:, q, :], ss[:, q, :], 1e-24).then_inc(ss_sb, 1)
                k, q, there = lagged(n, p, 1)
                if there:
                    dve.wait_ge(s_ps, k + 1)
                    for par in range(2):
                        nc.vector.reduce_max(mx[:].rearrange("p (b w) -> p w b", w=2)[:, par],
                                             bank[:, SB[par], :].rearrange("p (b s) -> p b s", b=4), X).then_inc(mx_sb, 1)
                    dve.wait_ge(mx_sb, 2 * k + 2)
                    wait(dve, p_sb, 2 * k - 2)
                    nc.vector.scalar_tensor_tensor(out=nb[:, q, :], in0=mx[:], scalar=-1.0, in1=rn[:, q, 0:8],
                                                   op0=ALU.mult, op1=ALU.mult).then_inc(nb_sb, 1)
                k3, _, there3 = lagged(n, p, 3)
                if there3:
                    dve.wait_ge(h_ps, k3 + 1)
                    nc.vector.bn_stats(stats[:], bank[:, OB, 0:D]).then_inc(st_sb, 1)
                    dve.wait_ge(st_sb, k3 + 1)
                k, q, there = lagged(n, p, 2)
                if there:
                    dve.wait_ge(wo_ps, k + 1)
                    dve.wait_ge(ctok_ready, k + 1)
                    wait(dve, h_ps, k - 1)
                    wait(dve, c1b_sb, k - 1)
                    nc.vector.tensor_tensor(c1[:, q, :], bank[:, TA, 0:D], flat(g["ctok"][:, at(k), :]),
                                            ALU.add).then_inc(c1_sb, 1)
                k, q, there = lagged(n, p, 3)
                if there:
                    nc.vector.bn_aggr(mv[:], stats[:]).then_inc(mv_sb, 1)
                    dve.wait_ge(mv_sb, k + 1)
                    wait(dve, rstd_sb, k)
                    nc.vector.tensor_scalar_add(ve[:], mv[:, 1:2], 1e-5).then_inc(ve_sb, 1)
                k, q, there = lagged(n, p, 4)
                if there:
                    dve.wait_ge(w2_ps, k + 1)
                    dve.wait_ge(c1b_sb, k + 1)
                    wait(dve, cT_ps, k - 1)
                    wait(dve, ctok_ready, B + k - 1 if not (isinstance(k, int) and k < 2) else 0)
                    nc.vector.tensor_tensor(c2[:, q, :], bank[:, VB, 0:D], c1b[:, q, :],
                                            ALU.add).then_inc(c2_sb, 1)
                k, q, there = lagged(n, p, 3)
                if there:
                    dve.wait_ge(rstd_sb, k + 1)
                    wait(dve, xhT_ps, k)
                    nc.vector.tensor_scalar(xh[:], bank[:, OB, 0:D], mv[:, 0:1], rstd[:], ALU.subtract,
                                            ALU.mult).then_inc(xh_sb, 1)
                k, q, there = lagged(n, p, 1)
                if there:
                    dve.wait_ge(p_sb, 2 * k + 2)
                    nc.vector.reciprocal(rl[:], ls[:, q, :]).then_inc(rl_sb, 1)
                    dve.wait_ge(rl_sb, k + 1)
                    dve.wait_ge(o_ps, k + 1)
                    wait(dve, oT_ps, k - 1)
                    nc.vector.tensor_tensor(heads(on[:, q, :]), heads(bank[:, OB, :]),
                                            rl[:].unsqueeze(2).to_broadcast([128, HEADS, DH]), ALU.mult).then_inc(on_sb, 1)
                k, q, there = lagged(n, p, 3)
                if there:
                    dve.wait_ge(w1_ps, k + 1)
                    wait(dve, hh_sb, k)
                    nc.vector.tensor_tensor(ag[:], bank[:, Q:K + 1, 0:HID],
                                            g["b1"][:, layer(dve, k), :].rearrange("p a (w c) -> p (a w) c", w=2),
                                            ALU.add).then_inc(ag_sb, 1)
                k, q, there = lagged(n, p, 0)
                if there:
                    for dst, src, ready, done in ((0, TA, qT_ps, qT_sb), (4, TB, kT_ps, kT_sb)):
                        dve.wait_ge(ready, k + 1)
                        wait(dve, s_ps, k - 1)
                        nc.vector.tensor_copy(qkT[:, q, dst:dst + 4, :],
                                              bank[:, src, :].rearrange("p (b s) -> p b s", b=4)).then_inc(done, 1)

            turns(dve, step)

        @block.gpsimd
        def _(pool):
            def take_input(k, q):
                pool.wait_ge(cT_ready, k + 1)
                wait(pool, qk_ps, k - 1)
                nc.gpsimd.tensor_copy(hT[:, q, :], flat(g["cT"][:, at(k), :])).then_inc(hT_sb, 1)

            def step(n, p):
                k, q, there = lagged(n, p, -1)
                if there:
                    take_input(k, q)
                k, q, there = lagged(n, p, 0)
                if there:
                    pool.wait_ge(ss_sb, k + 1)
                    wait(pool, p_sb, 2 * k - 2)
                    nc.gpsimd.tensor_tensor(rn[:, q, :], ss[:, q, :], g["nhalf"][:].to_broadcast([128, 16]),
                                            ALU.pow).then_inc(rn_sb, 1)
                k, q, there = lagged(n, p, 3)
                if there:
                    pool.wait_ge(ve_sb, k + 1)
                    wait(pool, xh_sb, k)
                    nc.gpsimd.tensor_tensor(rstd[:], ve[:], g["nhalf"][:], ALU.pow).then_inc(rstd_sb, 1)
                k, q, there = lagged(n, p, 0)
                if there:
                    pool.wait_ge(t_sb, 3 * k + 3)
                    wait(pool, qT_ps, k - 1)
                    wait(pool, kT_ps, k - 1)
                    wait(pool, kn_sb, k)
                    nc.gpsimd.tensor_tensor(qk[:, q, 0:INNER], t1[:, 0:INNER], t2[:, 0:INNER], ALU.add).then_inc(add_sb, 1)
                    nc.gpsimd.tensor_tensor(kn[:], t1[:, INNER:], t2[:, INNER:], ALU.add).then_inc(add_sb, 1)
                    pool.wait_ge(rn_sb, k + 1)
                    pool.wait_ge(add_sb, 2 * k + 2)
                    nc.gpsimd.tensor_tensor(heads(qk[:, q, INNER:]), heads(kn[:]),
                                            rn[:, q, 8:16].unsqueeze(2).to_broadcast([128, HEADS, DH]),
                                            ALU.mult).then_inc(kn_sb, 1)
                k, q, there = lagged(n, p, 2)
                if there:
                    pool.wait_ge(c1_sb, k + 1)
                    wait(pool, c2_sb, k - 1)
                    nc.gpsimd.tensor_tensor(c1b[:, q, :], c1[:, q, :], flat(g["b2"][:, layer(pool, k), :]),
                                            ALU.add).then_inc(c1b_sb, 1)
                k, q, there = lagged(n, p, 4)
                if there:
                    pool.wait_ge(c2_sb, k + 1)
                    nc.gpsimd.tensor_copy(flat(g["ctok"][:, at(k + B), :]), c2[:, q, :]).then_inc(ctok_ready, 1)
                k, q, there = lagged(n, p, 3)
                if there:
                    pool.wait_ge(gl_sb, k + 1)
                    wait(pool, hhT_ps, k - 1)
                    nc.gpsimd.tensor_tensor(hh[:, q, :], ag[:, 0, :], gl[:], ALU.mult).then_inc(hh_sb, 1)

            take_input(0, 0)
            turns(pool, step)
            for c in range(4):
                lo, hi = c * B // 4, (c + 1) * B // 4
                pool.wait_ge(ctok_ready, 2 * B + hi)
                nc.gpsimd.tensor_tensor(g["x1"][:, lo:hi, :], g["x1"][:, lo:hi, :],
                                        g["ctok"][:, 2 * B + lo:2 * B + hi, :], ALU.add).then_inc(res_sb, 1)

        @block.sync
        def _(sp):
            for c in range(4):
                lo, hi = c * B // 4, (c + 1) * B // 4
                sp.wait_ge(res_sb, c + 1)
                sp.dma_start(out_dram[:, lo:hi, :], g["x1"][:, lo:hi, :]).then_inc(stored, 16)
            sp.wait_ge(stored, 64)


def lay_out(i):
    c = np.ascontiguousarray
    f = {k: np.asarray(v) for k, v in i.items()}
    x = f["x"]
    gates = lambda skill, shared: c(np.concatenate([skill, shared[None]]).transpose(1, 0, 2))
    w_down = np.concatenate([f["L1_cond_skill_down"], f["L1_cond_shared_down"][None]])
    pad = np.zeros((DEPTH, 3 * 128 - HID, D), np.float32)
    w2 = np.concatenate([f["L1_ffn_w2"], pad], 1)
    chunks = lambda w, n: c(w.reshape(w.shape[0], n, 128, D).transpose(2, 0, 1, 3).reshape(128, w.shape[0], n * D))
    return {
        "xT": c(x.reshape(T, D).T), "xtok": c(x.transpose(1, 0, 2)),
        "AsT": c(f["L0_cond_As"].reshape(E * RANK, D).T),
        "BsT": c(f["L0_cond_Bs"].transpose(0, 2, 1).reshape(E * RANK, D)),
        "WbT": c(f["L0_cond_W_base"].T), "WrT": c(f["L0_ffn_Wr"].T),
        "wcol": c(np.repeat(f["cond_8"].T, RANK, axis=0)), "cond": c(f["cond_8"].reshape(1, -1)),
        "rows": c(np.concatenate([f["L0_cond_b_base"], f["L0_ffn_ln_gamma"], f["L0_ffn_ln_beta"]])[None]),
        "qs": c(np.concatenate([f["L1_ffn_q_scale"], f["L1_ffn_k_scale"]], 1).reshape(1, -1)),
        "w12": c(f["L0_ffn_W12"].transpose(2, 0, 1)),
        "w3": c(f["L0_ffn_W3"].transpose(2, 0, 1).reshape(NF, 128, E, D).transpose(1, 2, 0, 3).reshape(128, E, NF * D)),
        "wg": gates(f["L1_cond_skill_gate"], f["L1_cond_shared_gate"]),
        "wu": gates(f["L1_cond_skill_up"], f["L1_cond_shared_up"]),
        "wd": chunks(w_down, NF), "wqkv": c(f["L1_ffn_wqkv"].transpose(1, 0, 2)), "wo": chunks(f["L1_ffn_wo"], NF),
        "w1": c(f["L1_ffn_w1"].transpose(1, 0, 2)), "w2": chunks(w2, 3),
        "b1": c(f["L1_ffn_b1"].reshape(1, -1)), "b2": c(f["L1_ffn_b2"].reshape(1, -1)),
        "lngb": c(np.stack([f["L1_ffn_ln_g"], f["L1_ffn_ln_b"]], -1).transpose(1, 0, 2)),
    }


def kernel(**inputs):
    import concourse.bacc as _bacc
    from concourse.bass_utils import run_bass_kernel_spmd as _run

    nc = _bacc.Bacc("TRN2", target_bir_lowering=False, num_devices=1)
    arrays, args = {}, {}
    for name, a in {**lay_out(inputs), **{k: np.ascontiguousarray(v) for k, v in constants().items()}}.items():
        arrays[f"in_{name}"] = a
        args[name] = nc.dram_tensor(f"in_{name}", a.shape, mybir.dt.from_np(a.dtype), kind="ExternalInput").ap()
    out = nc.dram_tensor("out", (B, S, D), F32, kind="ExternalOutput").ap()
    build(nc, args, out.rearrange("b s d -> s b d"))
    r = _run(nc, [arrays], core_ids=[0])
    return r.results[0]["out"]
```

```python
import numpy as np

import concourse.bass as bass
from concourse import mybir
from concourse.alu_op_type import AluOpType as ALU

F32 = mybir.dt.float32
BF16 = mybir.dt.bfloat16
I32 = mybir.dt.int32
U32 = mybir.dt.uint32
ACT = mybir.ActivationFunctionType
X = mybir.AxisListType.X

B, S, D = 16, 128, 128
T = B * S
E = 8
RANK = 16
LORA_SCALE = 32.0 / RANK
FF = 512
NF = FF // 128
CAP = -(-(-(-T * 2 * 5 // 4)) // E)
NSLOT = E * CAP
NCH = CAP // 128
HALF = (3 * 128, 2 * 128)
HEADS, DH = 8, 64
INNER = HEADS * DH
HID = int(D * 4 * 2 / 3)
HCH = [(0, 128), (128, 128), (256, HID - 256)]
DEPTH = 2
WINDOW = 64
NV = DEPTH * B
G = 4
NG = B // G
DROP = float(1 << 20)
MASKED = -1e30


def constants():
    f = np.float32
    eye = np.eye(128, dtype=f)
    shift = np.eye(128, k=1, dtype=f)
    i, j = np.arange(128)[:, None], np.arange(128)[None, :]
    mask = np.where((i < j) | (i > j + WINDOW), MASKED, 0.0).astype(f)
    before = (i < j).astype(f)
    half = np.arange(0, DH, 2, dtype=f)
    inv = (f(1.0) / f(10000.0) ** (half / f(DH))).astype(f)
    t = np.arange(S, dtype=f)
    freqs = t[:, None] * inv[None, :]
    freqs = np.concatenate([freqs, freqs], -1).astype(f)
    base = (half + f(0.4 * DH)) / f(1.4 * DH)
    power = (t - S // 2) / f(WINDOW // 2)
    sc = (base[None, :].astype(f) ** power[:, None].astype(f)).astype(f)
    sc = np.concatenate([sc, sc], -1)
    cos, sin = np.cos(freqs).astype(f), np.sin(freqs).astype(f)
    sign = np.where(np.arange(DH) < DH // 2, -1.0, 1.0).astype(f)
    qk = np.stack([sc * f(8.0), f(1.0) / sc], 1)
    rot = np.stack([cos[:, None] * qk, (sin * sign)[:, None] * qk], 1).astype(f)
    e = np.arange(E, dtype=f)
    table = np.zeros((3, B, E), f)
    table[0] = E - e
    table[1] = e
    table[2] = e * CAP
    return {"eye": eye, "shift": shift, "masks": np.stack([mask, before], 1), "rotary": np.ascontiguousarray(rot),
            "table": table.reshape(1, -1)}


def build(nc, a, out_dram):
    from contextlib import ExitStack
    stack = ExitStack()
    with stack:
        def sb(name, shape, dt=F32, ctx=stack):
            return ctx.enter_context(nc.sbuf_tensor(name, shape, dt))

        def sem(name, ctx=stack):
            return ctx.enter_context(nc.semaphore(name))

        xbuf = nc.dram_tensor("xbuf", (NSLOT, D), F32, kind="Internal").ap()
        ybuf = nc.dram_tensor("ybuf", (NSLOT, D), F32, kind="Internal").ap()
        g = {}
        bank = stack.enter_context(nc.psum_tensor("bank", [128, 8, 512], F32))
        g["eye"] = sb("eye", [128, 128])
        g["shift"] = sb("shift", [128, 128])
        g["mask"] = sb("mask", [128, 128], BF16)
        g["eye16"] = sb("eye16", [128, 128], BF16)
        g["nhalf"] = sb("nhalf", [128, 1])
        g["wqkv"] = sb("wqkv", [128, DEPTH, 3 * INNER])
        g["wo"] = sb("wo", [128, DEPTH, NF * D])
        g["w1"] = sb("w1", [128, DEPTH, 2 * HID])
        g["b1"] = sb("b1", [128, DEPTH, 2 * HID])
        g["w2"] = sb("w2", [128, DEPTH, 3 * D])
        g["b2"] = sb("b2", [128, DEPTH, D])
        g["lngb"] = sb("lngb", [128, DEPTH, 2])
        g["rot"] = sb("rot", [128, 2, DEPTH, 2 * DH])
        g["x1"] = sb("x1_all", [128, B, D])
        g["ctok"] = sb("ctok", [128, 3 * B, D])
        g["xtok"] = g["ctok"][:, 2 * B:, :]
        g["cT"] = sb("cT", [128, 3 * B, S])
        g["sel"] = sb("sel", [128, B, 2], I32)
        g["selw"] = sb("selw", [128, B, 2])
        g["cT_ready"] = sem("cT_ready")
        g["ctok_ready"] = sem("ctok_ready")
        g["late"] = sem("late_weights")
        g["gidx"] = sb("gidx", [128, 2, B], U32)
        g["gw"] = sb("gw", [128, 2, B])
        with ExitStack() as moe:
            g["wg"] = sb("wg", [128, E + 1, FF], ctx=moe)
            g["wu"] = sb("wu", [128, E + 1, FF], ctx=moe)
            g["wd"] = sb("wd", [128, E + 1, NF * D], ctx=moe)
            route(nc, a, g, bank, xbuf, stack, sb, sem)
            experts(nc, a, g, bank, xbuf, ybuf, sb, sem)
            with ExitStack() as own:
                sequence_experts(nc, g, bank, ybuf, own, sb, sem)
        with ExitStack() as own:
            transformer(nc, g, bank, out_dram, own, sb, sem)


LATE = [("wg", "wg"), ("wu", "wu"), ("wd", "wd"), ("wqkv", "wqkv"), ("wo", "wo"), ("w1", "w1"),
        ("w2", "w2"), ("lngb", "lngb"), ("shift", "shift")]
LATE_ROWS = [("b1", DEPTH * 2 * HID), ("b2", DEPTH * D)]
N_LATE = 16 * (len(LATE) + len(LATE_ROWS))


def route(nc, a, g, bank, xbuf, stack, sb, sem):
    from contextlib import ExitStack
    with ExitStack() as own:
        xT = sb("xT", [128, T], ctx=own)
        AsT = sb("AsT", [128, 128], ctx=own)
        BsT = sb("BsT", [128, 128], ctx=own)
        WbT = sb("WbT", [128, 128], ctx=own)
        WrT = sb("WrT", [128, E], ctx=own)
        wcol = sb("wcol", [128, B], ctx=own)
        rows = sb("rows", [128, 3, D], ctx=own)
        cond = sb("cond", [128, B, E], ctx=own)
        table = sb("table_sb", [128, 3, B, E], ctx=own)
        qs = sb("qs", [128, DEPTH, 2 * DH], ctx=own)
        rotc = sb("rotc", [128, 2, 2 * DH], ctx=own)
        masks = sb("masks", [128, 2, 128], ctx=own)
        before = sb("before", [128, 128], BF16, ctx=own)
        ones = sb("ones", [128, 128], BF16, ctx=own)
        hs = sb("hs", [128, 2, G * S], ctx=own)
        c0 = sb("c0", [128, 2, G, D], ctx=own)
        stats = sb("stats", [128, 2, G, 6], ctx=own)
        mv = sb("mv", [128, 2, G, 2], ctx=own)
        rstd = sb("rstd", [128, 2, G], ctx=own)
        xh = sb("xh", [128, 2, G, D], ctx=own)
        xg = sb("xg", [128, G, D], ctx=own)
        xn = sb("xn", [128, B, D], ctx=own)
        xnT = sb("xnT", [128, 2, G * S], ctx=own)
        zero = sb("zero", [128, NSLOT * D // 512], ctx=own)
        lg = sb("lg", [128, B, E], ctx=own)
        ex = sb("ex", [128, B, E], ctx=own)
        pr = sb("pr", [128, B, E], ctx=own)
        pr2 = sb("pr2", [128, B, E], ctx=own)
        oh = sb("oh", [128, 2, B, E], ctx=own)
        tmp = sb("tmp", [128, B, E], ctx=own)
        tmp2 = sb("tmp2", [128, B, E], ctx=own)
        tmp3 = sb("tmp3", [128, B, E], ctx=own)
        both = sb("both", [128, B, E], BF16, ctx=own)
        col = sb("col", [128, 8, B], ctx=own)
        sidx = sb("sidx", [128, 2, B], U32, ctx=own)

        first = sem("first_loads", own)
        xin = [sem(f"x_loads{i}", own) for i in range(NG)]
        early = sem("early_loads", own)
        zeroed = sem("zero_tile", own)
        cleared = sem("xbuf_cleared", own)
        h_ps, hs_sb = sem("h_ps", own), sem("hs_sb", own)
        c0_ps, c0_sb = sem("c0_ps", own), sem("c0_sb", own)
        st_done, mv_done, rstd_done = sem("st_done", own), sem("mv_done", own), sem("rstd_done", own)
        xh_done, xg_done, xn_done = sem("xh_done", own), sem("xg_done", own), sem("xn_done", own)
        xnT_ps, xnT_sb, lg_ps = sem("xnT_ps", own), sem("xnT_sb", own), sem("lg_ps", own)
        chain = sem("router_steps", own)
        lg_ready, ex_ready = sem("lg_ready", own), sem("ex_ready", own)
        both_ready, rank_ps = sem("both_ready", own), sem("rank_ps", own)
        sidx_ready, scattered = sem("sidx_ready", own), sem("scattered", own)
        small = sem("small_constants", own)
        nh_done, rot_done = sem("nh_done", own), sem("rot_done", own)

        with nc.Block() as block:
            @block.sync
            def _(sp):
                sp.dma_start(AsT[:], a["AsT"]).then_inc(first, 16)
                sp.dma_start(xT[:, 0:G * S], a["xT"][:, 0:G * S]).then_inc(xin[0], 16)
                sp.dma_start(wcol[:], a["wcol"]).then_inc(first, 16)
                sp.dma_start(WbT[:], a["WbT"]).then_inc(first, 16)
                sp.dma_start(BsT[:], a["BsT"]).then_inc(first, 16)
                sp.dma_start(rows[:].rearrange("p a d -> p (a d)"),
                             a["rows"][0, :].partition_broadcast(128)).then_inc(first, 16)
                for i in range(1, NG):
                    sp.dma_start(xT[:, i * G * S:(i + 1) * G * S],
                                 a["xT"][:, i * G * S:(i + 1) * G * S]).then_inc(xin[i], 16)
                sp.dma_start(g["eye"][:], a["eye"]).then_inc(early, 16)
                sp.dma_start(WrT[:], a["WrT"]).then_inc(early, 16)
                sp.dma_start(cond[:].rearrange("p b e -> p (b e)"),
                             a["cond"][0, :].partition_broadcast(128)).then_inc(early, 16)
                sp.dma_start(table[:].rearrange("p k b e -> p (k b e)"),
                             a["table"][0, :].partition_broadcast(128)).then_inc(early, 16)
                sp.dma_start(masks[:], a["masks"]).then_inc(early, 16)
                sp.dma_start(qs[:].rearrange("p l d -> p (l d)"),
                             a["qs"][0, :].partition_broadcast(128)).then_inc(early, 16)
                sp.dma_start(rotc[:], a["rotary"]).then_inc(early, 16)
                sp.dma_start(g["xtok"], a["xtok"]).then_inc(early, 16)
                sp.wait_ge(zeroed, 1)
                for i in range(4):
                    sp.dma_start(xbuf.rearrange("(q p r) d -> q p (r d)", q=4, p=128)[i],
                                 zero[:]).then_inc(cleared, 16)
                for sbuf, dram in LATE:
                    sp.dma_start(g[sbuf][:], a[dram]).then_inc(g["late"], 16)
                for name, n in LATE_ROWS:
                    sp.dma_start(g[name][:].rearrange("p l d -> p (l d)"),
                                 a[name][0, :].partition_broadcast(128)).then_inc(g["late"], 16)

            @block.tensor
            def _(pe):
                pe.wait_ge(first, 80)
                for i in range(NG):
                    tok = slice(i * G * S, (i + 1) * G * S)
                    pe.wait_ge(xin[i], 16)
                    if i >= 2:
                        pe.wait_ge(hs_sb, i - 1)
                    nc.tensor.matmul(bank[:, i % 2, :], AsT[:], xT[:, tok], start=True, stop=True).then_inc(h_ps, 1)
                    pe.wait_ge(hs_sb, i + 1)
                    if i >= 2:
                        pe.wait_ge(c0_sb, i - 1)
                    for t in range(G):
                        o = bank[:, 2 + i % 2, t * D:(t + 1) * D]
                        nc.tensor.matmul(o, xT[:, i * G * S + t * S:i * G * S + (t + 1) * S], WbT[:],
                                         start=True, stop=False)
                        last = nc.tensor.matmul(o, hs[:, i % 2, t * S:(t + 1) * S], BsT[:], start=False, stop=True)
                    last.then_inc(c0_ps, 1)
                pe.wait_ge(early, 128)
                for i in range(NG):
                    pe.wait_ge(xn_done, i + 1)
                    if i >= 2:
                        pe.wait_ge(xnT_sb, i - 1)
                    for t in range(G):
                        last = nc.tensor.transpose(bank[:, 4 + i % 2, t * S:(t + 1) * S], xn[:, i * G + t, :],
                                                   g["eye"][:])
                    last.then_inc(xnT_ps, 1)
                    pe.wait_ge(xnT_sb, i + 1)
                    for t in range(G):
                        n = i * G + t
                        last = nc.tensor.matmul(bank[:, 6, n * E:(n + 1) * E], xnT[:, i % 2, t * S:(t + 1) * S],
                                                WrT[:], start=True, stop=True)
                    last.then_inc(lg_ps, 1)
                pe.wait_ge(both_ready, 1)
                pe.wait_ge(small, 2)
                nc.tensor.matmul(bank[:, 7, 0:B * E], before[:], both[:].rearrange("p b e -> p (b e)"),
                                 start=True, stop=False)
                for t in range(B - 1):
                    last = nc.tensor.matmul(bank[:, 7, (t + 1) * E:B * E], ones[:],
                                            both[:, t:t + 1, :].to_broadcast([128, B - 1 - t, E]),
                                            start=False, stop=(t == B - 2))
                last.then_inc(rank_ps, 1)

            @block.scalar
            def _(act):
                act.wait_ge(early, 128)
                nc.scalar.copy(g["eye16"][:], g["eye"][:])
                nc.scalar.copy(g["mask"][:], masks[:, 0, :])
                nc.scalar.copy(before[:], masks[:, 1, :]).then_inc(small, 1)
                for i in range(NG):
                    act.wait_ge(xnT_ps, i + 1)
                    if i >= 2:
                        act.wait_ge(lg_ps, i - 1)
                    nc.scalar.copy(xnT[:, i % 2, :], bank[:, 4 + i % 2, :]).then_inc(xnT_sb, 1)
                for i in range(2):
                    act.wait_ge(lg_ready, i + 1)
                    nc.scalar.activation(ex[:], lg[:], ACT.Exp).then_inc(ex_ready, 1)

            @block.gpsimd
            def _(pool):
                nc.gpsimd.memset(zero[:], 0.0).then_inc(zeroed, 1)
                nc.gpsimd.memset(ones[:], 1.0).then_inc(small, 1)
                nc.gpsimd.memset(g["nhalf"][:], -0.5).then_inc(nh_done, 1)
                nc.gpsimd.memset(g["cT"][:, :, 0:1], 0.0).then_inc(nh_done, 1)
                pool.wait_ge(nh_done, 2)
                pool.wait_ge(first, 80)
                for i in range(NG):
                    pool.wait_ge(mv_done, i + 1)
                    nc.gpsimd.tensor_tensor(rstd[:, i % 2, :], mv[:, i % 2, :, 1],
                                            g["nhalf"][:].to_broadcast([128, G]), ALU.pow).then_inc(rstd_done, 1)
                    pool.wait_ge(xh_done, i + 1)
                    if i >= 1:
                        pool.wait_ge(xn_done, i)
                    nc.gpsimd.tensor_tensor(xg[:], xh[:, i % 2], rows[:, 1:2, :].to_broadcast([128, G, D]),
                                            ALU.mult).then_inc(xg_done, 1)
                    pool.wait_ge(xg_done, i + 1)
                    nc.gpsimd.tensor_tensor(xn[:, i * G:(i + 1) * G, :], xg[:],
                                            rows[:, 2:3, :].to_broadcast([128, G, D]), ALU.add).then_inc(xn_done, 1)
                pool.wait_ge(early, 128)
                for l in range(DEPTH):
                    nc.gpsimd.tensor_tensor(g["rot"][:, 0, l, :], rotc[:, 0, :], qs[:, l, :], ALU.mult).then_inc(rot_done, 1)
                    for h in range(2):
                        pick = lambda t, k: t.rearrange("p (w h d) -> p w h d", w=2, h=2)[:, :, k, :]
                        nc.gpsimd.tensor_tensor(pick(g["rot"][:, 1, l, :], h), pick(rotc[:, 1, :], h),
                                                pick(qs[:, l, :], 1 - h), ALU.mult).then_inc(rot_done, 1)
                pool.wait_ge(sidx_ready, 2)
                pool.wait_ge(cleared, 64)
                for t in range(B):
                    for k in range(2):
                        nc.gpsimd.indirect_dma_start(
                            xbuf, bass.IndirectOffsetOnAxis(ap=sidx[:, k, t:t + 1], axis=0), xn[:, t, :], None,
                            bounds_check=NSLOT - 1, oob_is_err=False).then_inc(scattered, 16)
                pool.wait_ge(scattered, 2 * B * 16)

            @block.vector
            def _(dve):
                steps = [0]

                def then(ins):
                    steps[0] += 1
                    ins.then_inc(chain, 1)
                    dve.wait_ge(chain, steps[0])

                def per_tile(c):
                    return c.unsqueeze(2).to_broadcast([128, B, E])

                def softmax_top2(exps, eps, w_out):
                    then(nc.vector.reduce_sum(col[:, 1, :], exps[:], X))
                    if eps:
                        then(nc.vector.tensor_scalar_add(col[:, 1, :], col[:, 1, :], eps))
                    then(nc.vector.reciprocal(col[:, 2, :], col[:, 1, :]))
                    then(nc.vector.tensor_tensor(pr[:], exps[:], per_tile(col[:, 2, :]), ALU.mult))
                    for k, p in enumerate((pr, pr2)):
                        then(nc.vector.reduce_max(w_out[:, k, :], p[:], X))
                        then(nc.vector.tensor_tensor(tmp[:], p[:], per_tile(w_out[:, k, :]), ALU.is_equal))
                        then(nc.vector.tensor_tensor(tmp2[:], tmp[:], table[:, 0], ALU.mult))
                        then(nc.vector.reduce_max(col[:, 3, :], tmp2[:], X))
                        then(nc.vector.tensor_tensor(oh[:, k], tmp2[:], per_tile(col[:, 3, :]), ALU.is_equal))
                        if k == 0:
                            then(nc.vector.scalar_tensor_tensor(
                                out=pr2[:].rearrange("p b e -> p (b e)"), in0=oh[:, 0].rearrange("p b e -> p (b e)"),
                                scalar=-4.0, in1=pr[:].rearrange("p b e -> p (b e)"), op0=ALU.mult, op1=ALU.add))

                dve.wait_ge(first, 80)
                dve.wait_ge(early, 128)
                then(nc.vector.reduce_max(col[:, 0, :], cond[:], X))
                nc.vector.tensor_tensor(lg[:], cond[:], per_tile(col[:, 0, :]), ALU.subtract).then_inc(lg_ready, 1)
                for i in range(NG):
                    dve.wait_ge(h_ps, i + 1)
                    if i >= 2:
                        dve.wait_ge(c0_ps, i - 1)
                    nc.vector.scalar_tensor_tensor(
                        out=hs[:, i % 2, :].rearrange("p (t s) -> p t s", t=G),
                        in0=bank[:, i % 2, :].rearrange("p (t s) -> p t s", t=G), scalar=LORA_SCALE,
                        in1=wcol[:, i * G:(i + 1) * G].unsqueeze(2).to_broadcast([128, G, S]),
                        op0=ALU.mult, op1=ALU.mult).then_inc(hs_sb, 1)
                    dve.wait_ge(c0_ps, i + 1)
                    if i >= 2:
                        dve.wait_ge(xh_done, i - 1)
                    nc.vector.tensor_tensor(c0[:, i % 2], bank[:, 2 + i % 2, :].rearrange("p (t d) -> p t d", t=G),
                                            rows[:, 0:1, :].to_broadcast([128, G, D]), ALU.add).then_inc(c0_sb, 1)
                    dve.wait_ge(c0_sb, i + 1)
                    for t in range(G):
                        nc.vector.bn_stats(stats[:, i % 2, t, :], c0[:, i % 2, t, :]).then_inc(st_done, 1)
                    dve.wait_ge(st_done, (i + 1) * G)
                    if i >= 2:
                        dve.wait_ge(rstd_done, i - 1)
                    for t in range(G):
                        last = nc.vector.bn_aggr(mv[:, i % 2, t, :], stats[:, i % 2, t, :])
                    then(last)
                    nc.vector.tensor_scalar_add(mv[:, i % 2, :, 1], mv[:, i % 2, :, 1], 1e-5).then_inc(mv_done, 1)
                    dve.wait_ge(rstd_done, i + 1)
                    if i >= 2:
                        dve.wait_ge(xg_done, i - 1)
                    for t in range(G):
                        last = nc.vector.tensor_scalar(xh[:, i % 2, t, :], c0[:, i % 2, t, :], mv[:, i % 2, t, 0:1],
                                                       rstd[:, i % 2, t:t + 1], ALU.subtract, ALU.mult)
                    last.then_inc(xh_done, 1)
                dve.wait_ge(ex_ready, 1)
                softmax_top2(ex, 0.0, col[:, 4:6])
                then(nc.vector.tensor_tensor(col[:, 6, :], col[:, 4, :], col[:, 5, :], ALU.add))
                then(nc.vector.reciprocal(col[:, 7, :], col[:, 6, :]))
                for k in range(2):
                    then(nc.vector.tensor_tensor(col[:, 4 + k, :], col[:, 4 + k, :], col[:, 7, :], ALU.mult))
                    then(nc.vector.tensor_scalar_mul(col[:, 6, :], col[:, 4 + k, :], 1.0 - 1.0 / 12))
                    then(nc.vector.scalar_tensor_tensor(out=g["selw"][:, :, k], in0=col[:, 4 + k, :], scalar=1.0 / 12,
                                                        in1=col[:, 6, :], op0=ALU.mult, op1=ALU.add))
                    then(nc.vector.tensor_tensor(tmp[:], oh[:, k], table[:, 1], ALU.mult))
                    then(nc.vector.reduce_sum(col[:, 3, :], tmp[:], X))
                    then(nc.vector.tensor_copy(g["sel"][:, :, k], col[:, 3, :]))

                dve.wait_ge(lg_ps, NG)
                logits = bank[:, 6, 0:B * E].rearrange("p (b e) -> p b e", b=B)
                then(nc.vector.tensor_scalar(tmp3[:], logits, 10000.0, -10000.0, ALU.min, ALU.max))
                then(nc.vector.reduce_max(col[:, 0, :], tmp3[:], X))
                nc.vector.tensor_tensor(lg[:], tmp3[:], per_tile(col[:, 0, :]), ALU.subtract).then_inc(lg_ready, 1)
                dve.wait_ge(ex_ready, 2)
                softmax_top2(ex, 1e-12, col[:, 4:6])
                nc.vector.tensor_tensor(both[:], oh[:, 0], oh[:, 1], ALU.add).then_inc(both_ready, 1)
                dve.wait_ge(rank_ps, 1)
                rank = bank[:, 7, 0:B * E].rearrange("p (b e) -> p b e", b=B)
                then(nc.vector.tensor_scalar(tmp[:], rank, float(CAP), None, ALU.is_lt))
                then(nc.vector.tensor_tensor(tmp2[:], rank, table[:, 2], ALU.add))
                then(nc.vector.scalar_tensor_tensor(
                    out=tmp3[:].rearrange("p b e -> p (b e)"), in0=tmp[:].rearrange("p b e -> p (b e)"), scalar=-DROP,
                    in1=tmp2[:].rearrange("p b e -> p (b e)"), op0=ALU.mult, op1=ALU.add))
                for k in range(2):
                    then(nc.vector.tensor_tensor(pr[:], oh[:, k], tmp3[:], ALU.mult))
                    then(nc.vector.reduce_sum(col[:, 0, :], pr[:], X))
                    then(nc.vector.tensor_scalar_add(col[:, 0, :], col[:, 0, :], DROP))
                    nc.vector.tensor_copy(sidx[:, k, :], col[:, 0, :]).then_inc(sidx_ready, 1)
                then(nc.vector.tensor_scalar_add(pr2[:], table[:, 2], CAP - 1.0))
                then(nc.vector.tensor_tensor(tmp2[:], tmp2[:], pr2[:], ALU.min))
                for k in range(2):
                    then(nc.vector.tensor_tensor(pr[:], oh[:, k], tmp2[:], ALU.mult))
                    then(nc.vector.reduce_sum(col[:, 1, :], pr[:], X))
                    nc.vector.tensor_copy(g["gidx"][:, k, :], col[:, 1, :])
                    then(nc.vector.tensor_tensor(pr[:], oh[:, k], tmp[:], ALU.mult))
                    then(nc.vector.reduce_sum(col[:, 2, :], pr[:], X))
                    then(nc.vector.tensor_tensor(g["gw"][:, k, :], col[:, 4 + k, :], col[:, 2, :], ALU.mult))


def experts(nc, a, g, bank, xbuf, ybuf, sb, sem):
    from contextlib import ExitStack
    starts = (0, HALF[0])
    nchunk = tuple(h // 128 for h in HALF)
    with ExitStack() as own:
        w12 = sb("w12", [128, 2, 2 * FF], ctx=own)
        w3 = sb("w3", [128, 2, NF * D], ctx=own)
        xs = sb("xs", [128, 2, NCH, D], ctx=own)
        xsT = sb("xsT", [128, 2, CAP], ctx=own)
        sg = sb("sg", [128, 2, HALF[0]], ctx=own)
        h = sb("h", [128, 2, NF, CAP], ctx=own)
        ys = sb("ys", [128, 2, NCH, D], ctx=own)
        w_in = [sem(f"w_in{i}", own) for i in range(2)]
        x_in = [sem(f"x_in{i}", own) for i in range(2)]
        xsT_ps, xsT_sb = sem("xsT_ps", own), sem("xsT_sb", own)
        gu_ps, sg_sb, h_sb = sem("gu_ps", own), sem("sg_sb", own), sem("h_sb", own)
        y_ps = [sem(f"y_ps{i}", own) for i in range(2)]
        y_sb = [sem(f"y_sb{i}", own) for i in range(2)]
        y_out = [sem(f"y_out{i}", own) for i in range(2)]
        U = 2 * NF

        def turns(eng, step):
            for e in range(2):
                step(e, e)
            with eng.Fori(1, E // 2 - 1) as m:
                for p in range(2):
                    step(m * 2 + p, p)
            for e in range(E - 2, E):
                step(e, e % 2)

        first = lambda e: isinstance(e, int) and e < 1
        fresh = lambda e: isinstance(e, int) and e < 2

        with nc.Block() as block:
            @block.sync
            def _(sp):
                def load(e, p):
                    if not fresh(e):
                        sp.wait_ge(y_ps[1], e - 1)
                    at = bass.ds(e, 1) if not isinstance(e, int) else slice(e, e + 1)
                    rows = bass.ds(e * CAP, CAP) if not isinstance(e, int) else slice(e * CAP, (e + 1) * CAP)
                    sp.dma_start(xs[:, p, :, :], xbuf[rows, :].rearrange("(c p) d -> p c d", p=128)).then_inc(x_in[p], 16)
                    sp.dma_start(w12[:, p:p + 1, :], a["w12"][:, at, :]).then_inc(w_in[p], 16)
                    sp.dma_start(w3[:, p:p + 1, :], a["w3"][:, at, :]).then_inc(w_in[p], 16)
                turns(sp, load)

            @block.tensor
            def _(pe):
                def transpose_x(e, p):
                    pe.wait_ge(x_in[p], ((e - p) // 2 + 1) * 16 if isinstance(e, int) else ((e - p) >> 1) * 16 + 16)
                    if not first(e):
                        pe.wait_ge(xsT_sb, 2 * e)
                    for c in range(NCH):
                        k = 0 if c < nchunk[0] else 1
                        o = c * 128 - starts[k]
                        ins = nc.tensor.transpose(bank[:, 4 + k, o:o + 128], xs[:, p, c, :], g["eye"][:])
                        if c in (nchunk[0] - 1, NCH - 1):
                            ins.then_inc(xsT_ps, 1)

                def gate_up(e, p, k):
                    pe.wait_ge(xsT_sb, 2 * e + k + 1)
                    for f in range(NF):
                        u = k * NF + f
                        if not (first(e) and u < 2):
                            pe.wait_ge(h_sb, e * U + u - 1)
                        for j in range(2):
                            ins = nc.tensor.matmul(bank[:, 2 * (u % 2) + j, 0:HALF[k]],
                                                   w12[:, p, j * FF + f * 128:j * FF + (f + 1) * 128],
                                                   xsT[:, p, starts[k]:starts[k] + HALF[k]], start=True, stop=True)
                        ins.then_inc(gu_ps, 1)

                def down(e, p, k):
                    pe.wait_ge(h_sb, e * U + (k + 1) * NF)
                    if not first(e):
                        pe.wait_ge(y_sb[k], e)
                    for c in range(nchunk[k]):
                        at = starts[k] + c * 128
                        for f in range(NF):
                            ins = nc.tensor.matmul(bank[:, 6 + k, c * D:(c + 1) * D], h[:, p, f, at:at + 128],
                                                   w3[:, p, f * D:(f + 1) * D], start=(f == 0), stop=(f == NF - 1))
                    ins.then_inc(y_ps[k], 1)

                def step(e, p):
                    pe.wait_ge(w_in[p], ((e - p) // 2 + 1) * 32 if isinstance(e, int) else ((e - p) >> 1) * 32 + 32)
                    gate_up(e, p, 0)
                    if not first(e):
                        down(e - 1, 1 - p, 1)
                    if not (isinstance(e, int) and e == E - 1):
                        transpose_x(e + 1, 1 - p)
                    gate_up(e, p, 1)
                    down(e, p, 0)

                transpose_x(0, 0)
                turns(pe, step)
                down(E - 1, (E - 1) % 2, 1)

            @block.scalar
            def _(act):
                def step(e, p):
                    for k in range(2):
                        for f in range(NF):
                            u = k * NF + f
                            act.wait_ge(gu_ps, e * U + u + 1)
                            if not (first(e) and u < 2):
                                act.wait_ge(h_sb, e * U + u - 1)
                            nc.scalar.activation(sg[:, u % 2, 0:HALF[k]], bank[:, 2 * (u % 2), 0:HALF[k]],
                                                 ACT.Silu).then_inc(sg_sb, 1)
                            if u == 1 and not first(e):
                                store(e - 1, 1 - p, 0)
                            if u == NF and not first(e):
                                store(e - 1, 1 - p, 1)

                def store(e, p, k):
                    act.wait_ge(y_ps[k], e + 1)
                    if not fresh(e):
                        act.wait_ge(y_out[p], ((e - p) // 2) * 32 if isinstance(e, int) else ((e - p) >> 1) * 32)
                    c0 = starts[k] // 128
                    nc.scalar.copy(ys[:, p, c0:c0 + nchunk[k], :],
                                   bank[:, 6 + k, 0:nchunk[k] * D].rearrange("p (c d) -> p c d", d=D)).then_inc(y_sb[k], 1)
                    act.wait_ge(y_sb[k], e + 1)
                    rows = bass.ds(e * CAP + starts[k], HALF[k]) if not isinstance(e, int) else \
                        slice(e * CAP + starts[k], e * CAP + starts[k] + HALF[k])
                    act.dma_start(ybuf[rows, :].rearrange("(c p) d -> p c d", p=128),
                                  ys[:, p, c0:c0 + nchunk[k], :]).then_inc(y_out[p], 16)

                turns(act, step)
                for k in range(2):
                    store(E - 1, (E - 1) % 2, k)
                for p in range(2):
                    act.wait_ge(y_out[p], E // 2 * 32)

            @block.vector
            def _(dve):
                def transposed(e, p, k):
                    dve.wait_ge(xsT_ps, 2 * e + k + 1)
                    if not fresh(e):
                        dve.wait_ge(gu_ps, (e - 1) * U)
                    nc.vector.tensor_copy(xsT[:, p, starts[k]:starts[k] + HALF[k]],
                                          bank[:, 4 + k, 0:HALF[k]]).then_inc(xsT_sb, 1)

                def step(e, p):
                    for k in range(2):
                        for f in range(NF):
                            u = k * NF + f
                            dve.wait_ge(sg_sb, e * U + u + 1)
                            if not fresh(e) and f == 0:
                                dve.wait_ge(y_ps[k], e - 1)
                            nc.vector.tensor_tensor(h[:, p, f, starts[k]:starts[k] + HALF[k]],
                                                    sg[:, u % 2, 0:HALF[k]], bank[:, 2 * (u % 2) + 1, 0:HALF[k]],
                                                    ALU.mult).then_inc(h_sb, 1)
                            if u == NF and not (isinstance(e, int) and e == E - 1):
                                transposed(e + 1, 1 - p, 0)
                                transposed(e + 1, 1 - p, 1)

                transposed(0, 0, 0)
                transposed(0, 0, 1)
                turns(dve, step)


def shifted_out(g, nc, tile, ps):
    flat = lambda ap: ap.rearrange("p a s -> p (a s)")
    nc.scalar.copy(flat(g["cT"][0:64, tile, :]), ps[0:64, :])
    return nc.scalar.copy(flat(g["cT"][64:128, tile, 1:S]), ps[64:128, 0:S - 1])


def sequence_experts(nc, g, bank, ybuf, own, sb, sem):
    U = 3
    gy = sb("gy", [128, B, 2, D], ctx=own)
    xa = sb("xa", [128, 2, D], ctx=own)
    x1 = sb("x1", [128, 2, D], ctx=own)
    x1Ts = sb("x1Ts", [128, 2, S], ctx=own)
    ge = sb("ge", [128, 2, FF], ctx=own)
    h = sb("hseq", [128, 2, FF], ctx=own)
    hT = sb("hTseq", [128, 2, FF], ctx=own)
    cs = sb("cs", [128, 2, D], ctx=own)
    gsem = [sem(f"gather{i}", own) for i in range(4)]
    gathered, xa_sb, x1_sb = sem("gathered", own), sem("xa_sb", own), sem("x1_sb", own)
    x1T_ps, x1T_sb, x1_kept = sem("x1T_ps", own), sem("x1T_sb", own), sem("x1_kept", own)
    gu_ps, ge_sb, h_sb = sem("gus_ps", own), sem("ge_sb", own), sem("hs_sb2", own)
    hT_ps, hT_sb, down_done = sem("hTs_ps", own), sem("hTs_sb", own), sem("down_done", own)
    cs_sb, cT_ps = sem("cs_sb", own), sem("cTs_ps", own)
    ctok_sb, cT_sb = g["ctok_ready"], g["cT_ready"]
    LAG = 3

    def turns(eng, step):
        for n in range(6):
            step(n, n % 2)
        with eng.Fori(3, B // 2) as m:
            for p in range(2):
                step(m * 2 + p, p)
        for n in range(B, B + LAG):
            step(n, n % 2)

    def lagged(n, p, lag):
        if isinstance(n, int):
            k = n - lag
            return k, k % 2, 0 <= k < B, k >= 2
        return n - lag, (p - lag) % 2, True, True

    at = lambda k: slice(k, k + 1) if isinstance(k, int) else bass.ds(k, 1)

    with nc.Block() as block:
        @block.gpsimd
        def _(pool):
            def keep(b):
                pool.wait_ge(x1_sb, b + 1)
                nc.gpsimd.tensor_copy(g["x1"][:, b, :], x1[:, b % 2, :]).then_inc(x1_kept, 1)

            def keep_c(b):
                pool.wait_ge(cs_sb, b + 1)
                nc.gpsimd.tensor_copy(g["ctok"][:, b, :], cs[:, b % 2, :]).then_inc(ctok_sb, 1)

            for b in range(B + 5):
                if b < B:
                    for k in range(2):
                        nc.gpsimd.indirect_dma_start(
                            gy[:, b, k, :], None, ybuf,
                            bass.IndirectOffsetOnAxis(ap=g["gidx"][:, k, b:b + 1], axis=0),
                            bounds_check=NSLOT - 1, oob_is_err=False).then_inc(gsem[b % 4], 16)
                if 1 <= b <= B:
                    pool.wait_ge(gsem[(b - 1) % 4], ((b - 1) // 4 + 1) * 32)
                    pool.sem_inc(gathered, 1)
                if 2 <= b < B + 2:
                    keep(b - 2)
                if b >= 5:
                    keep_c(b - 5)

        @block.vector
        def _(dve):
            def step(n, p):
                k, q, there, later = lagged(n, p, 0)
                if there:
                    dve.wait_ge(gathered, k + 1)
                    if later:
                        dve.wait_ge(x1T_ps, k - 1)
                        dve.wait_ge(x1_kept, k - 1)
                    for j, (src, dst, done) in enumerate(((g["xtok"][:, at(k), :], xa[:, q:q + 1, :], xa_sb),
                                                          (xa[:, q:q + 1, :], x1[:, q:q + 1, :], x1_sb))):
                        if j:
                            dve.wait_ge(xa_sb, k + 1)
                        nc.vector.scalar_tensor_tensor(
                            out=dst.rearrange("p a d -> p (a d)"), in0=gy[:, at(k), j, :].rearrange("p a d -> p (a d)"),
                            scalar=g["gw"][:, j, at(k)], in1=src.rearrange("p a d -> p (a d)"),
                            op0=ALU.mult, op1=ALU.add).then_inc(done, 1)
                k, q, there, later = lagged(n, p, 1)
                if there:
                    for u in range(U):
                        r = (q * U + u) % 2
                        dve.wait_ge(ge_sb, k * U + u + 1)
                        if later or k * U + u >= 2:
                            dve.wait_ge(hT_ps, k * U + u - 1)
                        if u < 2:
                            nc.vector.scalar_tensor_tensor(
                                out=h[:, r, :], in0=ge[:, r, :],
                                scalar=g["selw"][:, at(k), u:u + 1].rearrange("p a b -> p (a b)"),
                                in1=bank[:, 2 * r + 1, :], op0=ALU.mult, op1=ALU.mult).then_inc(h_sb, 1)
                        else:
                            nc.vector.tensor_tensor(h[:, r, :], ge[:, r, :], bank[:, 2 * r + 1, :],
                                                    ALU.mult).then_inc(h_sb, 1)
                k, q, there, later = lagged(n, p, 2)
                if there:
                    dve.wait_ge(down_done, U * (k + 1))
                    if later:
                        dve.wait_ge(ctok_sb, k - 1)
                        dve.wait_ge(cT_ps, k - 1)
                    nc.vector.tensor_copy(cs[:, q, :], bank[:, 6, 0:D]).then_inc(cs_sb, 1)

            turns(dve, step)

        @block.scalar
        def _(act):
            def step(n, p):
                k, q, there, later = lagged(n, p, 0)
                if there:
                    act.wait_ge(x1T_ps, k + 1)
                    if later:
                        act.wait_ge(gu_ps, (k - 1) * U)
                    nc.scalar.copy(x1Ts[:, q, :], bank[:, 7, 0:S]).then_inc(x1T_sb, 1)
                k, q, there, later = lagged(n, p, 1)
                k2, q2, there2, later2 = lagged(n, p, 2)
                for u in range(U):
                    if there:
                        r = (q * U + u) % 2
                        act.wait_ge(gu_ps, k * U + u + 1)
                        if later or k * U + u >= 2:
                            act.wait_ge(h_sb, k * U + u - 1)
                        nc.scalar.activation(ge[:, r, :], bank[:, 2 * r, :], ACT.Gelu_apprx_tanh).then_inc(ge_sb, 1)
                    if there2:
                        r = (q2 * U + u) % 2
                        act.wait_ge(hT_ps, k2 * U + u + 1)
                        if later2 or k2 * U + u >= 2:
                            act.wait_ge(down_done, k2 * U + u - 1)
                        nc.scalar.copy(hT[:, r, :], bank[:, 4 + r, :]).then_inc(hT_sb, 1)
                k, q, there, later = lagged(n, p, 3)
                if there:
                    act.wait_ge(cT_ps, k + 1)
                    shifted_out(g, nc, at(k), bank[:, 7, S:2 * S]).then_inc(cT_sb, 1)

        
            turns(act, step)

        @block.tensor
        def _(pe):
            pe.wait_ge(g["late"], N_LATE)

            def down(k, q, u):
                r = (q * U + u) % 2
                e = E if u == 2 else chosen(k, u)
                pe.wait_ge(hT_sb, k * U + u + 1)
                for f in range(NF):
                    ins = nc.tensor.matmul(bank[:, 6, 0:D], hT[:, r, f * 128:(f + 1) * 128],
                                           g["wd"][:, at(e), f * D:(f + 1) * D],
                                           start=(u == 0 and f == 0), stop=(u == 2 and f == NF - 1))
                ins.then_inc(down_done, 1)

            def chosen(k, u):
                return pe.value_load(g["sel"][0:1, at(k), u:u + 1].rearrange("p a b -> p (a b)"), min_val=0, max_val=E - 1)

            def step(n, p):
                k, q, there, later = lagged(n, p, 0)
                k1, q1, there1, later1 = lagged(n, p, 1)
                k2, q2, there2, later2 = lagged(n, p, 2)
                k3, q3, there3, later3 = lagged(n, p, 3)
                for u in range(U):
                    if there1:
                        r = (q1 * U + u) % 2
                        if u == 0:
                            pe.wait_ge(x1T_sb, k1 + 1)
                        if later1 or k1 * U + u >= 2:
                            pe.wait_ge(h_sb, k1 * U + u - 1)
                        e = E if u == 2 else chosen(k1, u)
                        nc.tensor.matmul(bank[:, 2 * r, :], x1Ts[:, q1, :], g["wg"][:, at(e), :], start=True, stop=True)
                        nc.tensor.matmul(bank[:, 2 * r + 1, :], x1Ts[:, q1, :], g["wu"][:, at(e), :],
                                         start=True, stop=True).then_inc(gu_ps, 1)
                    if there2:
                        r = (q2 * U + u) % 2
                        pe.wait_ge(h_sb, k2 * U + u + 1)
                        if later2 or k2 * U + u >= 2:
                            pe.wait_ge(hT_sb, k2 * U + u - 1)
                        for f in range(NF):
                            ins = nc.tensor.transpose(bank[:, 4 + r, f * 128:(f + 1) * 128],
                                                      h[:, r, f * 128:(f + 1) * 128], g["eye"][:])
                        ins.then_inc(hT_ps, 1)
                        if u == 0 and (later2 or k2 >= 1):
                            pe.wait_ge(cs_sb, k2)
                        if u >= 1:
                            down(k2, q2, u - 1)
                    if u == 0 and there:
                        pe.wait_ge(x1_sb, k + 1)
                        if later or k >= 1:
                            pe.wait_ge(x1T_sb, k)
                        if not isinstance(k, int) or k >= 4:
                            pe.wait_ge(cT_sb, k - 3)
                        nc.tensor.transpose(bank[:, 7, 0:S], x1[:, q, :], g["eye"][:]).then_inc(x1T_ps, 1)
                    if u == 1 and there3:
                        pe.wait_ge(cs_sb, k3 + 1)
                        if later3 or k3 >= 1:
                            pe.wait_ge(cT_sb, k3)
                        pe.wait_ge(x1T_sb, min(k3 + 4, B) if isinstance(k3, int) else k3 + 4)
                        nc.tensor.transpose(bank[:, 7, S:2 * S], cs[:, q3, :], g["eye"][:]).then_inc(cT_ps, 1)
                if there2:
                    down(k2, q2, 2)

            turns(pe, step)


def transformer(nc, g, bank, out_dram, own, sb, sem):
    hT = sb("hT", [128, 2, S], ctx=own)
    sq = sb("sq", [128, 2 * INNER], ctx=own)
    ss = sb("ss", [128, 2, 16], ctx=own)
    rn = sb("rn", [128, 2, 16], ctx=own)
    t1 = sb("t1", [128, 2 * INNER], ctx=own)
    t2 = sb("t2", [128, 2 * INNER], ctx=own)
    kn = sb("kn", [128, INNER], ctx=own)
    qk = sb("qk", [128, 2, 2 * INNER], ctx=own)
    qkT = sb("qkT", [128, 2, 8, S], ctx=own)
    v = sb("v", [128, 2, INNER], ctx=own)
    mx = sb("mx", [128, HEADS], ctx=own)
    nb = sb("nb", [128, 2, HEADS], ctx=own)
    pa = sb("pa", [128, 2, 4, S], ctx=own)
    ls = sb("ls", [128, 2, HEADS], ctx=own)
    rl = sb("rl", [128, HEADS], ctx=own)
    pT = sb("pT", [128, 2, 4, S], ctx=own)
    oT = sb("oT", [128, INNER], ctx=own)
    c1 = sb("c1", [128, 2, 4, DH], ctx=own)
    c1b = sb("c1b", [128, 8, D], ctx=own)
    hs = sb("hs3", [128, D], ctx=own)
    stats = sb("stats2", [128, 6], ctx=own)
    mv = sb("mv2", [128, 2], ctx=own)
    ve = sb("ve", [128, 1], ctx=own)
    rstd = sb("rstd2", [128, 1], ctx=own)
    xh = sb("xh2", [128, D], ctx=own)
    xhT = sb("xhT", [128, S], ctx=own)
    ag = sb("ag", [128, 2, 2, HID], ctx=own)
    gl = sb("gl", [128, 2, HID], ctx=own)
    hh = sb("hh", [128, 2, HID], ctx=own)
    hhT = sb("hhT", [128, 3, S], ctx=own)
    c2 = sb("c2", [128, 2, D], ctx=own)
    hT_sb, qk_ps, v_ps, v_sb, sq_sb = (sem("d_" + n, own) for n in ("hT_sb", "qk_ps", "v_ps", "v_sb", "sq_sb"))
    ss0_sb, ss_sb, rnk_sb, rnq_sb = (sem("d_" + n, own) for n in ("ss0_sb", "ss_sb", "rnk_sb", "rnq_sb"))
    t_sb, add_sb, kn_sb = (sem("d_" + n, own) for n in ("t_sb", "add_sb", "kn_sb"))
    qT_ps, kT_ps, qT_sb, kT_sb = (sem("d_" + n, own) for n in ("qT_ps", "kT_ps", "qT_sb", "kT_sb"))
    s_ps, mx_sb, nb_sb, p_sb = (sem("d_" + n, own) for n in ("s_ps", "mx_sb", "nb_sb", "p_sb"))
    rl_sb, pn_sb = (sem("d_" + n, own) for n in ("rl_sb", "pn_sb"))
    pT_ps, pT_sb, o_ps, oT_sb = (sem("d_" + n, own) for n in ("pT_ps", "pT_sb", "o_ps", "oT_sb"))
    wo_ps, c1_sb, c1b_sb, h_ps, h_sb = (sem("d_" + n, own) for n in ("wo_ps", "c1_sb", "c1b_sb", "h_ps", "h_sb"))
    st_sb, mv_sb, ve_sb, rstd_sb, xh_sb = (sem("d_" + n, own) for n in ("st_sb", "mv_sb", "ve_sb", "rstd_sb", "xh_sb"))
    xhT_ps, xhT_sb, w1_ps, ag_sb = (sem("d_" + n, own) for n in ("xhT_ps", "xhT_sb", "w1_ps", "ag_sb"))
    gl_sb, hh_sb, hhT_ps, hhT_sb = (sem("d_" + n, own) for n in ("gl_sb", "hh_sb", "hhT_ps", "hhT_sb"))
    w2_ps, c2_sb, cT_ps = (sem("d_" + n, own) for n in ("w2_ps", "c2_sb", "cT_ps"))
    c1z_sb, res_sb, stored = sem("d_c1z_sb", own), sem("d_res_sb", own), sem("d_stored", own)
    cT_ready, ctok_ready = g["cT_ready"], g["ctok_ready"]
    LAG = 7
    FIRST = 10
    Q, K, VB, TA, TB, OB = 0, 1, 2, 5, 6, 7
    SB = (3, 4)

    def turns(eng, step):
        for n in range(FIRST):
            step(n, n % 2)
        with eng.Fori(FIRST // 2, NV // 2) as m:
            for p in range(2):
                step(m * 2 + p, p)
        for n in range(NV, NV + LAG + 1):
            step(n, n % 2)

    def lagged(n, p, lag):
        if isinstance(n, int):
            return n - lag, (n - lag) % 2, 0 <= n - lag < NV
        return n - lag, (p - lag) % 2, True

    def wait(eng, semaphore, value, most=None):
        if isinstance(value, int):
            if most is not None:
                value = min(value, most)
            if value <= 0:
                return
        eng.wait_ge(semaphore, value)

    def edge(eng, semaphore, value, most=None):
        if isinstance(value, int):
            wait(eng, semaphore, value, most)

    at = lambda k: slice(k, k + 1) if isinstance(k, int) else bass.ds(k, 1)
    ring = lambda k: slice(k % 8, k % 8 + 1) if isinstance(k, int) else bass.ds(k & 7, 1)
    layer = lambda k: at(k // B) if isinstance(k, int) else \
        bass.ds(nc.s_assert_within(k >> 4, 0, DEPTH - 1, skip_runtime_bounds_check_because="k is below DEPTH * B"), 1)
    flat = lambda ap: ap.rearrange("p a d -> p (a d)")
    heads = lambda ap: ap.rearrange("p (h d) -> p h d", d=DH)
    halves = lambda ap: ap.rearrange("p (w d) -> p w d", w=2)

    with nc.Block() as block:
        @block.tensor
        def _(pe):
            def turn(dst, src, blocks, ready):
                for b in range(blocks):
                    ins = nc.tensor.transpose(bank[:, dst, b * 128:(b + 1) * 128], src(b), g["eye"][:])
                ins.then_inc(ready, 1)

            def step(n, p):
                k, q, there = lagged(n, p, 1)
                if there:
                    pe.wait_ge(hT_sb, k + 1)
                    wait(pe, h_sb, k - 2)
                    edge(pe, v_sb, k)
                    nc.tensor.matmul(bank[:, VB, :], hT[:, q, :], flat(g["wqkv"][:, layer(k), 2 * INNER:]), start=True,
                                     stop=True).then_inc(v_ps, 1)
                    pe.wait_ge(add_sb, 2 * k + 2)
                    wait(pe, c1_sb, k - 1)
                    edge(pe, xhT_sb, k - 3)
                    edge(pe, pT_sb, 2 * k - 3)
                    edge(pe, qT_sb, k)
                    turn(TA, lambda b: qk[:, q, b * 128:(b + 1) * 128], 4, qT_ps)
                    pe.wait_ge(kn_sb, k + 1)
                    wait(pe, c2_sb, k - 5)
                    edge(pe, hhT_sb, k - 5)
                    edge(pe, pT_sb, 2 * k - 2)
                    edge(pe, kT_sb, k)
                    turn(TB, lambda b: qk[:, q, INNER + b * 128:INNER + (b + 1) * 128], 4, kT_ps)
                k, q, there = lagged(n, p, 0)
                if there:
                    pe.wait_ge(hT_sb, k + 1)
                    wait(pe, ag_sb, k - 4)
                    edge(pe, t_sb, 3 * k)
                    nc.tensor.matmul(bank[:, Q, :], hT[:, q, :], flat(g["wqkv"][:, layer(k), 0:INNER]), start=True,
                                     stop=True)
                    nc.tensor.matmul(bank[:, K, :], hT[:, q, :], flat(g["wqkv"][:, layer(k), INNER:2 * INNER]),
                                     start=True, stop=True).then_inc(qk_ps, 1)
                k, q, there = lagged(n, p, 7)
                if there:
                    pe.wait_ge(c2_sb, k + 1)
                    wait(pe, oT_sb, k + 5, NV)
                    edge(pe, cT_ready, B + k)
                    turn(OB, lambda b: c2[:, q, :], 1, cT_ps)
                k, q, there = lagged(n, p, 2)
                if there:
                    for par in range(2):
                        pe.wait_ge(pn_sb, 2 * k + par + 1)
                        wait(pe, (qT_sb, kT_sb)[par], k + 2, NV)
                        edge(pe, (c1_sb, c2_sb)[par], (k, k - 4)[par])
                        turn((TA, TB)[par], lambda b: pa[:, par, b, :], 4, pT_ps)
                k, q, there = lagged(n, p, 1)
                if there:
                    pe.wait_ge(qT_sb, k + 1)
                    pe.wait_ge(kT_sb, k + 1)
                    wait(pe, p_sb, 2 * k)
                    for par in range(2):
                        nc.tensor.matmul(bank[:, SB[par], :], g["eye16"][:],
                                         g["mask"][:].unsqueeze(1).to_broadcast([128, 4, 128]), start=True, stop=False)
                    for b in range(4):
                        for par in range(2):
                            rows = slice(64 * par, 64 * par + 64)
                            ins = nc.tensor.matmul(bank[:, SB[par], b * S:(b + 1) * S], qkT[rows, q, b, :],
                                                   qkT[rows, q, 4 + b, :], start=False, stop=(b == 3))
                    ins.then_inc(s_ps, 1)
                k, q, there = lagged(n, p, 3)
                if there:
                    pe.wait_ge(c1_sb, k + 1)
                    wait(pe, v_sb, k + 3, NV)
                    edge(pe, h_sb, k)
                    nc.tensor.matmul(bank[:, VB, 0:D], g["eye"][:], c1[:, q, 0:2, :], start=True, stop=False)
                    nc.tensor.matmul(bank[:, VB, 0:D], g["shift"][:], c1[:, q, 2:4, :], start=False,
                                     stop=True).then_inc(h_ps, 1)
                k, q, there = lagged(n, p, 4)
                if there:
                    pe.wait_ge(xh_sb, k + 1)
                    wait(pe, pT_sb, 2 * k + 5, 2 * NV)
                    edge(pe, c1_sb, k + 2, NV)
                    turn(TA, lambda b: xh[:], 1, xhT_ps)
                k, q, there = lagged(n, p, 6)
                if there:
                    pe.wait_ge(hh_sb, k + 1)
                    wait(pe, pT_sb, 2 * k + 10, 2 * NV)
                    edge(pe, c2_sb, k)
                    for b, (c, w) in enumerate(HCH):
                        ins = nc.tensor.transpose(bank[0:w, TB, b * 128:(b + 1) * 128], hh[:, q, c:c + w], g["eye"][:])
                    ins.then_inc(hhT_ps, 1)
                k, q, there = lagged(n, p, 2)
                if there:
                    pe.wait_ge(v_sb, k + 1)
                    pe.wait_ge(pT_sb, 2 * k + 2)
                    if not (isinstance(k, int) and k < 5):
                        wait(pe, cT_ready, B + k - 4)
                    edge(pe, oT_sb, k)
                    for b in range(4):
                        for par in range(2):
                            h = 2 * b + par
                            ins = nc.tensor.matmul(bank[64 * par:64 * par + 64, OB, b * S:(b + 1) * S],
                                                   v[:, q, h * DH:(h + 1) * DH], pT[:, par, b, :], start=True, stop=True)
                    ins.then_inc(o_ps, 1)
                k, q, there = lagged(n, p, 4)
                if there:
                    pe.wait_ge(xhT_sb, k + 1)
                    wait(pe, t_sb, 3 * k + 15, 3 * NV)
                    edge(pe, ag_sb, k)
                    for j in range(2):
                        ins = nc.tensor.matmul(bank[:, (Q, K)[j], 0:HID], xhT[:],
                                               flat(g["w1"][:, layer(k), j * HID:(j + 1) * HID]), start=True, stop=True)
                    ins.then_inc(w1_ps, 1)
                k, q, there = lagged(n, p, 6)
                if there:
                    pe.wait_ge(hhT_sb, k + 1)
                    for b, (c, w) in enumerate(HCH):
                        ins = nc.tensor.matmul(bank[:, TB, 0:D], hhT[0:w, b, :],
                                               flat(g["w2"][0:w, layer(k), b * D:(b + 1) * D]), start=(b == 0), stop=(b == 2))
                    ins.then_inc(w2_ps, 1)
                k, q, there = lagged(n, p, 2)
                if there:
                    pe.wait_ge(oT_sb, k + 1)
                    wait(pe, xhT_sb, k - 1)
                    for b in range(4):
                        ins = nc.tensor.matmul(bank[:, TA, 0:D], oT[:, b * 128:(b + 1) * 128],
                                               flat(g["wo"][:, layer(k), b * D:(b + 1) * D]), start=(b == 0), stop=(b == 3))
                    ins.then_inc(wo_ps, 1)

            pe.wait_ge(c1z_sb, 1)
            turns(pe, step)

        @block.scalar
        def _(act):
            def step(n, p):
                k, q, there = lagged(n, p, 1)
                if there:
                    act.wait_ge(v_ps, k + 1)
                    wait(act, o_ps, k - 1)
                    nc.scalar.copy(v[:, q, :], bank[:, VB, :]).then_inc(v_sb, 1)
                k, q, there = lagged(n, p, 7)
                if there:
                    act.wait_ge(cT_ps, k + 1)
                    shifted_out(g, nc, at(k + B), bank[:, OB, 0:S]).then_inc(cT_ready, 1)
                k, q, there = lagged(n, p, 0)
                if there:
                    act.wait_ge(qk_ps, k + 1)
                    wait(act, ss0_sb, k)
                    nc.scalar.activation(sq[:], bank[:, Q:K + 1, :].rearrange("p a d -> p (a d)"),
                                         ACT.Square).then_inc(sq_sb, 1)
                k, q, there = lagged(n, p, 2)
                if there:
                    for par in range(2):
                        act.wait_ge(pT_ps, 2 * k + par + 1)
                        wait(act, o_ps, k)
                        nc.scalar.copy(pT[:, par].rearrange("p a s -> p (a s)"),
                                       bank[:, (TA, TB)[par], :]).then_inc(pT_sb, 1)
                k, q, there = lagged(n, p, 3)
                if there:
                    act.wait_ge(h_ps, k + 1)
                    wait(act, xh_sb, k)
                    nc.scalar.copy(hs[:], bank[:, VB, 0:D]).then_inc(h_sb, 1)
                k, q, there = lagged(n, p, 4)
                if there:
                    act.wait_ge(xhT_ps, k + 1)
                    wait(act, w1_ps, k)
                    l = layer(k)
                    nc.scalar.activation(xhT[:], bank[:, TA, 0:S], ACT.Identity, scale=flat(g["lngb"][:, l, 0:1]),
                                         bias=flat(g["lngb"][:, l, 1:2])).then_inc(xhT_sb, 1)
                k, q, there = lagged(n, p, 6)
                if there:
                    act.wait_ge(hhT_ps, k + 1)
                    wait(act, w2_ps, k)
                    w = HCH[2][1]
                    nc.scalar.copy(hhT[:, 0:2, :], bank[:, TB, 0:2 * S].rearrange("p (a s) -> p a s", a=2))
                    nc.scalar.copy(hhT[0:w, 2, :], bank[0:w, TB, 2 * S:3 * S]).then_inc(hhT_sb, 1)
                k, q, there = lagged(n, p, 2)
                if there:
                    act.wait_ge(o_ps, k + 1)
                    wait(act, wo_ps, k)
                    nc.scalar.copy(oT[:], bank[:, OB, :]).then_inc(oT_sb, 1)
                k, q, there = lagged(n, p, 1)
                if there:
                    act.wait_ge(nb_sb, k + 1)
                    wait(act, rl_sb, k - 1)
                    for par in range(2):
                        wait(act, pT_ps, 2 * k - 1 + par)
                        for b in range(4):
                            h = 2 * b + par
                            ins = nc.scalar.activation(pa[:, par, b, :], bank[:, SB[par], b * S:(b + 1) * S], ACT.Exp,
                                                       bias=nb[:, q, h:h + 1], scale=rn[:, q, h:h + 1],
                                                       accum_out=ls[:, q, h:h + 1])
                        ins.then_inc(p_sb, 1)
                if p == 1:
                    for lag in (5, 4):
                        k, q, there = lagged(n, p, lag)
                        if there:
                            act.wait_ge(ag_sb, k + 1)
                            wait(act, hh_sb, k - 1)
                            nc.scalar.activation(gl[:, q, :], ag[:, q, 1, :], ACT.Gelu).then_inc(gl_sb, 1)

            turns(act, step)

        @block.vector
        def _(dve):
            def step(n, p):
                k, q, there = lagged(n, p, 1)
                if there:
                    for dst, src, ready, done in ((0, TA, qT_ps, qT_sb), (4, TB, kT_ps, kT_sb)):
                        dve.wait_ge(ready, k + 1)
                        wait(dve, s_ps, k - 1)
                        nc.vector.tensor_copy(qkT[:, q, dst:dst + 4, :],
                                              bank[:, src, :].rearrange("p (b s) -> p b s", b=4)).then_inc(done, 1)
                k, q, there = lagged(n, p, 2)
                if there:
                    dve.wait_ge(p_sb, 2 * k + 2)
                    nc.vector.reciprocal(rl[:], ls[:, q, :]).then_inc(rl_sb, 1)
                    dve.wait_ge(rl_sb, k + 1)
                    for par in range(2):
                        nc.vector.tensor_tensor(
                            pa[:, par], pa[:, par],
                            rl[:].rearrange("p (b w) -> p w b", w=2)[:, par].unsqueeze(2).to_broadcast([128, 4, S]),
                            ALU.mult).then_inc(pn_sb, 1)
                k, q, there = lagged(n, p, 4)
                if there:
                    dve.wait_ge(rstd_sb, k + 1)
                    wait(dve, xhT_ps, k)
                    nc.vector.tensor_scalar(xh[:], hs[:], mv[:, 0:1], rstd[:], ALU.subtract, ALU.mult).then_inc(xh_sb, 1)
                k, q, there = lagged(n, p, 0)
                if there:
                    dve.wait_ge(sq_sb, k + 1)
                    wait(dve, rnq_sb, k - 1)
                    nc.vector.reduce_sum(ss[:, q, :], heads(sq[:]), X).then_inc(ss0_sb, 1)
                    wait(dve, add_sb, 2 * k)
                    l = layer(k)
                    src = bank[:, Q:K + 1, :].rearrange("p w (h d) -> p w h d", d=DH)
                    both = lambda t: t[:].rearrange("p (w h d) -> p w h d", w=2, d=DH)
                    table = lambda j, lo, hi: g["rot"][:, j, l, :].rearrange(
                        "p a (w d) -> p (a w) d", w=2)[:, :, lo:hi].unsqueeze(2).to_broadcast([128, 2, HEADS, hi - lo])
                    nc.vector.tensor_tensor(both(t1), src, table(0, 0, DH), ALU.mult).then_inc(t_sb, 1)
                    dve.wait_ge(ss0_sb, k + 1)
                    nc.vector.tensor_scalar_max(ss[:, q, :], ss[:, q, :], 1e-24).then_inc(ss_sb, 1)
                    for lo, hi, fl in ((0, 32, 32), (32, 64, 0)):
                        nc.vector.tensor_tensor(both(t2)[:, :, :, lo:hi], src[:, :, :, fl:fl + 32], table(1, lo, hi),
                                                ALU.mult).then_inc(t_sb, 1)
                k, q, there = lagged(n, p, 1)
                if there:
                    dve.wait_ge(s_ps, k + 1)
                    for par in range(2):
                        nc.vector.reduce_max(mx[:].rearrange("p (b w) -> p w b", w=2)[:, par],
                                             bank[:, SB[par], :].rearrange("p (b s) -> p b s", b=4), X).then_inc(mx_sb, 1)
                    dve.wait_ge(mx_sb, 2 * k + 2)
                    dve.wait_ge(rnq_sb, k + 1)
                    wait(dve, p_sb, 2 * k - 2)
                    nc.vector.scalar_tensor_tensor(out=nb[:, q, :], in0=mx[:], scalar=-1.0, in1=rn[:, q, 0:8],
                                                   op0=ALU.mult, op1=ALU.mult).then_inc(nb_sb, 1)
                k3, _, there3 = lagged(n, p, 3)
                if there3:
                    dve.wait_ge(h_sb, k3 + 1)
                    nc.vector.bn_stats(stats[:], hs[:]).then_inc(st_sb, 1)
                    dve.wait_ge(st_sb, k3 + 1)
                k, q, there = lagged(n, p, 4)
                if there:
                    dve.wait_ge(w1_ps, k + 1)
                    wait(dve, hh_sb, k - 1)
                    nc.vector.tensor_tensor(ag[:, q], bank[:, Q:K + 1, 0:HID],
                                            g["b1"][:, layer(k), :].rearrange("p a (w c) -> p (a w) c", w=2),
                                            ALU.add).then_inc(ag_sb, 1)
                if there3:
                    nc.vector.bn_aggr(mv[:], stats[:]).then_inc(mv_sb, 1)
                    dve.wait_ge(mv_sb, k3 + 1)
                    wait(dve, rstd_sb, k3)
                    nc.vector.tensor_scalar_add(ve[:], mv[:, 1:2], 1e-5).then_inc(ve_sb, 1)
                k, q, there = lagged(n, p, 6)
                if there:
                    dve.wait_ge(w2_ps, k + 1)
                    dve.wait_ge(c1b_sb, k + 1)
                    wait(dve, cT_ps, k - 1)
                    if not (isinstance(k, int) and k < 2):
                        wait(dve, ctok_ready, B + k - 1)
                    nc.vector.tensor_tensor(c2[:, q, :], bank[:, TB, 0:D], flat(c1b[:, ring(k), :]),
                                            ALU.add).then_inc(c2_sb, 1)
                k, q, there = lagged(n, p, 2)
                if there:
                    dve.wait_ge(wo_ps, k + 1)
                    dve.wait_ge(ctok_ready, k + 1)
                    wait(dve, h_ps, k - 1)
                    wait(dve, c1b_sb, k - 1)
                    nc.vector.tensor_tensor(c1[:, q, 0:4:3, :], halves(bank[:, TA, 0:D]), halves(flat(g["ctok"][:, at(k), :])),
                                            ALU.add).then_inc(c1_sb, 1)

            turns(dve, step)

        @block.gpsimd
        def _(pool):
            def take_input(k, q):
                pool.wait_ge(cT_ready, k + 1)
                wait(pool, v_ps, k - 1)
                nc.gpsimd.tensor_copy(hT[:, q, :], flat(g["cT"][:, at(k), :])).then_inc(hT_sb, 1)

            def step(n, p):
                k, q, there = lagged(n, p, -1)
                if there:
                    take_input(k, q)
                k, q, there = lagged(n, p, 3)
                if there:
                    pool.wait_ge(c1_sb, k + 1)
                    wait(pool, c2_sb, k - 5)
                    nc.gpsimd.tensor_tensor(halves(flat(c1b[:, ring(k), :])), c1[:, q, 0:4:3, :],
                                            halves(flat(g["b2"][:, layer(k), :])), ALU.add).then_inc(c1b_sb, 1)
                k, q, there = lagged(n, p, 7)
                if there:
                    pool.wait_ge(c2_sb, k + 1)
                    nc.gpsimd.tensor_copy(flat(g["ctok"][:, at(k + B), :]), c2[:, q, :]).then_inc(ctok_ready, 1)
                k, q, there = lagged(n, p, 0)
                if there:
                    pool.wait_ge(ss_sb, k + 1)
                    wait(pool, kn_sb, k - 1)
                    nc.gpsimd.tensor_tensor(rn[:, q, 8:16], ss[:, q, 8:16], g["nhalf"][:].to_broadcast([128, 8]),
                                            ALU.pow).then_inc(rnk_sb, 1)
                    pool.wait_ge(t_sb, 3 * k + 3)
                    wait(pool, kT_ps, k - 1)
                    wait(pool, kn_sb, k)
                    nc.gpsimd.tensor_tensor(kn[:], t1[:, INNER:], t2[:, INNER:], ALU.add).then_inc(add_sb, 1)
                    nc.gpsimd.tensor_tensor(qk[:, q, 0:INNER], t1[:, 0:INNER], t2[:, 0:INNER], ALU.add).then_inc(add_sb, 1)
                    pool.wait_ge(rnk_sb, k + 1)
                    pool.wait_ge(add_sb, 2 * k + 1)
                    nc.gpsimd.tensor_tensor(heads(qk[:, q, INNER:]), heads(kn[:]),
                                            rn[:, q, 8:16].unsqueeze(2).to_broadcast([128, HEADS, DH]),
                                            ALU.mult).then_inc(kn_sb, 1)
                    wait(pool, p_sb, 2 * k - 2)
                    nc.gpsimd.tensor_tensor(rn[:, q, 0:8], ss[:, q, 0:8], g["nhalf"][:].to_broadcast([128, 8]),
                                            ALU.pow).then_inc(rnq_sb, 1)
                k, q, there = lagged(n, p, 3)
                if there:
                    pool.wait_ge(ve_sb, k + 1)
                    wait(pool, xh_sb, k)
                    nc.gpsimd.tensor_tensor(rstd[:], ve[:], g["nhalf"][:], ALU.pow).then_inc(rstd_sb, 1)
                if p == 1:
                    for lag in (5, 4):
                        k, q, there = lagged(n, p, lag)
                        if there:
                            pool.wait_ge(gl_sb, k + 1)
                            wait(pool, hhT_ps, k - 1)
                            nc.gpsimd.tensor_tensor(hh[:, q, :], ag[:, q, 0, :], gl[:, q, :], ALU.mult).then_inc(hh_sb, 1)

            nc.gpsimd.memset(c1[:, :, 1:3, :], 0.0).then_inc(c1z_sb, 1)
            take_input(0, 0)
            turns(pool, step)
            for c in range(4):
                lo, hi = c * B // 4, (c + 1) * B // 4
                pool.wait_ge(ctok_ready, 2 * B + hi)
                nc.gpsimd.tensor_tensor(g["x1"][:, lo:hi, :], g["x1"][:, lo:hi, :],
                                        g["ctok"][:, 2 * B + lo:2 * B + hi, :], ALU.add).then_inc(res_sb, 1)

        @block.sync
        def _(sp):
            for c in range(4):
                lo, hi = c * B // 4, (c + 1) * B // 4
                sp.wait_ge(res_sb, c + 1)
                sp.dma_start(out_dram[:, lo:hi, :], g["x1"][:, lo:hi, :]).then_inc(stored, 16)
            sp.wait_ge(stored, 64)


def lay_out(i):
    c = np.ascontiguousarray
    f = {k: np.asarray(v) for k, v in i.items()}
    x = f["x"]
    gates = lambda skill, shared: c(np.concatenate([skill, shared[None]]).transpose(1, 0, 2))
    w_down = np.concatenate([f["L1_cond_skill_down"], f["L1_cond_shared_down"][None]])
    pad = np.zeros((DEPTH, 3 * 128 - HID, D), np.float32)
    w2 = np.concatenate([f["L1_ffn_w2"], pad], 1)
    chunks = lambda w, n: c(w.reshape(w.shape[0], n, 128, D).transpose(2, 0, 1, 3).reshape(128, w.shape[0], n * D))
    return {
        "xT": c(x.reshape(T, D).T), "xtok": c(x.transpose(1, 0, 2)),
        "AsT": c(f["L0_cond_As"].reshape(E * RANK, D).T),
        "BsT": c(f["L0_cond_Bs"].transpose(0, 2, 1).reshape(E * RANK, D)),
        "WbT": c(f["L0_cond_W_base"].T), "WrT": c(f["L0_ffn_Wr"].T),
        "wcol": c(np.repeat(f["cond_8"].T, RANK, axis=0)), "cond": c(f["cond_8"].reshape(1, -1)),
        "rows": c(np.concatenate([f["L0_cond_b_base"], f["L0_ffn_ln_gamma"], f["L0_ffn_ln_beta"]])[None]),
        "qs": c(np.concatenate([f["L1_ffn_q_scale"], f["L1_ffn_k_scale"]], 1).reshape(1, -1)),
        "w12": c(f["L0_ffn_W12"].transpose(2, 0, 1)),
        "w3": c(f["L0_ffn_W3"].transpose(2, 0, 1).reshape(NF, 128, E, D).transpose(1, 2, 0, 3).reshape(128, E, NF * D)),
        "wg": gates(f["L1_cond_skill_gate"], f["L1_cond_shared_gate"]),
        "wu": gates(f["L1_cond_skill_up"], f["L1_cond_shared_up"]),
        "wd": chunks(w_down, NF), "wqkv": c(f["L1_ffn_wqkv"].transpose(1, 0, 2)), "wo": chunks(f["L1_ffn_wo"], NF),
        "w1": c(f["L1_ffn_w1"].transpose(1, 0, 2)), "w2": chunks(w2, 3),
        "b1": c(f["L1_ffn_b1"].reshape(1, -1)), "b2": c(f["L1_ffn_b2"].reshape(1, -1)),
        "lngb": c(np.stack([f["L1_ffn_ln_g"], f["L1_ffn_ln_b"]], -1).transpose(1, 0, 2)),
    }


def kernel(**inputs):
    import concourse.bacc as _bacc
    from concourse.bass_utils import run_bass_kernel_spmd as _run

    nc = _bacc.Bacc("TRN2", target_bir_lowering=False, num_devices=1)
    arrays, args = {}, {}
    for name, a in {**lay_out(inputs), **{k: np.ascontiguousarray(v) for k, v in constants().items()}}.items():
        arrays[f"in_{name}"] = a
        args[name] = nc.dram_tensor(f"in_{name}", a.shape, mybir.dt.from_np(a.dtype), kind="ExternalInput").ap()
    out = nc.dram_tensor("out", (B, S, D), F32, kind="ExternalOutput").ap()
    build(nc, args, out.rearrange("b s d -> s b d"))
    r = _run(nc, [arrays], core_ids=[0])
    return r.results[0]["out"]
```

```python
import numpy as np

import concourse.bass as bass
from concourse import mybir
from concourse.alu_op_type import AluOpType as ALU

F32 = mybir.dt.float32
BF16 = mybir.dt.bfloat16
I32 = mybir.dt.int32
U32 = mybir.dt.uint32
ACT = mybir.ActivationFunctionType
X = mybir.AxisListType.X

B, S, D = 16, 128, 128
T = B * S
E = 8
RANK = 16
LORA_SCALE = 32.0 / RANK
FF = 512
NF = FF // 128
CAP = -(-(-(-T * 2 * 5 // 4)) // E)
NSLOT = E * CAP
NCH = CAP // 128
HALF = (3 * 128, 2 * 128)
HEADS, DH = 8, 64
INNER = HEADS * DH
HID = int(D * 4 * 2 / 3)
HCH = [(0, 128), (128, 128), (256, HID - 256)]
DEPTH = 2
WINDOW = 64
NV = DEPTH * B
G = 4
NG = B // G
DROP = float(1 << 20)
MASKED = -1e30


def constants():
    f = np.float32
    eye = np.eye(128, dtype=f)
    shift = np.eye(128, k=1, dtype=f)
    i, j = np.arange(128)[:, None], np.arange(128)[None, :]
    mask = np.where((i < j) | (i > j + WINDOW), MASKED, 0.0).astype(f)
    before = (i < j).astype(f)
    half = np.arange(0, DH, 2, dtype=f)
    inv = (f(1.0) / f(10000.0) ** (half / f(DH))).astype(f)
    t = np.arange(S, dtype=f)
    freqs = t[:, None] * inv[None, :]
    freqs = np.concatenate([freqs, freqs], -1).astype(f)
    base = (half + f(0.4 * DH)) / f(1.4 * DH)
    power = (t - S // 2) / f(WINDOW // 2)
    sc = (base[None, :].astype(f) ** power[:, None].astype(f)).astype(f)
    sc = np.concatenate([sc, sc], -1)
    cos, sin = np.cos(freqs).astype(f), np.sin(freqs).astype(f)
    sign = np.where(np.arange(DH) < DH // 2, -1.0, 1.0).astype(f)
    qk = np.stack([sc * f(8.0), f(1.0) / sc], 1)
    rot = np.stack([cos[:, None] * qk, (sin * sign)[:, None] * qk], 1).astype(f)
    e = np.arange(E, dtype=f)
    table = np.zeros((3, B, E), f)
    table[0] = E - e
    table[1] = e * FF
    table[2] = e * CAP
    return {"eye": eye, "shift": shift, "masks": np.stack([mask, before], 1), "rotary": np.ascontiguousarray(rot),
            "table": table.reshape(1, -1)}


def build(nc, a, out_dram):
    from contextlib import ExitStack
    stack = ExitStack()
    with stack:
        def sb(name, shape, dt=F32, ctx=stack):
            return ctx.enter_context(nc.sbuf_tensor(name, shape, dt))

        def sem(name, ctx=stack):
            return ctx.enter_context(nc.semaphore(name))

        xbuf = nc.dram_tensor("xbuf", (NSLOT, D), F32, kind="Internal").ap()
        ybuf = nc.dram_tensor("ybuf", (NSLOT, D), F32, kind="Internal").ap()
        g = {}
        bank = stack.enter_context(nc.psum_tensor("bank", [128, 8, 512], F32))
        g["eye"] = sb("eye", [128, 128])
        g["shift"] = sb("shift", [128, 128])
        g["mask"] = sb("mask", [128, 128], BF16)
        g["eye16"] = sb("eye16", [128, 128], BF16)
        g["nhalf"] = sb("nhalf", [128, 1])
        g["wqkv"] = sb("wqkv", [128, DEPTH, 3 * INNER])
        g["wo"] = sb("wo", [128, DEPTH, NF * D])
        g["w1"] = sb("w1", [128, DEPTH, 2 * HID])
        g["b1"] = sb("b1", [128, DEPTH, 2 * HID])
        g["w2"] = sb("w2", [128, DEPTH, 3 * D])
        g["b2"] = sb("b2", [128, DEPTH, D])
        g["lngb"] = sb("lngb", [128, DEPTH, 2])
        g["rot"] = sb("rot", [128, 2, DEPTH, 2 * DH])
        g["x1"] = sb("x1_all", [128, B, D])
        g["ctok"] = sb("ctok", [128, 3 * B, D])
        g["xtok"] = g["ctok"][:, 2 * B:, :]
        g["cT"] = sb("cT", [128, 3 * B, S])
        g["sel"] = sb("sel", [128, B, 2], I32)
        g["selw"] = sb("selw", [128, B, 2])
        g["cT_ready"] = sem("cT_ready")
        g["ctok_ready"] = sem("ctok_ready")
        g["late"] = sem("late_weights")
        g["gidx"] = sb("gidx", [128, 2, B], U32)
        g["gw"] = sb("gw", [128, 2, B])
        with ExitStack() as moe:
            g["wg"] = sb("wg", [128, E + 1, FF], ctx=moe)
            g["wu"] = sb("wu", [128, E + 1, FF], ctx=moe)
            g["wd"] = sb("wd", [128, E + 1, NF * D], ctx=moe)
            route(nc, a, g, bank, xbuf, stack, sb, sem)
            experts(nc, a, g, bank, xbuf, ybuf, sb, sem)
            with ExitStack() as own:
                sequence_experts(nc, g, bank, ybuf, own, sb, sem)
        with ExitStack() as own:
            transformer(nc, g, bank, out_dram, own, sb, sem)


LATE = [("wg", "wg"), ("wu", "wu"), ("wd", "wd"), ("wqkv", "wqkv"), ("wo", "wo"), ("w1", "w1"),
        ("w2", "w2"), ("lngb", "lngb"), ("shift", "shift")]
LATE_ROWS = [("b1", DEPTH * 2 * HID), ("b2", DEPTH * D)]
N_LATE = 16 * (len(LATE) + len(LATE_ROWS))


def route(nc, a, g, bank, xbuf, stack, sb, sem):
    from contextlib import ExitStack
    with ExitStack() as own:
        xT = sb("xT", [128, T], ctx=own)
        AsT = sb("AsT", [128, 128], ctx=own)
        BsT = sb("BsT", [128, 128], ctx=own)
        WbT = sb("WbT", [128, 128], ctx=own)
        WrT = sb("WrT", [128, E], ctx=own)
        wcol = sb("wcol", [128, B], ctx=own)
        rows = sb("rows", [128, 3, D], ctx=own)
        cond = sb("cond", [128, B, E], ctx=own)
        table = sb("table_sb", [128, 3, B, E], ctx=own)
        qs = sb("qs", [128, DEPTH, 2 * DH], ctx=own)
        rotc = sb("rotc", [128, 2, 2 * DH], ctx=own)
        masks = sb("masks", [128, 2, 128], ctx=own)
        before = sb("before", [128, 128], BF16, ctx=own)
        ones = sb("ones", [128, 128], BF16, ctx=own)
        hs = sb("hs", [128, 2, G * S], ctx=own)
        c0 = sb("c0", [128, 2, G, D], ctx=own)
        stats = sb("stats", [128, 2, G, 6], ctx=own)
        mv = sb("mv", [128, 2, G, 2], ctx=own)
        rstd = sb("rstd", [128, 2, G], ctx=own)
        xh = sb("xh", [128, 2, G, D], ctx=own)
        xg = sb("xg", [128, G, D], ctx=own)
        xn = sb("xn", [128, B, D], ctx=own)
        xnT = sb("xnT", [128, 2, G * S], ctx=own)
        zero = sb("zero", [128, NSLOT * D // 512], ctx=own)
        lg = sb("lg", [128, B, E], ctx=own)
        ex = sb("ex", [128, B, E], ctx=own)
        pr = sb("pr", [128, B, E], ctx=own)
        pr2 = sb("pr2", [128, B, E], ctx=own)
        oh = sb("oh", [128, 2, B, E], ctx=own)
        tmp = sb("tmp", [128, B, E], ctx=own)
        tmp2 = sb("tmp2", [128, B, E], ctx=own)
        tmp3 = sb("tmp3", [128, B, E], ctx=own)
        both = sb("both", [128, B, E], BF16, ctx=own)
        kept = sb("kept", [128, B, E], ctx=own)
        slot = sb("slot", [128, B, E], ctx=own)
        col = sb("col", [128, 8, B], ctx=own)
        sidx = sb("sidx", [128, 2, B], U32, ctx=own)

        WT = B // 2
        flat_be = lambda t: t.rearrange("p b e -> p (b e)")

        first = sem("first_loads", own)
        xin = [sem(f"x_loads{i}", own) for i in range(NG)]
        early = sem("early_loads", own)
        router_in = sem("router_loads", own)
        zeroed = sem("zero_tile", own)
        cleared = sem("xbuf_cleared", own)
        h_ps, hs_sb = sem("h_ps", own), sem("hs_sb", own)
        c0_ps, c0_sb = sem("c0_ps", own), sem("c0_sb", own)
        st_done, mv_done, rstd_done = sem("st_done", own), sem("mv_done", own), sem("rstd_done", own)
        xh_done, xg_done, xn_done = sem("xh_done", own), sem("xg_done", own), sem("xn_done", own)
        xnT_ps, xnT_sb, lg_ps = sem("xnT_ps", own), sem("xnT_sb", own), sem("lg_ps", own)
        chain = sem("router_steps", own)
        lg_ready, ex_ready = sem("lg_ready", own), sem("ex_ready", own)
        both_ready, rank_ps = sem("both_ready", own), sem("rank_ps", own)
        sidx_ready, scattered = sem("sidx_ready", own), sem("scattered", own)
        small = sem("small_constants", own)
        nh_done, rot_done = sem("nh_done", own), sem("rot_done", own)

        with nc.Block() as block:
            @block.sync
            def _(sp):
                sp.dma_start(AsT[:], a["AsT"]).then_inc(first, 16)
                sp.dma_start(xT[:, 0:G * S], a["xT"][:, 0:G * S]).then_inc(xin[0], 16)
                sp.dma_start(wcol[:], a["wcol"]).then_inc(first, 16)
                sp.dma_start(WbT[:], a["WbT"]).then_inc(first, 16)
                sp.dma_start(BsT[:], a["BsT"]).then_inc(first, 16)
                sp.dma_start(rows[:].rearrange("p a d -> p (a d)"),
                             a["rows"][0, :].partition_broadcast(128)).then_inc(first, 16)
                sp.dma_start(g["eye"][:], a["eye"]).then_inc(router_in, 16)
                sp.dma_start(WrT[:], a["WrT"]).then_inc(router_in, 16)
                for i in range(1, NG):
                    sp.dma_start(xT[:, i * G * S:(i + 1) * G * S],
                                 a["xT"][:, i * G * S:(i + 1) * G * S]).then_inc(xin[i], 16)
                sp.dma_start(cond[:].rearrange("p b e -> p (b e)"),
                             a["cond"][0, :].partition_broadcast(128)).then_inc(early, 16)
                sp.dma_start(table[:].rearrange("p k b e -> p (k b e)"),
                             a["table"][0, :].partition_broadcast(128)).then_inc(early, 16)
                sp.dma_start(masks[:], a["masks"]).then_inc(early, 16)
                sp.dma_start(qs[:].rearrange("p l d -> p (l d)"),
                             a["qs"][0, :].partition_broadcast(128)).then_inc(early, 16)
                sp.dma_start(rotc[:], a["rotary"]).then_inc(early, 16)
                sp.dma_start(g["xtok"], a["xtok"]).then_inc(early, 16)
                sp.wait_ge(zeroed, 1)
                for i in range(4):
                    sp.dma_start(xbuf.rearrange("(q p r) d -> q p (r d)", q=4, p=128)[i],
                                 zero[:]).then_inc(cleared, 16)
                for sbuf, dram in LATE:
                    sp.dma_start(g[sbuf][:], a[dram]).then_inc(g["late"], 16)
                for name, n in LATE_ROWS:
                    sp.dma_start(g[name][:].rearrange("p l d -> p (l d)"),
                                 a[name][0, :].partition_broadcast(128)).then_inc(g["late"], 16)

            @block.tensor
            def _(pe):
                def lora(i):
                    pe.wait_ge(xin[i], 16)
                    if i >= 2:
                        pe.wait_ge(hs_sb, i - 1)
                    nc.tensor.matmul(bank[:, i % 2, :], AsT[:], xT[:, i * G * S:(i + 1) * G * S], start=True,
                                     stop=True).then_inc(h_ps, 1)

                def project(i):
                    pe.wait_ge(hs_sb, i + 1)
                    if i >= 2:
                        pe.wait_ge(c0_sb, i - 1)
                    for t in range(G):
                        o = bank[:, 2 + i % 2, t * D:(t + 1) * D]
                        nc.tensor.matmul(o, xT[:, i * G * S + t * S:i * G * S + (t + 1) * S], WbT[:],
                                         start=True, stop=False)
                        last = nc.tensor.matmul(o, hs[:, i % 2, t * S:(t + 1) * S], BsT[:], start=False, stop=True)
                    last.then_inc(c0_ps, 1)

                def router(i):
                    pe.wait_ge(xn_done, i + 1)
                    if i >= 2:
                        pe.wait_ge(xnT_sb, i - 1)
                    for t in range(G):
                        last = nc.tensor.transpose(bank[:, 4 + i % 2, t * S:(t + 1) * S], xn[:, i * G + t, :],
                                                   g["eye"][:])
                    last.then_inc(xnT_ps, 1)
                    pe.wait_ge(xnT_sb, i + 1)
                    for t in range(G):
                        n = i * G + t
                        last = nc.tensor.matmul(bank[:, 6 + n // WT, n * E:(n + 1) * E], xnT[:, i % 2, t * S:(t + 1) * S],
                                                WrT[:], start=True, stop=True)
                    last.then_inc(lg_ps, 1)

                def rank(w):
                    pe.wait_ge(both_ready, w + 1)
                    pe.wait_ge(small, 2)
                    at = slice(w * WT * E, (w + 1) * WT * E)
                    nc.tensor.matmul(bank[:, 2 + w, 0:WT * E], before[:], flat_be(both[:])[:, at],
                                     start=True, stop=False)
                    for t in range((w + 1) * WT - 1):
                        lo = max(t + 1, w * WT)
                        last = nc.tensor.matmul(bank[:, 2 + w, (lo - w * WT) * E:WT * E], ones[:],
                                                both[:, t:t + 1, :].to_broadcast([128, (w + 1) * WT - lo, E]),
                                                start=False, stop=(t == (w + 1) * WT - 2))
                    last.then_inc(rank_ps, 1)

                pe.wait_ge(first, 80)
                lora(0)
                lora(1)
                for i in range(NG):
                    project(i)
                    if i + 2 < NG:
                        lora(i + 2)
                pe.wait_ge(router_in, 32)
                for i in range(NG - 1):
                    router(i)
                rank(0)
                router(NG - 1)
                rank(1)

            @block.scalar
            def _(act):
                def exps(tiles, i):
                    act.wait_ge(lg_ready, i + 1)
                    nc.scalar.activation(ex[:, tiles, :], lg[:, tiles, :], ACT.Exp).then_inc(ex_ready, 1)

                act.wait_ge(router_in, 32)
                act.wait_ge(early, 96)
                nc.scalar.copy(g["eye16"][:], g["eye"][:])
                nc.scalar.copy(g["mask"][:], masks[:, 0, :])
                nc.scalar.copy(before[:], masks[:, 1, :]).then_inc(small, 1)
                for i in range(NG):
                    act.wait_ge(xnT_ps, i + 1)
                    if i >= 2:
                        act.wait_ge(lg_ps, i - 1)
                    nc.scalar.copy(xnT[:, i % 2, :], bank[:, 4 + i % 2, :]).then_inc(xnT_sb, 1)
                    if (i + 1) % (NG // 2) == 0:
                        w = (i + 1) // (NG // 2) - 1
                        exps(slice(w * WT, (w + 1) * WT), w)
                exps(slice(0, B), 2)

            @block.gpsimd
            def _(pool):
                nc.gpsimd.memset(zero[:], 0.0).then_inc(zeroed, 1)
                nc.gpsimd.memset(ones[:], 1.0).then_inc(small, 1)
                nc.gpsimd.memset(g["nhalf"][:], -0.5).then_inc(nh_done, 1)
                nc.gpsimd.memset(g["cT"][:, :, 0:1], 0.0).then_inc(nh_done, 1)
                pool.wait_ge(nh_done, 2)
                pool.wait_ge(first, 80)
                for i in range(NG + 1):
                    if i < NG:
                        pool.wait_ge(mv_done, i + 1)
                        nc.gpsimd.tensor_tensor(rstd[:, i % 2, :], mv[:, i % 2, :, 1],
                                                g["nhalf"][:].to_broadcast([128, G]), ALU.pow).then_inc(rstd_done, 1)
                    if i >= 1:
                        pool.wait_ge(xh_done, i)
                        if i >= 2:
                            pool.wait_ge(xn_done, i - 1)
                        nc.gpsimd.tensor_tensor(xg[:], xh[:, (i - 1) % 2], rows[:, 1:2, :].to_broadcast([128, G, D]),
                                                ALU.mult).then_inc(xg_done, 1)
                        pool.wait_ge(xg_done, i)
                        nc.gpsimd.tensor_tensor(xn[:, (i - 1) * G:i * G, :], xg[:],
                                                rows[:, 2:3, :].to_broadcast([128, G, D]), ALU.add).then_inc(xn_done, 1)
                pool.wait_ge(early, 96)
                for l in range(DEPTH):
                    nc.gpsimd.tensor_tensor(g["rot"][:, 0, l, :], rotc[:, 0, :], qs[:, l, :], ALU.mult).then_inc(rot_done, 1)
                    for h in range(2):
                        pick = lambda t, k: t.rearrange("p (w h d) -> p w h d", w=2, h=2)[:, :, k, :]
                        nc.gpsimd.tensor_tensor(pick(g["rot"][:, 1, l, :], h), pick(rotc[:, 1, :], h),
                                                pick(qs[:, l, :], 1 - h), ALU.mult).then_inc(rot_done, 1)
                pool.wait_ge(cleared, 64)
                for t in range(B):
                    if t % WT == 0:
                        pool.wait_ge(sidx_ready, 2 * (t // WT + 1))
                    for k in range(2):
                        nc.gpsimd.indirect_dma_start(
                            xbuf, bass.IndirectOffsetOnAxis(ap=sidx[:, k, t:t + 1], axis=0), xn[:, t, :], None,
                            bounds_check=NSLOT - 1, oob_is_err=False).then_inc(scattered, 16)
                pool.wait_ge(scattered, 2 * B * 16)

            @block.vector
            def _(dve):
                steps = [0]

                def then(ins):
                    steps[0] += 1
                    ins.then_inc(chain, 1)
                    dve.wait_ge(chain, steps[0])

                def per_tile(c):
                    return c.unsqueeze(2).to_broadcast([128, c.shape[1], E])

                def softmax_top2(exps, eps, w_out, ts):
                    then(nc.vector.reduce_sum(col[:, 1, ts], exps[:, ts], X))
                    if eps:
                        then(nc.vector.tensor_scalar_add(col[:, 1, ts], col[:, 1, ts], eps))
                    then(nc.vector.reciprocal(col[:, 2, ts], col[:, 1, ts]))
                    then(nc.vector.tensor_tensor(pr[:, ts], exps[:, ts], per_tile(col[:, 2, ts]), ALU.mult))
                    for k, p in enumerate((pr, pr2)):
                        then(nc.vector.reduce_max(w_out[:, k, ts], p[:, ts], X))
                        then(nc.vector.tensor_tensor(tmp[:, ts], p[:, ts], per_tile(w_out[:, k, ts]), ALU.is_equal))
                        then(nc.vector.tensor_tensor(tmp2[:, ts], tmp[:, ts], table[:, 0, ts], ALU.mult))
                        then(nc.vector.reduce_max(col[:, 3, ts], tmp2[:, ts], X))
                        then(nc.vector.tensor_tensor(oh[:, k, ts], tmp2[:, ts], per_tile(col[:, 3, ts]), ALU.is_equal))
                        if k == 0:
                            then(nc.vector.scalar_tensor_tensor(
                                out=flat_be(pr2[:, ts]), in0=flat_be(oh[:, 0, ts]),
                                scalar=-4.0, in1=flat_be(pr[:, ts]), op0=ALU.mult, op1=ALU.add))

                dve.wait_ge(first, 80)
                def scale_h(i):
                    dve.wait_ge(h_ps, i + 1)
                    if i >= 2:
                        dve.wait_ge(c0_ps, i - 1)
                    nc.vector.scalar_tensor_tensor(
                        out=hs[:, i % 2, :].rearrange("p (t s) -> p t s", t=G),
                        in0=bank[:, i % 2, :].rearrange("p (t s) -> p t s", t=G), scalar=LORA_SCALE,
                        in1=wcol[:, i * G:(i + 1) * G].unsqueeze(2).to_broadcast([128, G, S]),
                        op0=ALU.mult, op1=ALU.mult).then_inc(hs_sb, 1)

                def statistics(i):
                    dve.wait_ge(c0_ps, i + 1)
                    if i >= 2:
                        dve.wait_ge(xh_done, i - 1)
                    nc.vector.tensor_tensor(c0[:, i % 2], bank[:, 2 + i % 2, :].rearrange("p (t d) -> p t d", t=G),
                                            rows[:, 0:1, :].to_broadcast([128, G, D]), ALU.add).then_inc(c0_sb, 1)
                    dve.wait_ge(c0_sb, i + 1)
                    for t in range(G):
                        nc.vector.bn_stats(stats[:, i % 2, t, :], c0[:, i % 2, t, :]).then_inc(st_done, 1)
                    dve.wait_ge(st_done, (i + 1) * G)
                    if i >= 2:
                        dve.wait_ge(rstd_done, i - 1)
                    for t in range(G):
                        last = nc.vector.bn_aggr(mv[:, i % 2, t, :], stats[:, i % 2, t, :])
                    then(last)
                    nc.vector.tensor_scalar_add(mv[:, i % 2, :, 1], mv[:, i % 2, :, 1], 1e-5).then_inc(mv_done, 1)

                def normalise(i):
                    dve.wait_ge(rstd_done, i + 1)
                    if i >= 2:
                        dve.wait_ge(xg_done, i - 1)
                    for t in range(G):
                        last = nc.vector.tensor_scalar(xh[:, i % 2, t, :], c0[:, i % 2, t, :], mv[:, i % 2, t, 0:1],
                                                       rstd[:, i % 2, t:t + 1], ALU.subtract, ALU.mult)
                    last.then_inc(xh_done, 1)

                scale_h(0)
                scale_h(1)
                for i in range(NG):
                    statistics(i)
                    if i + 2 < NG:
                        scale_h(i + 2)
                    if i >= 1:
                        normalise(i - 1)
                normalise(NG - 1)

                dve.wait_ge(early, 96)
                for w in range(2):
                    ts = slice(w * WT, (w + 1) * WT)
                    dve.wait_ge(lg_ps, (w + 1) * NG // 2)
                    logits = bank[:, 6 + w, w * WT * E:(w + 1) * WT * E].rearrange("p (b e) -> p b e", e=E)
                    then(nc.vector.tensor_scalar(tmp3[:, ts], logits, 10000.0, -10000.0, ALU.min, ALU.max))
                    then(nc.vector.reduce_max(col[:, 0, ts], tmp3[:, ts], X))
                    nc.vector.tensor_tensor(lg[:, ts], tmp3[:, ts], per_tile(col[:, 0, ts]), ALU.subtract).then_inc(lg_ready, 1)
                    dve.wait_ge(ex_ready, w + 1)
                    softmax_top2(ex, 1e-12, col[:, 4:6], ts)
                    nc.vector.tensor_tensor(both[:, ts], oh[:, 0, ts], oh[:, 1, ts], ALU.add).then_inc(both_ready, 1)
                    dve.wait_ge(rank_ps, w + 1)
                    rank = bank[:, 2 + w, 0:WT * E].rearrange("p (b e) -> p b e", e=E)
                    then(nc.vector.tensor_scalar(kept[:, ts], rank, float(CAP), None, ALU.is_lt))
                    then(nc.vector.tensor_tensor(slot[:, ts], rank, table[:, 2, ts], ALU.add))
                    then(nc.vector.scalar_tensor_tensor(
                        out=flat_be(tmp3[:, ts]), in0=flat_be(kept[:, ts]), scalar=-DROP,
                        in1=flat_be(slot[:, ts]), op0=ALU.mult, op1=ALU.add))
                    for k in range(2):
                        then(nc.vector.tensor_tensor(pr[:, ts], oh[:, k, ts], tmp3[:, ts], ALU.mult))
                        then(nc.vector.reduce_sum(col[:, 0, ts], pr[:, ts], X))
                        then(nc.vector.tensor_scalar_add(col[:, 0, ts], col[:, 0, ts], DROP))
                        nc.vector.tensor_copy(sidx[:, k, ts], col[:, 0, ts]).then_inc(sidx_ready, 1)
                then(nc.vector.tensor_scalar_add(pr2[:], table[:, 2], CAP - 1.0))
                then(nc.vector.tensor_tensor(tmp2[:], slot[:], pr2[:], ALU.min))
                for k in range(2):
                    then(nc.vector.tensor_tensor(pr[:], oh[:, k], tmp2[:], ALU.mult))
                    then(nc.vector.reduce_sum(col[:, 1, :], pr[:], X))
                    nc.vector.tensor_copy(g["gidx"][:, k, :], col[:, 1, :])
                    then(nc.vector.tensor_tensor(pr[:], oh[:, k], kept[:], ALU.mult))
                    then(nc.vector.reduce_sum(col[:, 2, :], pr[:], X))
                    then(nc.vector.tensor_tensor(g["gw"][:, k, :], col[:, 4 + k, :], col[:, 2, :], ALU.mult))

                then(nc.vector.reduce_max(col[:, 0, :], cond[:], X))
                nc.vector.tensor_tensor(lg[:], cond[:], per_tile(col[:, 0, :]), ALU.subtract).then_inc(lg_ready, 1)
                dve.wait_ge(ex_ready, 3)
                softmax_top2(ex, 0.0, col[:, 4:6], slice(0, B))
                then(nc.vector.tensor_tensor(col[:, 6, :], col[:, 4, :], col[:, 5, :], ALU.add))
                then(nc.vector.reciprocal(col[:, 7, :], col[:, 6, :]))
                for k in range(2):
                    then(nc.vector.tensor_tensor(col[:, 4 + k, :], col[:, 4 + k, :], col[:, 7, :], ALU.mult))
                    then(nc.vector.tensor_scalar_mul(col[:, 6, :], col[:, 4 + k, :], 1.0 - 1.0 / 12))
                    then(nc.vector.scalar_tensor_tensor(out=g["selw"][:, :, k], in0=col[:, 4 + k, :], scalar=1.0 / 12,
                                                        in1=col[:, 6, :], op0=ALU.mult, op1=ALU.add))
                    then(nc.vector.tensor_tensor(tmp[:], oh[:, k], table[:, 1], ALU.mult))
                    then(nc.vector.reduce_sum(col[:, 3, :], tmp[:], X))
                    then(nc.vector.tensor_copy(g["sel"][:, :, k], col[:, 3, :]))


def experts(nc, a, g, bank, xbuf, ybuf, sb, sem):
    from contextlib import ExitStack
    starts = (0, HALF[0])
    nchunk = tuple(h // 128 for h in HALF)
    with ExitStack() as own:
        w12 = sb("w12", [128, 2, 2 * FF], ctx=own)
        w3 = sb("w3", [128, 2, NF * D], ctx=own)
        xs = sb("xs", [128, 2, NCH, D], ctx=own)
        xsT = sb("xsT", [128, 2, CAP], ctx=own)
        sg = sb("sg", [128, 2, HALF[0]], ctx=own)
        h = sb("h", [128, 2, NF, CAP], ctx=own)
        ys = sb("ys", [128, 2, NCH, D], ctx=own)
        w_in = [sem(f"w_in{i}", own) for i in range(2)]
        x_in = [sem(f"x_in{i}", own) for i in range(2)]
        xsT_ps, xsT_sb = sem("xsT_ps", own), sem("xsT_sb", own)
        gu_ps, sg_sb, h_sb = sem("gu_ps", own), sem("sg_sb", own), sem("h_sb", own)
        y_ps = [sem(f"y_ps{i}", own) for i in range(2)]
        y_sb = [sem(f"y_sb{i}", own) for i in range(2)]
        y_out = [sem(f"y_out{i}", own) for i in range(2)]
        U = 2 * NF

        def turns(eng, step):
            for e in range(2):
                step(e, e)
            with eng.Fori(1, E // 2 - 1) as m:
                for p in range(2):
                    step(m * 2 + p, p)
            for e in range(E - 2, E):
                step(e, e % 2)

        first = lambda e: isinstance(e, int) and e < 1
        fresh = lambda e: isinstance(e, int) and e < 2

        with nc.Block() as block:
            @block.sync
            def _(sp):
                def load(e, p):
                    at = bass.ds(e, 1) if not isinstance(e, int) else slice(e, e + 1)
                    rows = bass.ds(e * CAP, CAP) if not isinstance(e, int) else slice(e * CAP, (e + 1) * CAP)
                    if not fresh(e):
                        sp.wait_ge(xsT_ps, 2 * e - 2)
                    sp.dma_start(xs[:, p, :, :], xbuf[rows, :].rearrange("(c p) d -> p c d", p=128)).then_inc(x_in[p], 16)
                    if not fresh(e):
                        sp.wait_ge(gu_ps, (e - 1) * U)
                    sp.dma_start(w12[:, p:p + 1, :], a["w12"][:, at, :]).then_inc(w_in[p], 16)
                    if not fresh(e):
                        sp.wait_ge(y_ps[1], e - 1)
                    sp.dma_start(w3[:, p:p + 1, :], a["w3"][:, at, :]).then_inc(w_in[p], 16)
                turns(sp, load)

            @block.tensor
            def _(pe):
                def transpose_x(e, p):
                    pe.wait_ge(x_in[p], ((e - p) // 2 + 1) * 16 if isinstance(e, int) else ((e - p) >> 1) * 16 + 16)
                    if not first(e):
                        pe.wait_ge(xsT_sb, 2 * e)
                    for c in range(NCH):
                        k = 0 if c < nchunk[0] else 1
                        o = c * 128 - starts[k]
                        ins = nc.tensor.transpose(bank[:, 4 + k, o:o + 128], xs[:, p, c, :], g["eye"][:])
                        if c in (nchunk[0] - 1, NCH - 1):
                            ins.then_inc(xsT_ps, 1)

                def gate_up(e, p, k, f):
                    u = k * NF + f
                    if f == 0:
                        pe.wait_ge(xsT_sb, 2 * e + k + 1)
                    if not (first(e) and u < 2):
                        pe.wait_ge(h_sb, e * U + u - 1)
                    for j in range(2):
                        ins = nc.tensor.matmul(bank[:, 2 * (u % 2) + j, 0:HALF[k]],
                                               w12[:, p, j * FF + f * 128:j * FF + (f + 1) * 128],
                                               xsT[:, p, starts[k]:starts[k] + HALF[k]], start=True, stop=True)
                    ins.then_inc(gu_ps, 1)

                def down(e, p, k, c):
                    if c == 0:
                        pe.wait_ge(h_sb, e * U + (k + 1) * NF)
                        if not first(e):
                            pe.wait_ge(y_sb[k], e)
                    at = starts[k] + c * 128
                    for f in range(NF):
                        ins = nc.tensor.matmul(bank[:, 6 + k, c * D:(c + 1) * D], h[:, p, f, at:at + 128],
                                               w3[:, p, f * D:(f + 1) * D], start=(f == 0), stop=(f == NF - 1))
                    if c == nchunk[k] - 1:
                        ins.then_inc(y_ps[k], 1)

                def step(e, p):
                    pe.wait_ge(w_in[p], ((e - p) // 2 + 1) * 32 if isinstance(e, int) else ((e - p) >> 1) * 32 + 32)
                    for f in range(NF):
                        gate_up(e, p, 0, f)
                        if f < nchunk[1] and not first(e):
                            down(e - 1, 1 - p, 1, f)
                    for f in range(NF):
                        gate_up(e, p, 1, f)
                        if f == 0 and not (isinstance(e, int) and e == E - 1):
                            transpose_x(e + 1, 1 - p)
                        if f < nchunk[0]:
                            down(e, p, 0, f)

                transpose_x(0, 0)
                turns(pe, step)
                for c in range(nchunk[1]):
                    down(E - 1, (E - 1) % 2, 1, c)

            @block.scalar
            def _(act):
                def step(e, p):
                    for k in range(2):
                        for f in range(NF):
                            u = k * NF + f
                            act.wait_ge(gu_ps, e * U + u + 1)
                            if not (first(e) and u < 2):
                                act.wait_ge(h_sb, e * U + u - 1)
                            nc.scalar.activation(sg[:, u % 2, 0:HALF[k]], bank[:, 2 * (u % 2), 0:HALF[k]],
                                                 ACT.Silu).then_inc(sg_sb, 1)
                            if u == 1 and not first(e):
                                store(e - 1, 1 - p, 0)
                            if u == NF and not first(e):
                                store(e - 1, 1 - p, 1)

                def store(e, p, k):
                    act.wait_ge(y_ps[k], e + 1)
                    if not fresh(e):
                        act.wait_ge(y_out[p], ((e - p) // 2) * 32 if isinstance(e, int) else ((e - p) >> 1) * 32)
                    c0 = starts[k] // 128
                    nc.scalar.copy(ys[:, p, c0:c0 + nchunk[k], :],
                                   bank[:, 6 + k, 0:nchunk[k] * D].rearrange("p (c d) -> p c d", d=D)).then_inc(y_sb[k], 1)
                    act.wait_ge(y_sb[k], e + 1)
                    rows = bass.ds(e * CAP + starts[k], HALF[k]) if not isinstance(e, int) else \
                        slice(e * CAP + starts[k], e * CAP + starts[k] + HALF[k])
                    act.dma_start(ybuf[rows, :].rearrange("(c p) d -> p c d", p=128),
                                  ys[:, p, c0:c0 + nchunk[k], :]).then_inc(y_out[p], 16)

                turns(act, step)
                for k in range(2):
                    store(E - 1, (E - 1) % 2, k)
                for p in range(2):
                    act.wait_ge(y_out[p], E // 2 * 32)

            @block.vector
            def _(dve):
                def transposed(e, p, k):
                    dve.wait_ge(xsT_ps, 2 * e + k + 1)
                    if not fresh(e):
                        dve.wait_ge(gu_ps, (e - 1) * U)
                    nc.vector.tensor_copy(xsT[:, p, starts[k]:starts[k] + HALF[k]],
                                          bank[:, 4 + k, 0:HALF[k]]).then_inc(xsT_sb, 1)

                def step(e, p):
                    for k in range(2):
                        for f in range(NF):
                            u = k * NF + f
                            dve.wait_ge(sg_sb, e * U + u + 1)
                            if not fresh(e) and f == 0:
                                dve.wait_ge(y_ps[k], e - 1)
                            nc.vector.tensor_tensor(h[:, p, f, starts[k]:starts[k] + HALF[k]],
                                                    sg[:, u % 2, 0:HALF[k]], bank[:, 2 * (u % 2) + 1, 0:HALF[k]],
                                                    ALU.mult).then_inc(h_sb, 1)
                            if u in (NF + 1, NF + 2) and not (isinstance(e, int) and e == E - 1):
                                transposed(e + 1, 1 - p, u - NF - 1)

                transposed(0, 0, 0)
                transposed(0, 0, 1)
                turns(dve, step)


def shifted_out(g, nc, tile, ps):
    flat = lambda ap: ap.rearrange("p a s -> p (a s)")
    nc.scalar.copy(flat(g["cT"][0:64, tile, :]), ps[0:64, :])
    return nc.scalar.copy(flat(g["cT"][64:128, tile, 1:S]), ps[64:128, 0:S - 1])


def sequence_experts(nc, g, bank, ybuf, own, sb, sem):
    U = 3
    gy = sb("gy", [128, B, 2, D], ctx=own)
    xa = sb("xa", [128, 2, D], ctx=own)
    x1 = sb("x1", [128, 2, D], ctx=own)
    x1Ts = sb("x1Ts", [128, 2, S], ctx=own)
    ge = sb("ge", [128, 2, FF], ctx=own)
    h = sb("hseq", [128, 2, FF], ctx=own)
    hT = sb("hTseq", [128, 2, FF], ctx=own)
    cs = sb("cs", [128, 2, D], ctx=own)
    gsem = [sem(f"gather{i}", own) for i in range(4)]
    gathered, xa_sb, x1_sb = sem("gathered", own), sem("xa_sb", own), sem("x1_sb", own)
    x1T_ps, x1T_sb, x1_kept = sem("x1T_ps", own), sem("x1T_sb", own), sem("x1_kept", own)
    gu_ps, ge_sb, h_sb = sem("gus_ps", own), sem("ge_sb", own), sem("hs_sb2", own)
    hT_ps, hT_sb, down_done = sem("hTs_ps", own), sem("hTs_sb", own), sem("down_done", own)
    cs_sb, cT_ps = sem("cs_sb", own), sem("cTs_ps", own)
    ctok_sb, cT_sb = g["ctok_ready"], g["cT_ready"]

    def turns(eng, step):
        for k in range(4):
            step(k, k % 2)
        with eng.Fori(2, B // 2 - 1) as m:
            for p in range(2):
                step(m * 2 + p, p)
        for k in range(B - 2, B + 1):
            step(k, k % 2)

    def wait(eng, semaphore, value):
        if not isinstance(value, int) or value > 0:
            eng.wait_ge(semaphore, value)

    def within(k, first, last):
        return not isinstance(k, int) or first <= k <= last

    at = lambda k: slice(k, k + 1) if isinstance(k, int) else bass.ds(k, 1)

    with nc.Block() as block:
        @block.gpsimd
        def _(pool):
            def keep(b):
                pool.wait_ge(x1_sb, b + 1)
                nc.gpsimd.tensor_copy(g["x1"][:, b, :], x1[:, b % 2, :]).then_inc(x1_kept, 1)

            def keep_c(b):
                pool.wait_ge(cs_sb, b + 1)
                nc.gpsimd.tensor_copy(g["ctok"][:, b, :], cs[:, b % 2, :]).then_inc(ctok_sb, 1)

            for b in range(B + 5):
                if b < B:
                    for k in range(2):
                        nc.gpsimd.indirect_dma_start(
                            gy[:, b, k, :], None, ybuf,
                            bass.IndirectOffsetOnAxis(ap=g["gidx"][:, k, b:b + 1], axis=0),
                            bounds_check=NSLOT - 1, oob_is_err=False).then_inc(gsem[b % 4], 16)
                if 1 <= b <= B:
                    pool.wait_ge(gsem[(b - 1) % 4], ((b - 1) // 4 + 1) * 32)
                    pool.sem_inc(gathered, 1)
                if 2 <= b < B + 2:
                    keep(b - 2)
                if b >= 5:
                    keep_c(b - 5)

        @block.vector
        def _(dve):
            def add_experts(k, q):
                dve.wait_ge(gathered, k + 1)
                wait(dve, x1T_ps, k - 1)
                wait(dve, x1_kept, k - 1)
                for j, (src, dst, done) in enumerate(((g["xtok"][:, at(k), :], xa[:, q:q + 1, :], xa_sb),
                                                      (xa[:, q:q + 1, :], x1[:, q:q + 1, :], x1_sb))):
                    if j:
                        dve.wait_ge(xa_sb, k + 1)
                    nc.vector.scalar_tensor_tensor(
                        out=dst.rearrange("p a d -> p (a d)"), in0=gy[:, at(k), j, :].rearrange("p a d -> p (a d)"),
                        scalar=g["gw"][:, j, at(k)], in1=src.rearrange("p a d -> p (a d)"),
                        op0=ALU.mult, op1=ALU.add).then_inc(done, 1)

            def step(k, p):
                for u in range(U):
                    j, r = k * U + u, (p * U + u) % 2
                    if within(k, 0, B - 1):
                        dve.wait_ge(ge_sb, j + 1)
                        wait(dve, hT_ps, j - 1)
                        if u < 2:
                            nc.vector.scalar_tensor_tensor(
                                out=h[:, r, :], in0=ge[:, r, :],
                                scalar=g["selw"][:, at(k), u:u + 1].rearrange("p a b -> p (a b)"),
                                in1=bank[:, 2 * r + 1, :], op0=ALU.mult, op1=ALU.mult).then_inc(h_sb, 1)
                        else:
                            nc.vector.tensor_tensor(h[:, r, :], ge[:, r, :], bank[:, 2 * r + 1, :],
                                                    ALU.mult).then_inc(h_sb, 1)
                    if u == 0 and within(k, 0, B - 3):
                        add_experts(k + 2, p)
                    if u == 1 and within(k, 1, B):
                        dve.wait_ge(down_done, U * k)
                        wait(dve, ctok_sb, k - 2)
                        wait(dve, cT_ps, k - 2)
                        nc.vector.tensor_copy(cs[:, 1 - p, :], bank[:, 6, 0:D]).then_inc(cs_sb, 1)

            add_experts(0, 0)
            add_experts(1, 1)
            turns(dve, step)

        @block.scalar
        def _(act):
            def keep_x1T(k, q):
                act.wait_ge(x1T_ps, k + 1)
                wait(act, gu_ps, (k - 1) * U)
                nc.scalar.copy(x1Ts[:, q, :], bank[:, 7, 0:S]).then_inc(x1T_sb, 1)

            def step(k, p):
                for u in range(U):
                    j, r = k * U + u, (p * U + u) % 2
                    if within(k, 0, B - 1):
                        act.wait_ge(gu_ps, j + 1)
                        wait(act, h_sb, j - 1)
                        nc.scalar.activation(ge[:, r, :], bank[:, 2 * r, :], ACT.Gelu_apprx_tanh).then_inc(ge_sb, 1)
                    if (not isinstance(k, int)) or 1 <= j <= U * B:
                        act.wait_ge(hT_ps, j)
                        wait(act, down_done, j - 2)
                        nc.scalar.copy(hT[:, 1 - r, :], bank[:, 5 - r, :]).then_inc(hT_sb, 1)
                    if u == 0 and within(k, 0, B - 2):
                        keep_x1T(k + 1, 1 - p)
                    if u == 2 and within(k, 1, B):
                        act.wait_ge(cT_ps, k)
                        shifted_out(g, nc, at(k - 1), bank[:, 7, S:2 * S]).then_inc(cT_sb, 1)

            keep_x1T(0, 0)
            turns(act, step)

        @block.tensor
        def _(pe):
            chosen_before = {}
            flat = lambda t: t[:].rearrange("p e f -> p (e f)")
            first = lambda e, n, off=0: slice(e + off, e + off + n) if isinstance(e, int) else bass.ds(e + off, n)

            def chosen(k, u):
                return pe.value_load(g["sel"][0:1, at(k), u:u + 1].rearrange("p a b -> p (a b)"), min_val=0,
                                     max_val=(E - 1) * FF)

            def turn_x1(k, q):
                pe.wait_ge(x1_sb, k + 1)
                wait(pe, x1T_sb, k)
                wait(pe, cT_sb, k - 2)
                nc.tensor.transpose(bank[:, 7, 0:S], x1[:, q, :], g["eye"][:]).then_inc(x1T_ps, 1)

            def step(k, p):
                for u in range(U):
                    j, r = k * U + u, (p * U + u) % 2
                    if within(k, 0, B - 1):
                        e = E * FF if u == 2 else chosen(k, u)
                        if u == 1:
                            e_second = e
                        if u == 0:
                            e_first = e
                            pe.wait_ge(x1T_sb, k + 1)
                        wait(pe, h_sb, j - 1)
                        for i, w in enumerate((g["wg"], g["wu"])):
                            ins = nc.tensor.matmul(bank[:, 2 * r + i, :], x1Ts[:, p, :], flat(w)[:, first(e, FF)],
                                                   start=True, stop=True)
                        ins.then_inc(gu_ps, 1)
                    if (not isinstance(k, int)) or 1 <= j <= U * B:
                        pe.wait_ge(h_sb, j)
                        wait(pe, hT_sb, j - 2)
                        for f in range(NF):
                            ins = nc.tensor.transpose(bank[:, 5 - r, f * 128:(f + 1) * 128],
                                                      h[:, 1 - r, f * 128:(f + 1) * 128], g["eye"][:])
                        ins.then_inc(hT_ps, 1)
                    if (not isinstance(k, int)) or 2 <= j <= U * B + 1:
                        if u == 0:
                            reload = k == B - 2 if isinstance(k, int) else p == 0
                            e = chosen(k - 1, 1) if reload else chosen_before["e"]
                        elif u == 1:
                            e = E * FF
                        else:
                            e = e_first
                            wait(pe, cs_sb, k)
                        pe.wait_ge(hT_sb, j - 1)
                        for f in range(NF):
                            ins = nc.tensor.matmul(bank[:, 6, 0:D], hT[:, r, f * 128:(f + 1) * 128],
                                                   flat(g["wd"])[:, first(e, D, f * D)],
                                                   start=(u == 2 and f == 0), stop=(u == 1 and f == NF - 1))
                        ins.then_inc(down_done, 1)
                    if u == 0 and within(k, 0, B - 2):
                        turn_x1(k + 1, 1 - p)
                    if u == 2 and within(k, 1, B):
                        pe.wait_ge(cs_sb, k)
                        pe.wait_ge(x1T_sb, min(k + 2, B) if isinstance(k, int) else k + 2)
                        wait(pe, cT_sb, k - 1)
                        nc.tensor.transpose(bank[:, 7, S:2 * S], cs[:, 1 - p, :], g["eye"][:]).then_inc(cT_ps, 1)
                if within(k, 0, B - 1):
                    chosen_before["e"] = e_second

            turn_x1(0, 0)
            pe.wait_ge(g["late"], N_LATE)
            turns(pe, step)


def transformer(nc, g, bank, out_dram, own, sb, sem):
    hT = sb("hT", [128, 2, S], ctx=own)
    sq = sb("sq", [128, 2 * INNER], ctx=own)
    ss = sb("ss", [128, 2, 16], ctx=own)
    rn = sb("rn", [128, 2, 16], ctx=own)
    t1 = sb("t1", [128, 2 * INNER], ctx=own)
    t2 = sb("t2", [128, 2 * INNER], ctx=own)
    kn = sb("kn", [128, INNER], ctx=own)
    qk = sb("qk", [128, 2, 2 * INNER], ctx=own)
    qkT = sb("qkT", [128, 2, 8, S], ctx=own)
    v = sb("v", [128, 2, INNER], ctx=own)
    mx = sb("mx", [128, HEADS], ctx=own)
    nb = sb("nb", [128, 2, HEADS], ctx=own)
    pa = sb("pa", [128, 2, 4, S], ctx=own)
    ls = sb("ls", [128, 2, HEADS], ctx=own)
    rl = sb("rl", [128, HEADS], ctx=own)
    pT = sb("pT", [128, 2, 4, S], ctx=own)
    oT = sb("oT", [128, INNER], ctx=own)
    c1 = sb("c1", [128, 2, 4, DH], ctx=own)
    c1b = sb("c1b", [128, 8, D], ctx=own)
    hs = sb("hs3", [128, D], ctx=own)
    stats = sb("stats2", [128, 6], ctx=own)
    mv = sb("mv2", [128, 2], ctx=own)
    ve = sb("ve", [128, 1], ctx=own)
    rstd = sb("rstd2", [128, 1], ctx=own)
    xh = sb("xh2", [128, D], ctx=own)
    xhT = sb("xhT", [128, S], ctx=own)
    ag = sb("ag", [128, 2, 2, HID], ctx=own)
    gl = sb("gl", [128, 2, HID], ctx=own)
    hh = sb("hh", [128, 2, HID], ctx=own)
    hhT = sb("hhT", [128, 3, S], ctx=own)
    c2 = sb("c2", [128, 2, D], ctx=own)
    hT_sb, qk_ps, v_ps, v_sb, sq_sb = (sem("d_" + n, own) for n in ("hT_sb", "qk_ps", "v_ps", "v_sb", "sq_sb"))
    ss0_sb, ss_sb, rnk_sb, rnq_sb = (sem("d_" + n, own) for n in ("ss0_sb", "ss_sb", "rnk_sb", "rnq_sb"))
    t_sb, add_sb, kn_sb = (sem("d_" + n, own) for n in ("t_sb", "add_sb", "kn_sb"))
    qT_ps, kT_ps, qT_sb, kT_sb = (sem("d_" + n, own) for n in ("qT_ps", "kT_ps", "qT_sb", "kT_sb"))
    s_ps, mx_sb, nb_sb, p_sb = (sem("d_" + n, own) for n in ("s_ps", "mx_sb", "nb_sb", "p_sb"))
    rl_sb, pn_sb = (sem("d_" + n, own) for n in ("rl_sb", "pn_sb"))
    pT_ps, pT_sb, o_ps, oT_sb = (sem("d_" + n, own) for n in ("pT_ps", "pT_sb", "o_ps", "oT_sb"))
    wo_ps, c1_sb, c1b_sb, h_ps, h_sb = (sem("d_" + n, own) for n in ("wo_ps", "c1_sb", "c1b_sb", "h_ps", "h_sb"))
    st_sb, mv_sb, ve_sb, rstd_sb, xh_sb = (sem("d_" + n, own) for n in ("st_sb", "mv_sb", "ve_sb", "rstd_sb", "xh_sb"))
    xhT_ps, xhT_sb, w1_ps, ag_sb = (sem("d_" + n, own) for n in ("xhT_ps", "xhT_sb", "w1_ps", "ag_sb"))
    gl_sb, hh_sb, hhT_ps, hhT_sb = (sem("d_" + n, own) for n in ("gl_sb", "hh_sb", "hhT_ps", "hhT_sb"))
    w2_ps, c2_sb, cT_ps = (sem("d_" + n, own) for n in ("w2_ps", "c2_sb", "cT_ps"))
    c1z_sb, res_sb, stored = sem("d_c1z_sb", own), sem("d_res_sb", own), sem("d_stored", own)
    cT_ready, ctok_ready = g["cT_ready"], g["ctok_ready"]
    LAG = 7
    FIRST = 10
    RESULTS = {NV + 3: (0, 4), NV + 4: (4, 12), NV + 5: (12, B - 1)}
    Q, K, VB, TA, TB, OB = 0, 1, 2, 5, 6, 7
    SB = (3, 4)

    def turns(eng, step):
        for n in range(FIRST):
            step(n, n % 2)
        with eng.Fori(FIRST // 2, NV // 2) as m:
            for p in range(2):
                step(m * 2 + p, p)
        for n in range(NV, NV + LAG + 1):
            step(n, n % 2)

    def lagged(n, p, lag):
        if isinstance(n, int):
            return n - lag, (n - lag) % 2, 0 <= n - lag < NV
        return n - lag, (p - lag) % 2, True

    def wait(eng, semaphore, value, most=None):
        if isinstance(value, int):
            if most is not None:
                value = min(value, most)
            if value <= 0:
                return
        eng.wait_ge(semaphore, value)

    def edge(eng, semaphore, value, most=None):
        if isinstance(value, int):
            wait(eng, semaphore, value, most)

    at = lambda k: slice(k, k + 1) if isinstance(k, int) else bass.ds(k, 1)
    ring = lambda k: slice(k % 8, k % 8 + 1) if isinstance(k, int) else bass.ds(k & 7, 1)
    layer = lambda k: at(k // B) if isinstance(k, int) else \
        bass.ds(nc.s_assert_within(k >> 4, 0, DEPTH - 1, skip_runtime_bounds_check_because="k is below DEPTH * B"), 1)
    flat = lambda ap: ap.rearrange("p a d -> p (a d)")
    heads = lambda ap: ap.rearrange("p (h d) -> p h d", d=DH)
    halves = lambda ap: ap.rearrange("p (w d) -> p w d", w=2)

    with nc.Block() as block:
        @block.tensor
        def _(pe):
            def turn(dst, src, blocks, ready):
                for b in range(blocks):
                    ins = nc.tensor.transpose(bank[:, dst, b * 128:(b + 1) * 128], src(b), g["eye"][:])
                ins.then_inc(ready, 1)

            def step(n, p):
                k, q, there = lagged(n, p, 1)
                if there:
                    pe.wait_ge(hT_sb, k + 1)
                    wait(pe, h_sb, k - 2)
                    edge(pe, v_sb, k)
                    nc.tensor.matmul(bank[:, VB, :], hT[:, q, :], flat(g["wqkv"][:, layer(k), 2 * INNER:]), start=True,
                                     stop=True).then_inc(v_ps, 1)
                    pe.wait_ge(add_sb, 2 * k + 2)
                    wait(pe, xhT_sb, k - 3)
                    edge(pe, pT_sb, 2 * k - 3)
                    edge(pe, qT_sb, k)
                    turn(TA, lambda b: qk[:, q, b * 128:(b + 1) * 128], 4, qT_ps)
                    pe.wait_ge(kn_sb, k + 1)
                    wait(pe, c2_sb, k - 5)
                    edge(pe, hhT_sb, k - 5)
                    edge(pe, pT_sb, 2 * k - 2)
                    edge(pe, kT_sb, k)
                    turn(TB, lambda b: qk[:, q, INNER + b * 128:INNER + (b + 1) * 128], 4, kT_ps)
                k, q, there = lagged(n, p, 0)
                if there:
                    pe.wait_ge(hT_sb, k + 1)
                    wait(pe, ag_sb, k - 4)
                    edge(pe, t_sb, 3 * k)
                    nc.tensor.matmul(bank[:, Q, :], hT[:, q, :], flat(g["wqkv"][:, layer(k), 0:INNER]), start=True,
                                     stop=True)
                    nc.tensor.matmul(bank[:, K, :], hT[:, q, :], flat(g["wqkv"][:, layer(k), INNER:2 * INNER]),
                                     start=True, stop=True).then_inc(qk_ps, 1)
                k, q, there = lagged(n, p, 7)
                if there:
                    pe.wait_ge(c2_sb, k + 1)
                    wait(pe, c1_sb, k + 5, NV)
                    edge(pe, cT_ready, B + k)
                    turn(OB, lambda b: c2[:, q, :], 1, cT_ps)
                k, q, there = lagged(n, p, 2)
                if there:
                    for par in range(2):
                        pe.wait_ge(pn_sb, 2 * k + par + 1)
                        wait(pe, (qT_sb, kT_sb)[par], k + 2, NV)
                        edge(pe, (xhT_sb, c2_sb)[par], (k - 2, k - 4)[par])
                        turn((TA, TB)[par], lambda b: pa[:, par, b, :], 4, pT_ps)
                k, q, there = lagged(n, p, 1)
                if there:
                    pe.wait_ge(qT_sb, k + 1)
                    pe.wait_ge(kT_sb, k + 1)
                    wait(pe, p_sb, 2 * k)
                    for par in range(2):
                        nc.tensor.matmul(bank[:, SB[par], :], g["eye16"][:],
                                         g["mask"][:].unsqueeze(1).to_broadcast([128, 4, 128]), start=True, stop=False)
                    for b in range(4):
                        for par in range(2):
                            rows = slice(64 * par, 64 * par + 64)
                            ins = nc.tensor.matmul(bank[:, SB[par], b * S:(b + 1) * S], qkT[rows, q, b, :],
                                                   qkT[rows, q, 4 + b, :], start=False, stop=(b == 3))
                    ins.then_inc(s_ps, 1)
                k, q, there = lagged(n, p, 3)
                if there:
                    pe.wait_ge(c1_sb, k + 1)
                    wait(pe, v_sb, k + 3, NV)
                    edge(pe, h_sb, k)
                    nc.tensor.matmul(bank[:, VB, 0:D], g["eye"][:], c1[:, q, 0:2, :], start=True, stop=False)
                    nc.tensor.matmul(bank[:, VB, 0:D], g["shift"][:], c1[:, q, 2:4, :], start=False,
                                     stop=True).then_inc(h_ps, 1)
                k, q, there = lagged(n, p, 4)
                if there:
                    pe.wait_ge(xh_sb, k + 1)
                    wait(pe, pT_sb, 2 * k + 5, 2 * NV)
                    turn(TA, lambda b: xh[:], 1, xhT_ps)
                k, q, there = lagged(n, p, 6)
                if there:
                    pe.wait_ge(hh_sb, k + 1)
                    wait(pe, pT_sb, 2 * k + 10, 2 * NV)
                    edge(pe, c2_sb, k)
                    for b, (c, w) in enumerate(HCH):
                        ins = nc.tensor.transpose(bank[0:w, TB, b * 128:(b + 1) * 128], hh[:, q, c:c + w], g["eye"][:])
                    ins.then_inc(hhT_ps, 1)
                k, q, there = lagged(n, p, 2)
                if there:
                    pe.wait_ge(v_sb, k + 1)
                    pe.wait_ge(pT_sb, 2 * k + 2)
                    if not (isinstance(k, int) and k < 5):
                        wait(pe, cT_ready, B + k - 4)
                    edge(pe, c1_sb, k)
                    for b in range(4):
                        for par in range(2):
                            h = 2 * b + par
                            ins = nc.tensor.matmul(bank[64 * par:64 * par + 64, OB, b * S:(b + 1) * S],
                                                   v[:, q, h * DH:(h + 1) * DH], pT[:, par, b, :], start=True, stop=True)
                    ins.then_inc(o_ps, 1)
                k, q, there = lagged(n, p, 4)
                if there:
                    pe.wait_ge(xhT_sb, k + 1)
                    wait(pe, t_sb, 3 * k + 15, 3 * NV)
                    edge(pe, ag_sb, k)
                    for j in range(2):
                        ins = nc.tensor.matmul(bank[:, (Q, K)[j], 0:HID], xhT[:],
                                               flat(g["w1"][:, layer(k), j * HID:(j + 1) * HID]), start=True, stop=True)
                    ins.then_inc(w1_ps, 1)
                k, q, there = lagged(n, p, 6)
                if there:
                    pe.wait_ge(hhT_sb, k + 1)
                    for b, (c, w) in enumerate(HCH):
                        ins = nc.tensor.matmul(bank[:, TB, 0:D], hhT[0:w, b, :],
                                               flat(g["w2"][0:w, layer(k), b * D:(b + 1) * D]), start=(b == 0), stop=(b == 2))
                    ins.then_inc(w2_ps, 1)
                k, q, there = lagged(n, p, 2)
                if there:
                    pe.wait_ge(oT_sb, k + 1)
                    for b in range(4):
                        ins = nc.tensor.matmul(bank[:, OB, 0:D], oT[:, b * 128:(b + 1) * 128],
                                               flat(g["wo"][:, layer(k), b * D:(b + 1) * D]), start=(b == 0), stop=(b == 3))
                    ins.then_inc(wo_ps, 1)

            pe.wait_ge(c1z_sb, 1)
            turns(pe, step)

        @block.scalar
        def _(act):
            def step(n, p):
                k, q, there = lagged(n, p, 0)
                if there:
                    act.wait_ge(qk_ps, k + 1)
                    wait(act, ss0_sb, k)
                    nc.scalar.activation(sq[:], bank[:, Q:K + 1, :].rearrange("p a d -> p (a d)"),
                                         ACT.Square).then_inc(sq_sb, 1)
                k, q, there = lagged(n, p, 1)
                if there:
                    act.wait_ge(v_ps, k + 1)
                    wait(act, o_ps, k - 1)
                    nc.scalar.copy(v[:, q, :], bank[:, VB, :]).then_inc(v_sb, 1)
                k, q, there = lagged(n, p, 7)
                if there:
                    act.wait_ge(cT_ps, k + 1)
                    shifted_out(g, nc, at(k + B), bank[:, OB, 0:S]).then_inc(cT_ready, 1)
                k, q, there = lagged(n, p, 2)
                if there:
                    for par in range(2):
                        act.wait_ge(pT_ps, 2 * k + par + 1)
                        wait(act, o_ps, k)
                        nc.scalar.copy(pT[:, par].rearrange("p a s -> p (a s)"),
                                       bank[:, (TA, TB)[par], :]).then_inc(pT_sb, 1)
                k, q, there = lagged(n, p, 3)
                if there:
                    act.wait_ge(h_ps, k + 1)
                    wait(act, xh_sb, k)
                    nc.scalar.copy(hs[:], bank[:, VB, 0:D]).then_inc(h_sb, 1)
                k, q, there = lagged(n, p, 4)
                if there:
                    act.wait_ge(xhT_ps, k + 1)
                    wait(act, w1_ps, k)
                    l = layer(k)
                    nc.scalar.activation(xhT[:], bank[:, TA, 0:S], ACT.Identity, scale=flat(g["lngb"][:, l, 0:1]),
                                         bias=flat(g["lngb"][:, l, 1:2])).then_inc(xhT_sb, 1)
                k, q, there = lagged(n, p, 6)
                if there:
                    act.wait_ge(hhT_ps, k + 1)
                    wait(act, w2_ps, k)
                    w = HCH[2][1]
                    nc.scalar.copy(hhT[:, 0:2, :], bank[:, TB, 0:2 * S].rearrange("p (a s) -> p a s", a=2))
                    nc.scalar.copy(hhT[0:w, 2, :], bank[0:w, TB, 2 * S:3 * S]).then_inc(hhT_sb, 1)
                k, q, there = lagged(n, p, 2)
                if there:
                    act.wait_ge(o_ps, k + 1)
                    wait(act, wo_ps, k)
                    nc.scalar.copy(oT[:], bank[:, OB, :]).then_inc(oT_sb, 1)
                k, q, there = lagged(n, p, 1)
                if there:
                    act.wait_ge(nb_sb, k + 1)
                    wait(act, rl_sb, 2 * k - 2)
                    for par in range(2):
                        wait(act, pT_ps, 2 * k - 1 + par)
                        for b in range(4):
                            h = 2 * b + par
                            ins = nc.scalar.activation(pa[:, par, b, :], bank[:, SB[par], b * S:(b + 1) * S], ACT.Exp,
                                                       bias=nb[:, q, h:h + 1], scale=rn[:, q, h:h + 1],
                                                       accum_out=ls[:, q, h:h + 1])
                        ins.then_inc(p_sb, 1)
                if p == 1:
                    for lag in (5, 4):
                        k, q, there = lagged(n, p, lag)
                        if there:
                            act.wait_ge(ag_sb, k + 1)
                            wait(act, hh_sb, k - 1)
                            nc.scalar.activation(gl[:, q, :], ag[:, q, 1, :], ACT.Gelu).then_inc(gl_sb, 1)

            turns(act, step)

        @block.vector
        def _(dve):
            def step(n, p):
                k, q, there = lagged(n, p, 1)
                if there:
                    for dst, src, ready, done in ((0, TA, qT_ps, qT_sb), (4, TB, kT_ps, kT_sb)):
                        dve.wait_ge(ready, k + 1)
                        wait(dve, s_ps, k - 1)
                        nc.vector.tensor_copy(qkT[:, q, dst:dst + 4, :],
                                              bank[:, src, :].rearrange("p (b s) -> p b s", b=4)).then_inc(done, 1)
                k, q, there = lagged(n, p, 2)
                if there:
                    half = lambda t, par: t.rearrange("p (b w) -> p w b", w=2)[:, par]
                    for par in range(2):
                        dve.wait_ge(p_sb, 2 * k + par + 1)
                        nc.vector.reciprocal(half(rl[:], par), half(ls[:, q, :], par)).then_inc(rl_sb, 1)
                        dve.wait_ge(rl_sb, 2 * k + par + 1)
                        nc.vector.tensor_tensor(pa[:, par], pa[:, par],
                                                half(rl[:], par).unsqueeze(2).to_broadcast([128, 4, S]),
                                                ALU.mult).then_inc(pn_sb, 1)
                k, q, there = lagged(n, p, 4)
                if there:
                    dve.wait_ge(rstd_sb, k + 1)
                    wait(dve, xhT_ps, k)
                    nc.vector.tensor_scalar(xh[:], hs[:], mv[:, 0:1], rstd[:], ALU.subtract, ALU.mult).then_inc(xh_sb, 1)
                k, q, there = lagged(n, p, 0)
                if there:
                    dve.wait_ge(sq_sb, k + 1)
                    wait(dve, rnq_sb, k - 1)
                    nc.vector.reduce_sum(ss[:, q, :], heads(sq[:]), X).then_inc(ss0_sb, 1)
                    dve.wait_ge(ss0_sb, k + 1)
                    nc.vector.tensor_scalar_max(ss[:, q, :], ss[:, q, :], 1e-24).then_inc(ss_sb, 1)
                    wait(dve, add_sb, 2 * k)
                    l = layer(k)
                    src = bank[:, Q:K + 1, :].rearrange("p w (h d) -> p w h d", d=DH)
                    both = lambda t: t[:].rearrange("p (w h d) -> p w h d", w=2, d=DH)
                    table = lambda j, lo, hi: g["rot"][:, j, l, :].rearrange(
                        "p a (w d) -> p (a w) d", w=2)[:, :, lo:hi].unsqueeze(2).to_broadcast([128, 2, HEADS, hi - lo])
                    nc.vector.tensor_tensor(both(t1), src, table(0, 0, DH), ALU.mult).then_inc(t_sb, 1)
                    for lo, hi, fl in ((0, 32, 32), (32, 64, 0)):
                        nc.vector.tensor_tensor(both(t2)[:, :, :, lo:hi], src[:, :, :, fl:fl + 32], table(1, lo, hi),
                                                ALU.mult).then_inc(t_sb, 1)
                k, q, there = lagged(n, p, 1)
                if there:
                    dve.wait_ge(s_ps, k + 1)
                    for par in range(2):
                        nc.vector.reduce_max(mx[:].rearrange("p (b w) -> p w b", w=2)[:, par],
                                             bank[:, SB[par], :].rearrange("p (b s) -> p b s", b=4), X).then_inc(mx_sb, 1)
                    dve.wait_ge(mx_sb, 2 * k + 2)
                    dve.wait_ge(rnq_sb, k + 1)
                    wait(dve, p_sb, 2 * k - 2)
                    nc.vector.scalar_tensor_tensor(out=nb[:, q, :], in0=mx[:], scalar=-1.0, in1=rn[:, q, 0:8],
                                                   op0=ALU.mult, op1=ALU.mult).then_inc(nb_sb, 1)
                k3, _, there3 = lagged(n, p, 3)
                if there3:
                    dve.wait_ge(h_sb, k3 + 1)
                    nc.vector.bn_stats(stats[:], hs[:]).then_inc(st_sb, 1)
                    dve.wait_ge(st_sb, k3 + 1)
                k, q, there = lagged(n, p, 4)
                if there:
                    dve.wait_ge(w1_ps, k + 1)
                    wait(dve, hh_sb, k - 1)
                    nc.vector.tensor_tensor(ag[:, q], bank[:, Q:K + 1, 0:HID],
                                            g["b1"][:, layer(k), :].rearrange("p a (w c) -> p (a w) c", w=2),
                                            ALU.add).then_inc(ag_sb, 1)
                if there3:
                    nc.vector.bn_aggr(mv[:], stats[:]).then_inc(mv_sb, 1)
                    dve.wait_ge(mv_sb, k3 + 1)
                    wait(dve, rstd_sb, k3)
                    nc.vector.tensor_scalar_add(ve[:], mv[:, 1:2], 1e-5).then_inc(ve_sb, 1)
                k, q, there = lagged(n, p, 2)
                if there:
                    dve.wait_ge(wo_ps, k + 1)
                    dve.wait_ge(ctok_ready, k + 1)
                    wait(dve, h_ps, k - 1)
                    wait(dve, c1b_sb, k - 1)
                    nc.vector.tensor_tensor(c1[:, q, 0:4:3, :], halves(bank[:, OB, 0:D]), halves(flat(g["ctok"][:, at(k), :])),
                                            ALU.add).then_inc(c1_sb, 1)
                k, q, there = lagged(n, p, 6)
                if there:
                    dve.wait_ge(w2_ps, k + 1)
                    dve.wait_ge(c1b_sb, k + 1)
                    wait(dve, cT_ps, k - 1)
                    if not (isinstance(k, int) and k < 2):
                        wait(dve, ctok_ready, B + k - 1)
                    nc.vector.tensor_tensor(c2[:, q, :], bank[:, TB, 0:D], flat(c1b[:, ring(k), :]),
                                            ALU.add).then_inc(c2_sb, 1)
                if isinstance(n, int) and n in RESULTS:
                    lo, hi = RESULTS[n]
                    dve.wait_ge(ctok_ready, 2 * B + hi)
                    nc.vector.tensor_tensor(g["x1"][:, lo:hi, :], g["x1"][:, lo:hi, :],
                                            g["ctok"][:, 2 * B + lo:2 * B + hi, :], ALU.add).then_inc(res_sb, 1)

            turns(dve, step)
            dve.wait_ge(c2_sb, NV)
            nc.vector.tensor_tensor(g["x1"][:, B - 1, :], g["x1"][:, B - 1, :], c2[:, (NV - 1) % 2, :],
                                    ALU.add).then_inc(res_sb, 1)

        @block.gpsimd
        def _(pool):
            def take_input(k, q):
                pool.wait_ge(cT_ready, k + 1)
                wait(pool, v_ps, k - 1)
                nc.gpsimd.tensor_copy(hT[:, q, :], flat(g["cT"][:, at(k), :])).then_inc(hT_sb, 1)

            def step(n, p):
                k, q, there = lagged(n, p, -1)
                if there:
                    take_input(k, q)
                k, q, there = lagged(n, p, 3)
                if there:
                    pool.wait_ge(c1_sb, k + 1)
                    wait(pool, c2_sb, k - 5)
                    nc.gpsimd.tensor_tensor(halves(flat(c1b[:, ring(k), :])), c1[:, q, 0:4:3, :],
                                            halves(flat(g["b2"][:, layer(k), :])), ALU.add).then_inc(c1b_sb, 1)
                k, q, there = lagged(n, p, 7)
                if there:
                    pool.wait_ge(c2_sb, k + 1)
                    nc.gpsimd.tensor_copy(flat(g["ctok"][:, at(k + B), :]), c2[:, q, :]).then_inc(ctok_ready, 1)
                k, q, there = lagged(n, p, 0)
                if there:
                    pool.wait_ge(ss_sb, k + 1)
                    wait(pool, kn_sb, k - 1)
                    nc.gpsimd.tensor_tensor(rn[:, q, 8:16], ss[:, q, 8:16], g["nhalf"][:].to_broadcast([128, 8]),
                                            ALU.pow).then_inc(rnk_sb, 1)
                    pool.wait_ge(t_sb, 3 * k + 3)
                    wait(pool, kT_ps, k - 1)
                    wait(pool, kn_sb, k)
                    nc.gpsimd.tensor_tensor(kn[:], t1[:, INNER:], t2[:, INNER:], ALU.add).then_inc(add_sb, 1)
                    nc.gpsimd.tensor_tensor(qk[:, q, 0:INNER], t1[:, 0:INNER], t2[:, 0:INNER], ALU.add).then_inc(add_sb, 1)
                    pool.wait_ge(rnk_sb, k + 1)
                    pool.wait_ge(add_sb, 2 * k + 1)
                    nc.gpsimd.tensor_tensor(heads(qk[:, q, INNER:]), heads(kn[:]),
                                            rn[:, q, 8:16].unsqueeze(2).to_broadcast([128, HEADS, DH]),
                                            ALU.mult).then_inc(kn_sb, 1)
                    wait(pool, p_sb, 2 * k - 2)
                    nc.gpsimd.tensor_tensor(rn[:, q, 0:8], ss[:, q, 0:8], g["nhalf"][:].to_broadcast([128, 8]),
                                            ALU.pow).then_inc(rnq_sb, 1)
                k, q, there = lagged(n, p, 3)
                if there:
                    pool.wait_ge(ve_sb, k + 1)
                    wait(pool, xh_sb, k)
                    nc.gpsimd.tensor_tensor(rstd[:], ve[:], g["nhalf"][:], ALU.pow).then_inc(rstd_sb, 1)
                if p == 1:
                    for lag in (5, 4):
                        k, q, there = lagged(n, p, lag)
                        if there:
                            pool.wait_ge(gl_sb, k + 1)
                            wait(pool, hhT_ps, k - 1)
                            nc.gpsimd.tensor_tensor(hh[:, q, :], ag[:, q, 0, :], gl[:, q, :], ALU.mult).then_inc(hh_sb, 1)

            nc.gpsimd.memset(c1[:, :, 1:3, :], 0.0).then_inc(c1z_sb, 1)
            take_input(0, 0)
            turns(pool, step)

        @block.sync
        def _(sp):
            for c, (lo, hi) in enumerate([*RESULTS.values(), (B - 1, B)]):
                sp.wait_ge(res_sb, c + 1)
                sp.dma_start(out_dram[:, lo:hi, :], g["x1"][:, lo:hi, :]).then_inc(stored, 16)
            sp.wait_ge(stored, 16 * (len(RESULTS) + 1))


def lay_out(i):
    c = np.ascontiguousarray
    f = {k: np.asarray(v) for k, v in i.items()}
    x = f["x"]
    gates = lambda skill, shared: c(np.concatenate([skill, shared[None]]).transpose(1, 0, 2))
    w_down = np.concatenate([f["L1_cond_skill_down"], f["L1_cond_shared_down"][None]])
    pad = np.zeros((DEPTH, 3 * 128 - HID, D), np.float32)
    w2 = np.concatenate([f["L1_ffn_w2"], pad], 1)
    chunks = lambda w, n: c(w.reshape(w.shape[0], n, 128, D).transpose(2, 0, 1, 3).reshape(128, w.shape[0], n * D))
    return {
        "xT": c(x.reshape(T, D).T), "xtok": c(x.transpose(1, 0, 2)),
        "AsT": c(f["L0_cond_As"].reshape(E * RANK, D).T),
        "BsT": c(f["L0_cond_Bs"].transpose(0, 2, 1).reshape(E * RANK, D)),
        "WbT": c(f["L0_cond_W_base"].T), "WrT": c(f["L0_ffn_Wr"].T),
        "wcol": c(np.repeat(f["cond_8"].T, RANK, axis=0)), "cond": c(f["cond_8"].reshape(1, -1)),
        "rows": c(np.concatenate([f["L0_cond_b_base"], f["L0_ffn_ln_gamma"], f["L0_ffn_ln_beta"]])[None]),
        "qs": c(np.concatenate([f["L1_ffn_q_scale"], f["L1_ffn_k_scale"]], 1).reshape(1, -1)),
        "w12": c(f["L0_ffn_W12"].transpose(2, 0, 1)),
        "w3": c(f["L0_ffn_W3"].transpose(2, 0, 1).reshape(NF, 128, E, D).transpose(1, 2, 0, 3).reshape(128, E, NF * D)),
        "wg": gates(f["L1_cond_skill_gate"], f["L1_cond_shared_gate"]),
        "wu": gates(f["L1_cond_skill_up"], f["L1_cond_shared_up"]),
        "wd": chunks(w_down, NF), "wqkv": c(f["L1_ffn_wqkv"].transpose(1, 0, 2)), "wo": chunks(f["L1_ffn_wo"], NF),
        "w1": c(f["L1_ffn_w1"].transpose(1, 0, 2)), "w2": chunks(w2, 3),
        "b1": c(f["L1_ffn_b1"].reshape(1, -1)), "b2": c(f["L1_ffn_b2"].reshape(1, -1)),
        "lngb": c(np.stack([f["L1_ffn_ln_g"], f["L1_ffn_ln_b"]], -1).transpose(1, 0, 2)),
    }


def kernel(**inputs):
    import concourse.bacc as _bacc
    from concourse.bass_utils import run_bass_kernel_spmd as _run

    nc = _bacc.Bacc("TRN2", target_bir_lowering=False, num_devices=1)
    arrays, args = {}, {}
    for name, a in {**lay_out(inputs), **{k: np.ascontiguousarray(v) for k, v in constants().items()}}.items():
        arrays[f"in_{name}"] = a
        args[name] = nc.dram_tensor(f"in_{name}", a.shape, mybir.dt.from_np(a.dtype), kind="ExternalInput").ap()
    out = nc.dram_tensor("out", (B, S, D), F32, kind="ExternalOutput").ap()
    build(nc, args, out.rearrange("b s d -> s b d"))
    r = _run(nc, [arrays], core_ids=[0])
    return r.results[0]["out"]
```
